# Optimizing a Trainium2 kernel written in Bass

```python
import numpy as np
import jax
import jax.numpy as jnp

def _softmax(x, axis=-1):
    return jax.nn.softmax(x, axis=axis)

def _gelu(x):
    return jax.nn.gelu(x, approximate=True)

def _silu(x):
    return jax.nn.silu(x)

def _sigmoid(x):
    return jax.nn.sigmoid(x)

def _layernorm(x, axis=-1, eps=1e-05):
    m = jnp.mean(x, axis=axis, keepdims=True)
    v = jnp.var(x, axis=axis, keepdims=True)
    return (x - m) / jnp.sqrt(v + eps)

def _scatter_add(tgt, idx, src, axis=0):
    return tgt.at[idx].add(src)

def _segment_sum(src, seg, n):
    return jax.ops.segment_sum(src, seg, n)
kernel_name = 'mk_gnn_preln_d1_gnn_r8_450712'

def setup_inputs(seed: int=0):
    np.random.seed(seed)
    _w = jnp.asarray

    def _rec_inputs():
        import jax
        import jax.numpy as jnp
        _gk = jax.random.key(seed)
        x = -0.000202 + 1 * jax.random.normal(jax.random.fold_in(_gk, 1), (12500, 128), jnp.float32)
        src = jax.random.randint(jax.random.fold_in(_gk, 2), (200000,), 0, 12500, jnp.int32)
        dst = jnp.minimum((12500 * jax.random.uniform(jax.random.fold_in(_gk, 3), (200000,)) ** 2.0).astype(jnp.int32), 99999)
        _o = jnp.argsort(dst, stable=True)
        src = src[_o]
        dst = dst[_o]
        edge_attr_4 = -0.0005303 + 1.00001 * jax.random.normal(jax.random.fold_in(_gk, 12), (200000, 4), jnp.float32)
        edge_weight = jax.random.uniform(jax.random.fold_in(_gk, 13), (200000,), jnp.float32, 0.0, 5.99999)
        node_vec1 = jax.random.uniform(jax.random.fold_in(_gk, 14), (12500, 1), jnp.float32, 0.0, 1)
        return (x, src, dst, edge_attr_4, edge_weight, node_vec1)
    x, src, dst, edge_attr_4, edge_weight, node_vec1 = _rec_inputs()

    def _L0_gnn_setup():
        import jax, jax.numpy as jnp
        import numpy as np
        N_NODES = 6250
        N_EDGES = 62500
        MUL = 32
        NUM_RBF = 8
        CUTOFF = 6.0

        def _forward(node_input, node_attr, edge_sh_attr, edge_scalar_distances, edge_src, edge_dst, sc_ws, sc_wv, lin1_ws, lin1_wv, fc_w1, fc_w2, fc_w3, lin2_ws, lin2_wv, alpha_w):
            N = node_input.shape[0]
            dt = node_input.dtype
            d = edge_scalar_distances[:, None]
            freqs = jnp.arange(1, NUM_RBF + 1, dtype=dt) * (jnp.pi / CUTOFF)
            fd = d * freqs
            small = jnp.abs(fd) < 1e-06
            safe_fd = jnp.where(small, jnp.ones_like(fd), fd)
            rbf = jnp.where(small, jnp.ones_like(fd), jnp.sin(safe_fd) / safe_fd)
            cut = (d <= CUTOFF).astype(dt) * (0.5 * (jnp.cos(jnp.pi * d / CUTOFF) + 1.0))
            rbf = cut * rbf
            h = jax.nn.silu(rbf @ fc_w1 / jnp.sqrt(jnp.asarray(NUM_RBF, dt)))
            h = jax.nn.silu(h @ fc_w2 / jnp.sqrt(jnp.asarray(64.0, dt)))
            weight = h @ fc_w3 / jnp.sqrt(jnp.asarray(64.0, dt))
            w00, w01, w10, w11 = jnp.split(weight, 4, axis=1)
            x_s = node_input[:, :MUL]
            x_v = node_input[:, MUL:].reshape(N, MUL, 3)
            a = node_attr

            def fctp(xs, xv, ws, wv, n_in):
                inv = 1.0 / jnp.sqrt(jnp.asarray(n_in, dt))
                s = xs @ ws * a * inv
                v = jnp.einsum('nim,io->nom', xv, wv) * a[:, :, None] * inv
                return (s, v)
            sc_s, sc_v = fctp(x_s, x_v, sc_ws, sc_wv, MUL)
            l1_s, l1_v = fctp(x_s, x_v, lin1_ws, lin1_wv, MUL)
            gs = l1_s[edge_src]
            gv = l1_v[edge_src]
            sh0 = edge_sh_attr[:, 0:1]
            sh1 = edge_sh_attr[:, 1:4]
            o00 = w00 * gs * sh0
            o01 = w01[:, :, None] * gs[:, :, None] * sh1[:, None, :]
            o10 = w10[:, :, None] * gv * sh0[:, :, None]
            o11 = w11 * (jnp.einsum('ecm,em->ec', gv, sh1) / jnp.sqrt(jnp.asarray(3.0, dt)))
            msg_s = jnp.concatenate([o00, o11], axis=1)
            msg_v = jnp.concatenate([o01, o10], axis=1)
            cnt = jax.ops.segment_sum(jnp.ones((edge_dst.shape[0],), dt), edge_dst, num_segments=N)
            cnt = jnp.clip(cnt, 1.0)[:, None]
            agg_s = jax.ops.segment_sum(msg_s, edge_dst, num_segments=N) / cnt
            agg_v = jax.ops.segment_sum(msg_v, edge_dst, num_segments=N) / cnt[:, :, None]
            inv2 = 1.0 / jnp.sqrt(jnp.asarray(2 * MUL, dt))
            l2_s = agg_s @ lin2_ws * a * inv2
            l2_v = jnp.einsum('nim,io->nom', agg_v, lin2_wv) * a[:, :, None] * inv2
            alpha = jnp.tanh(agg_s @ alpha_w * a * inv2)
            out_s = sc_s + alpha * l2_s
            out_v = sc_v + alpha[:, :, None] * l2_v
            return jnp.concatenate([out_s, out_v.reshape(N, 3 * MUL)], axis=1)
        key = jax.random.key(seed)
        ks = jax.random.split(key, 16)
        f = jnp.float32
        return {'node_input': jax.random.normal(ks[0], (N_NODES, 4 * MUL), dtype=f), 'node_attr': jnp.ones((N_NODES, 1), dtype=f), 'edge_sh_attr': jax.random.normal(ks[1], (N_EDGES, 4), dtype=f), 'edge_scalar_distances': jax.random.uniform(ks[2], (N_EDGES,), dtype=f, minval=0.1, maxval=CUTOFF), 'edge_src': jax.random.randint(ks[3], (N_EDGES,), 0, N_NODES, dtype=jnp.int32), 'edge_dst': jax.random.randint(ks[4], (N_EDGES,), 0, N_NODES, dtype=jnp.int32), 'sc_ws': jax.random.normal(ks[5], (MUL, MUL), dtype=f), 'sc_wv': jax.random.normal(ks[6], (MUL, MUL), dtype=f), 'lin1_ws': jax.random.normal(ks[7], (MUL, MUL), dtype=f), 'lin1_wv': jax.random.normal(ks[8], (MUL, MUL), dtype=f), 'fc_w1': jax.random.normal(ks[9], (NUM_RBF, 64), dtype=f), 'fc_w2': jax.random.normal(ks[10], (64, 64), dtype=f), 'fc_w3': jax.random.normal(ks[11], (64, 4 * MUL), dtype=f), 'lin2_ws': jax.random.normal(ks[12], (2 * MUL, MUL), dtype=f), 'lin2_wv': jax.random.normal(ks[13], (2 * MUL, MUL), dtype=f), 'alpha_w': jax.random.normal(ks[14], (2 * MUL, 1), dtype=f) * 0.1}
    _L0_gnn_all = _L0_gnn_setup()
    _L0_gnn_in = {k: v for k, v in _L0_gnn_all.items() if k in ('sc_ws', 'sc_wv', 'lin1_ws', 'lin1_wv', 'fc_w1', 'fc_w2', 'fc_w3', 'lin2_ws', 'lin2_wv', 'alpha_w')}
    del _L0_gnn_all
    return {'x': x, 'src': src, 'dst': dst, 'edge_attr_4': edge_attr_4, 'edge_weight': edge_weight, 'node_vec1': node_vec1, 'L0_gnn_sc_ws': _L0_gnn_in['sc_ws'], 'L0_gnn_sc_wv': _L0_gnn_in['sc_wv'], 'L0_gnn_lin1_ws': _L0_gnn_in['lin1_ws'], 'L0_gnn_lin1_wv': _L0_gnn_in['lin1_wv'], 'L0_gnn_fc_w1': _L0_gnn_in['fc_w1'], 'L0_gnn_fc_w2': _L0_gnn_in['fc_w2'], 'L0_gnn_fc_w3': _L0_gnn_in['fc_w3'], 'L0_gnn_lin2_ws': _L0_gnn_in['lin2_ws'], 'L0_gnn_lin2_wv': _L0_gnn_in['lin2_wv'], 'L0_gnn_alpha_w': _L0_gnn_in['alpha_w']}

def reference(x, src, dst, edge_attr_4, edge_weight, node_vec1, L0_gnn_sc_ws, L0_gnn_sc_wv, L0_gnn_lin1_ws, L0_gnn_lin1_wv, L0_gnn_fc_w1, L0_gnn_fc_w2, L0_gnn_fc_w3, L0_gnn_lin2_ws, L0_gnn_lin2_wv, L0_gnn_alpha_w):
    import jax
    import jax.numpy as jnp

    def _L0_gnn_ref(node_input, node_attr, edge_sh_attr, edge_scalar_distances, edge_src, edge_dst, sc_ws, sc_wv, lin1_ws, lin1_wv, fc_w1, fc_w2, fc_w3, lin2_ws, lin2_wv, alpha_w):
        import jax, jax.numpy as jnp
        import numpy as np
        N_NODES = 6250
        N_EDGES = 62500
        MUL = 32
        NUM_RBF = 8
        CUTOFF = 6.0

        def _forward(node_input, node_attr, edge_sh_attr, edge_scalar_distances, edge_src, edge_dst, sc_ws, sc_wv, lin1_ws, lin1_wv, fc_w1, fc_w2, fc_w3, lin2_ws, lin2_wv, alpha_w):
            N = node_input.shape[0]
            dt = node_input.dtype
            d = edge_scalar_distances[:, None]
            freqs = jnp.arange(1, NUM_RBF + 1, dtype=dt) * (jnp.pi / CUTOFF)
            fd = d * freqs
            small = jnp.abs(fd) < 1e-06
            safe_fd = jnp.where(small, jnp.ones_like(fd), fd)
            rbf = jnp.where(small, jnp.ones_like(fd), jnp.sin(safe_fd) / safe_fd)
            cut = (d <= CUTOFF).astype(dt) * (0.5 * (jnp.cos(jnp.pi * d / CUTOFF) + 1.0))
            rbf = cut * rbf
            h = jax.nn.silu(rbf @ fc_w1 / jnp.sqrt(jnp.asarray(NUM_RBF, dt)))
            h = jax.nn.silu(h @ fc_w2 / jnp.sqrt(jnp.asarray(64.0, dt)))
            weight = h @ fc_w3 / jnp.sqrt(jnp.asarray(64.0, dt))
            w00, w01, w10, w11 = jnp.split(weight, 4, axis=1)
            x_s = node_input[:, :MUL]
            x_v = node_input[:, MUL:].reshape(N, MUL, 3)
            a = node_attr

            def fctp(xs, xv, ws, wv, n_in):
                inv = 1.0 / jnp.sqrt(jnp.asarray(n_in, dt))
                s = xs @ ws * a * inv
                v = jnp.einsum('nim,io->nom', xv, wv) * a[:, :, None] * inv
                return (s, v)
            sc_s, sc_v = fctp(x_s, x_v, sc_ws, sc_wv, MUL)
            l1_s, l1_v = fctp(x_s, x_v, lin1_ws, lin1_wv, MUL)
            gs = l1_s[edge_src]
            gv = l1_v[edge_src]
            sh0 = edge_sh_attr[:, 0:1]
            sh1 = edge_sh_attr[:, 1:4]
            o00 = w00 * gs * sh0
            o01 = w01[:, :, None] * gs[:, :, None] * sh1[:, None, :]
            o10 = w10[:, :, None] * gv * sh0[:, :, None]
            o11 = w11 * (jnp.einsum('ecm,em->ec', gv, sh1) / jnp.sqrt(jnp.asarray(3.0, dt)))
            msg_s = jnp.concatenate([o00, o11], axis=1)
            msg_v = jnp.concatenate([o01, o10], axis=1)
            cnt = jax.ops.segment_sum(jnp.ones((edge_dst.shape[0],), dt), edge_dst, num_segments=N)
            cnt = jnp.clip(cnt, 1.0)[:, None]
            agg_s = jax.ops.segment_sum(msg_s, edge_dst, num_segments=N) / cnt
            agg_v = jax.ops.segment_sum(msg_v, edge_dst, num_segments=N) / cnt[:, :, None]
            inv2 = 1.0 / jnp.sqrt(jnp.asarray(2 * MUL, dt))
            l2_s = agg_s @ lin2_ws * a * inv2
            l2_v = jnp.einsum('nim,io->nom', agg_v, lin2_wv) * a[:, :, None] * inv2
            alpha = jnp.tanh(agg_s @ alpha_w * a * inv2)
            out_s = sc_s + alpha * l2_s
            out_v = sc_v + alpha[:, :, None] * l2_v
            return jnp.concatenate([out_s, out_v.reshape(N, 3 * MUL)], axis=1)
        return _forward(node_input, node_attr, edge_sh_attr, edge_scalar_distances, edge_src, edge_dst, sc_ws, sc_wv, lin1_ws, lin1_wv, fc_w1, fc_w2, fc_w3, lin2_ws, lin2_wv, alpha_w)
    h = jnp.maximum(_layernorm(x, axis=-1), 0.0)
    x = x + _L0_gnn_ref(h, node_vec1, edge_attr_4, edge_weight, src, dst, L0_gnn_sc_ws, L0_gnn_sc_wv, L0_gnn_lin1_ws, L0_gnn_lin1_wv, L0_gnn_fc_w1, L0_gnn_fc_w2, L0_gnn_fc_w3, L0_gnn_lin2_ws, L0_gnn_lin2_wv, L0_gnn_alpha_w)
    return x

_drawn_inputs = setup_inputs


def setup_inputs(seed=0):
    import zlib

    import numpy as np

    out = dict(_drawn_inputs(seed))
    spreads = {}
    factors = {}
    for name, (base, spread) in spreads.items():
        noise = np.random.default_rng([zlib.crc32(name.encode()), seed]).standard_normal(out[name].shape)
        drawn = base * np.exp(spread * noise) if base else spread * noise
        out[name] = jnp.asarray(drawn.astype(out[name].dtype))
    for name, factor in factors.items():
        out[name] = (out[name] * factor).astype(out[name].dtype)
    return out
```

```python
from contextlib import ExitStack

import numpy as np

import concourse.bass as bass
from concourse import mybir

F32 = mybir.dt.float32
I32 = mybir.dt.int32
ALU = mybir.AluOpType
ACT = mybir.ActivationFunctionType
AX_X = mybir.AxisListType.X

P = 128
NODES, DIM = 12500, 128
EDGES = 200000
MUL, RBF, HID = 32, 8, 64
CUTOFF = 6.0
EPS = 1e-5

TILES = 6
GROUP = TILES * P
SLOTS = 4
QUAD = SLOTS * GROUP
ITERS = EDGES // QUAD
assert EDGES - ITERS * QUAD <= GROUP
HALF = QUAD // 2
SEGS = 16
SEG = QUAD // SEGS
UNIT = 2 * SEG
UNITS = HALF // UNIT
EDGES_PAD = (ITERS + 2) * QUAD
DCOLS = EDGES_PAD // P
GROUPS = (ITERS + 1) * SLOTS
OFFSET = [(u % 2) * HALF + (u // 2) * GROUP for u in range(SLOTS)]
NO_NODE = 1 << 20

NBLK = -(-NODES // P)
NB = 4
STEPS = NBLK // NB
REST = NBLK - STEPS * NB
REST_ROWS = [min(P, NODES - (STEPS * NB + j) * P) for j in range(REST)]
MSG = 8 * MUL
COLS = MSG + 1
TINY = 2e-5
FAR = 65536.0
ROUND = 1.5 * 2 ** 23
TURN = float(np.nextafter(np.float32(2 * np.pi), np.float32(0)))


def at_least(eng, sem, value):
    if not isinstance(value, int) or value > 0:
        eng.wait_ge(sem, value)


def gnn_kernel(nc, x, src, dst, sh, dist, node_vec, sc_ws, sc_wv, lin1_ws, lin1_wv,
               fc_w1, fc_w2, fc_w3, lin2_ws, lin2_wv, alpha_w, out):
    lin_table = nc.dram_tensor("lin_table", [NODES, DIM], F32, kind="Internal").ap()
    sc_table = nc.dram_tensor("sc_table", [NODES, DIM], F32, kind="Internal").ap()
    a_table = nc.dram_tensor("a_table", [EDGES_PAD], F32, kind="Internal").ap()
    q_table = nc.dram_tensor("q_table", [EDGES_PAD], F32, kind="Internal").ap()
    key_table = nc.dram_tensor("key_table", [GROUPS * GROUP], F32, kind="Internal").ap()

    def node_rows(table, step):
        return table[bass.ds(step * (NB * P), NB * P), :].rearrange("(b p) d -> p b d", p=P)

    def rest_rows(table, j):
        lo = (STEPS * NB + j) * P
        return table[lo:lo + REST_ROWS[j], :]

    def group_blocks():
        return [(b, min(P, GROUPS - b * P)) for b in range(-(-GROUPS // P))]

    GB = len(group_blocks())

    with ExitStack() as top:
        def sb(name, shape, dt=F32, ctx=top):
            return ctx.enter_context(nc.sbuf_tensor(name, shape, dt))

        agg = sb("agg", [P, (NBLK + 1) * COLS])
        ident = sb("ident", [P, P])
        iota1 = sb("iota1", [P, P])
        sel_freq = sb("sel_freq", [SEGS, P])
        sel_one = sb("sel_one", [SEGS, P])
        w1 = sb("w1", [P, SEGS // 2, P])
        w2 = sb("w2", [P, P])
        w3 = sb("w3", [P, P])
        w_lin2 = sb("w_lin2", [P, 2, 2 * MUL])
        w_alpha = sb("w_alpha", [2 * MUL, 1])
        attr_lin = sb("attr_lin", [P, NBLK])
        attr_lin2 = sb("attr_lin2", [P, NBLK])
        dst_f = sb("dst_f", [P, GB, GROUP])
        row1 = sb("row1", [P, GB, GROUP])
        win_lo = sb("win_lo", [P, GB])
        win_hi = sb("win_hi", [P, GB])
        at_lo = sb("at_lo", [P, GROUPS])
        at_hi = sb("at_hi", [P, GROUPS])
        blk_f = sb("blk_f", [1, GROUPS])
        blk_i = sb("blk_i", [1, GROUPS], I32)
        passes_i = sb("passes_i", [1, 1], I32)

        with ExitStack() as st:
            def s1(name, shape, dt=F32):
                return sb(name, shape, dt, st)

            def sem(name):
                return st.enter_context(nc.semaphore(name))

            XB = 4
            xq = s1("xq", [P, XB, NB, DIM])
            bn = s1("bn", [P, 2, NB, 6])
            mean_var = s1("mean_var", [P, 2, NB, 2])
            var_eps = s1("var_eps", [P, 2, NB])
            std = s1("std", [P, 2, NB])
            rstd = s1("rstd", [P, 2, NB])
            shift = s1("shift", [P, 2, NB])
            h = s1("h", [P, 2, NB, DIM])
            hT = s1("hT", [P, 2, NB * P])
            node_out = s1("node_out", [P, XB, NB, 2 * DIM])
            w_nodes = s1("w_nodes", [P, 2 * DIM])
            iota_i = s1("iota_i", [P, P], I32)
            freq_i = s1("freq_i", [SEGS, P], I32)
            freq = s1("freq", [SEGS, P])
            part_i = s1("part_i", [P, 1], I32)
            part_f = s1("part_f", [P, 1])
            rowf_i = s1("rowf_i", [P, 1], I32)
            rowf = s1("rowf", [P, 1])
            row_scale = s1("row_scale", [P, 1])
            ones = s1("ones", [P, P])
            attr_raw = s1("attr_raw", [NBLK, P])
            dst_i = s1("dst_i", [P, GB, GROUP], I32)
            least = s1("least", [P, GB])
            most = s1("most", [P, GB])
            span = s1("span", [P, GB])
            widest = s1("widest", [P, 1])
            base_diag = s1("base_diag", [P, GB, P])
            base_i = s1("base_i", [P, GROUPS], I32)
            off_i = s1("off_i", [P, GROUPS], I32)
            off_f = s1("off_f", [P, GROUPS])
            blk0_i = s1("blk0_i", [1, GROUPS], I32)
            span_max = s1("span_max", [1, 1])
            span_i = s1("span_i", [1, 1], I32)
            more_i = s1("more_i", [1, 1], I32)
            d_in = s1("d_in", [P, DCOLS])
            d_abs = s1("d_abs", [P, DCOLS])
            a_all = s1("a_all", [P, DCOLS])
            turns = s1("turns", [P, DCOLS])
            psT = st.enter_context(nc.psum_tensor("psT", [P, 2, NB * P], F32))
            psN = st.enter_context(nc.psum_tensor("psN", [P, 2, NB, 2 * DIM], F32))
            psW = st.enter_context(nc.psum_tensor("psW", [P, 512], F32))
            psA = st.enter_context(nc.psum_tensor("psA", [P, 512], F32))

            x_in = [sem(f"x_in{b}") for b in range(XB)]
            stored = [sem(f"stored{b}") for b in range(XB)]
            dist_in, dst_in, attr_in = sem("dist_in"), sem("dst_in"), sem("attr_in")
            w_nodes_in, w_edges_in, tables_out = sem("w_nodes_in"), sem("w_edges_in"), sem("tables_out")
            zeroed, shaped, iotas, ones_set = sem("zeroed"), sem("shaped"), sem("iotas"), sem("ones_set")
            bn_done, aggr_done, var_ready, std_ready = sem("bn_done"), sem("aggr_done"), sem("var_ready"), sem("std_ready")
            rstd_ready, norm_ready, h_ready = sem("rstd_ready"), sem("norm_ready"), sem("h_ready")
            transposed, hT_ready, nodes_done, evacuated = sem("transposed"), sem("hT_ready"), sem("nodes_done"), sem("evacuated")
            attr_turned, attr_ready = sem("attr_turned"), sem("attr_ready")
            const_step, win_step, spread, span_row = sem("const_step"), sem("win_step"), sem("spread"), sem("span_row")
            abs_ready, dist_step, cos_ready = sem("abs_ready"), sem("dist_step"), sem("cos_ready")
            agg_zero, diag_ready = sem("agg_zero"), sem("diag_ready")

            UNROLL = XB
            LOOPS = (STEPS - UNROLL) // UNROLL
            PEELED = LOOPS * UNROLL

            with nc.Block() as block:
                @block.sync
                def _(sp):
                    def load_x(t, j):
                        t, b = t + j // XB, j % XB
                        sp.dma_start(xq[:, b], node_rows(x, t * XB + b)).then_inc(x_in[b], 16)

                    def load_rest():
                        b = STEPS % XB
                        for r in range(REST):
                            sp.dma_start(xq[0:REST_ROWS[r], b, r], rest_rows(x, r)).then_inc(x_in[b], 16)

                    def store(t, b):
                        sp.wait_ge(evacuated, t * XB + b + 1)
                        sp.dma_start(node_rows(lin_table, t * XB + b), node_out[:, b, :, 0:DIM]).then_inc(stored[b], 16)
                        sp.dma_start(node_rows(sc_table, t * XB + b), node_out[:, b, :, DIM:]).then_inc(stored[b], 16)

                    for j in range(XB):
                        load_x(0, j)
                    sp.wait_ge(zeroed, 1)
                    sp.dma_start(attr_raw[0:NBLK - 1, :], node_vec[0:(NBLK - 1) * P, :].rearrange("(b p) o -> b (p o)", p=P)).then_inc(attr_in, 16)
                    sp.dma_start(attr_raw[NBLK - 1:NBLK, 0:NODES - (NBLK - 1) * P],
                                 node_vec[(NBLK - 1) * P:, :].rearrange("(b p) o -> b (p o)", b=1)).then_inc(attr_in, 16)
                    for b, n in group_blocks():
                        sp.dma_start(dst_i[0:n, b, :], dst[b * P * GROUP:(b * P + n) * GROUP].rearrange("(g e) -> g e", e=GROUP)).then_inc(dst_in, 16)
                    sp.dma_start(d_in[:], dist.rearrange("(p c) -> p c", p=P)).then_inc(dist_in, 16)
                    with sp.Fori(0, LOOPS) as t:
                        for j in range(UNROLL):
                            sp.wait_ge(h_ready, t * UNROLL + j + 1)
                            load_x(t, j + XB)
                            store(t, j)
                    for k in range(PEELED, STEPS):
                        if k + XB == STEPS:
                            sp.wait_ge(h_ready, k + 1)
                            load_rest()
                        store(k // XB, k % XB)
                    sp.wait_ge(evacuated, STEPS + 1)
                    b = STEPS % XB
                    for r in range(REST):
                        sp.dma_start(rest_rows(lin_table, r), node_out[0:REST_ROWS[r], b, r, 0:DIM]).then_inc(stored[b], 16)
                        sp.dma_start(rest_rows(sc_table, r), node_out[0:REST_ROWS[r], b, r, DIM:]).then_inc(stored[b], 16)
                    sp.wait_ge(dist_step, 1)
                    sp.dma_start(a_table.rearrange("(p c) -> p c", p=P), a_all[:]).then_inc(tables_out, 16)
                    sp.wait_ge(dist_step, 8)
                    sp.dma_start(q_table.rearrange("(p c) -> p c", p=P), turns[:]).then_inc(tables_out, 16)
                    sp.wait_ge(tables_out, 32)
                    for b in range(XB):
                        steps = len(range(b, STEPS, XB))
                        sp.wait_ge(stored[b], 32 * steps + (32 * REST if b == STEPS % XB else 0))

                @block.gpsimd
                def _(pool):
                    pool.memset(attr_raw[:], 0.0).then_inc(zeroed, 1)
                    pool.memset(w_nodes[:], 0.0).then_inc(zeroed, 1)
                    pool.memset(ident[:], 0.0).then_inc(zeroed, 1)
                    pool.memset(ones[:], 1.0).then_inc(ones_set, 1)
                    pool.memset(sel_one[:], 1.0).then_inc(ones_set, 1)
                    pool.memset(least[:], 0.0).then_inc(ones_set, 1)
                    pool.memset(span[:], 0.0).then_inc(ones_set, 1)
                    pool.wait_ge(zeroed, 3)
                    pool.affine_select(out=ident[:], in_=ident[:], compare_op=ALU.not_equal, fill=1.0, base=0,
                                       pattern=[[-1, P]], channel_multiplier=1).then_inc(shaped, 1)
                    pool.memset(w1[:], 0.0).then_inc(zeroed, 1)
                    pool.memset(w2[:], 0.0).then_inc(zeroed, 1)
                    pool.memset(w_lin2[:], 0.0).then_inc(zeroed, 1)
                    pool.iota(iota_i[:], pattern=[[1, P]], base=1, channel_multiplier=0).then_inc(iotas, 1)
                    pool.iota(part_i[:], pattern=[[0, 1]], base=0, channel_multiplier=1).then_inc(iotas, 1)
                    pool.iota(freq_i[:], pattern=[[0, SEGS], [1, RBF]], base=1, channel_multiplier=0).then_inc(iotas, 1)
                    pool.wait_ge(ones_set, 2)
                    pool.affine_select(out=sel_one[:], in_=sel_one[:], compare_op=ALU.is_ge, fill=0.0, base=0,
                                       pattern=[[1, P]], channel_multiplier=-RBF).then_inc(shaped, 1)
                    pool.wait_ge(shaped, 2)
                    pool.affine_select(out=sel_one[:], in_=sel_one[:], compare_op=ALU.is_ge, fill=0.0, base=RBF - 1,
                                       pattern=[[-1, P]], channel_multiplier=RBF).then_inc(shaped, 1)
                    pool.wait_ge(zeroed, 6)
                    for s in range(SEGS):
                        half, q = s // (SEGS // 2), s % (SEGS // 2)
                        pool.dma_start(w1[s * RBF:(s + 1) * RBF, q, half * HID:(half + 1) * HID], fc_w1).then_inc(w_edges_in, 16)
                    for half in range(2):
                        rows = slice(half * HID, (half + 1) * HID)
                        pool.dma_start(w2[rows, rows], fc_w2).then_inc(w_edges_in, 16)
                        pool.dma_start(w3[rows, :], fc_w3).then_inc(w_edges_in, 16)
                    pool.dma_start(w_lin2[0:HID, 0, 0:MUL], lin2_ws).then_inc(w_edges_in, 16)
                    pool.dma_start(w_lin2[HID:P, 0, MUL:], lin2_wv).then_inc(w_edges_in, 16)
                    pool.dma_start(w_lin2[0:HID, 1, 0:MUL], lin2_wv).then_inc(w_edges_in, 16)
                    pool.dma_start(w_lin2[HID:P, 1, MUL:], lin2_wv).then_inc(w_edges_in, 16)
                    pool.dma_start(w_alpha[:], alpha_w).then_inc(w_edges_in, 16)
                    pool.memset(agg[:], 0.0).then_inc(agg_zero, 1)
                    pool.wait_ge(w_edges_in, 16 * (SEGS + 9))

                @block.scalar
                def _(act):
                    act.wait_ge(zeroed, 2)
                    for c, (ws, wv) in enumerate(((lin1_ws, lin1_wv), (sc_ws, sc_wv))):
                        act.dma_start(w_nodes[0:MUL, c * DIM:c * DIM + MUL], ws).then_inc(w_nodes_in, 16)
                        for m in range(3):
                            lo = c * DIM + (m + 1) * MUL
                            act.dma_start(w_nodes[MUL + m:DIM:3, lo:lo + MUL], wv).then_inc(w_nodes_in, 16)

                    def sqrt(t, j):
                        n, b = t * UNROLL + j, j % 2
                        act.wait_ge(var_ready, n + 1)
                        act.activation(std[:, b, :], var_eps[:, b, :], ACT.Sqrt).then_inc(std_ready, 1)

                    def normalize(t, j, blocks=NB):
                        n, b = t * UNROLL + j, j % 2
                        act.wait_ge(norm_ready, n + 1)
                        at_least(act, transposed, n - 1)
                        for k in range(blocks):
                            last = act.activation(h[:, b, k, :], xq[:, j % XB, k, :], ACT.Relu,
                                                  bias=shift[:, b, k:k + 1], scale=rstd[:, b, k:k + 1])
                        last.then_inc(h_ready, 1)

                    def evacuate(t, j, blocks=NB):
                        n, b = t * UNROLL + j, j % XB
                        act.wait_ge(nodes_done, n + 1)
                        at_least(act, stored[b], 32 * (t + j // XB))
                        for k in range(blocks):
                            blk = n * NB + k
                            last = act.activation(node_out[:, b, k, :], psN[:, j % 2, k, :], ACT.Copy,
                                                  scale=attr_lin[:, bass.ds(blk, 1)])
                        last.then_inc(evacuated, 1)

                    def step(t, j):
                        n = t * UNROLL + j
                        ahead = not isinstance(n, int)
                        if ahead or n + 1 <= STEPS:
                            normalize(t, j + 1, NB if ahead or n + 1 < STEPS else REST)
                        if ahead or n + 2 <= STEPS:
                            sqrt(t, j + 2)
                        evacuate(t, j, NB if ahead or n < STEPS else REST)

                    sqrt(0, 0)
                    sqrt(0, 1)
                    normalize(0, 0)
                    act.wait_ge(attr_ready, 2)
                    for j in range(UNROLL):
                        step(0, j)
                    with act.Fori(1, LOOPS) as t:
                        for j in range(UNROLL):
                            step(t, j)
                    for n in range(PEELED, STEPS + 1):
                        step(n // UNROLL, n % UNROLL)

                    act.wait_ge(dist_in, 16)
                    act.activation(d_abs[:], d_in[:], ACT.Abs).then_inc(abs_ready, 1)
                    act.wait_ge(dist_step, 4)
                    act.activation(turns[:], turns[:], ACT.Sin, scale=-TURN).then_inc(cos_ready, 1)

                @block.tensor
                def _(pe):
                    def turn(t, j, blocks=NB):
                        n, b = t * UNROLL + j, j % 2
                        pe.wait_ge(h_ready, n + 1)
                        at_least(pe, hT_ready, n - 1)
                        for k in range(blocks):
                            last = pe.transpose(psT[:, b, k * P:(k + 1) * P], h[:, b, k, :], ident[:])
                        last.then_inc(transposed, 1)

                    def product(t, j, blocks=NB):
                        n, b = t * UNROLL + j, j % 2
                        pe.wait_ge(hT_ready, n + 1)
                        at_least(pe, evacuated, n - 1)
                        for k in range(blocks):
                            last = pe.matmul(psN[:, b, k, :], hT[:, b, k * P:(k + 1) * P], w_nodes[:], start=True, stop=True)
                        last.then_inc(nodes_done, 1)

                    pe.wait_ge(shaped, 1)
                    pe.wait_ge(attr_in, 32)
                    pe.transpose(psA[:, 0:NBLK], attr_raw[:], ident[0:NBLK, 0:NBLK]).then_inc(attr_turned, 1)
                    turn(0, 0)
                    pe.wait_ge(w_nodes_in, 16 * 8)
                    for j in range(UNROLL):
                        product(0, j)
                        turn(0, j + 1)
                    with pe.Fori(1, LOOPS) as t:
                        for j in range(UNROLL):
                            product(t, j)
                            turn(t, j + 1)
                    for n in range(PEELED, STEPS + 1):
                        product(n // UNROLL, n % UNROLL, NB if n < STEPS else REST)
                        if n < STEPS:
                            turn(n // UNROLL, n % UNROLL + 1, NB if n + 1 < STEPS else REST)

                    pe.wait_ge(ones_set, 1)
                    pe.wait_ge(diag_ready, GB)
                    for b, n in group_blocks():
                        last = pe.matmul(psW[:, b * P:b * P + n], ones[0:n, :], base_diag[0:n, b, 0:n], start=True, stop=True)
                    last.then_inc(spread, 1)
                    pe.wait_ge(win_step, 8 * GB + 1)
                    pe.wait_ge(attr_ready, 2)
                    pe.matmul(psA[0:1, 0:P], widest[:], ident[:], start=True, stop=True).then_inc(span_row, 1)

                @block.vector
                def _(dve):
                    done = {"const": 0, "win": 0}

                    dve.wait_ge(iotas, 3)
                    dve.tensor_copy(iota1[:], iota_i[:]).then_inc(const_step, 1)
                    dve.tensor_copy(part_f[:], part_i[:]).then_inc(const_step, 1)
                    dve.tensor_copy(freq[:], freq_i[:]).then_inc(const_step, 1)
                    dve.tensor_scalar(rowf_i[:], part_i[:], RBF - 1, None, ALU.bitwise_and).then_inc(const_step, 1)
                    dve.wait_ge(const_step, 4)
                    dve.tensor_scalar(rowf[:], rowf_i[:], 1.0, None, ALU.add).then_inc(const_step, 1)
                    dve.wait_ge(shaped, 3)
                    dve.scalar_tensor_tensor(out=sel_freq[:], in0=freq[:], scalar=1.0 / (2 * CUTOFF), in1=sel_one[:],
                                             op0=ALU.mult, op1=ALU.mult).then_inc(const_step, 1)
                    dve.wait_ge(const_step, 5)
                    dve.reciprocal(row_scale[:], rowf[:]).then_inc(const_step, 1)
                    dve.wait_ge(attr_turned, 1)
                    dve.tensor_scalar(attr_lin[:], psA[:, 0:NBLK], float(MUL ** -0.5), None, ALU.mult).then_inc(attr_ready, 1)
                    dve.tensor_scalar(attr_lin2[:], psA[:, 0:NBLK], float((2 * MUL) ** -0.5), None, ALU.mult).then_inc(attr_ready, 1)

                    def stats(t, j, blocks=NB):
                        n, b = t * UNROLL + j, j % 2
                        landed = 16 * (t + j // XB + 1)
                        dve.wait_ge(x_in[j % XB], landed if blocks == NB else landed - 16 + 16 * REST)
                        for k in range(NB):
                            dve.bn_stats(bn[:, b, k, :], xq[:, j % XB, k, :]).then_inc(bn_done, 1)
                        dve.wait_ge(bn_done, n * NB + NB)
                        dve.nop(nofuse=True)
                        for k in range(NB):
                            dve.bn_aggr(mean_var[:, b, k, :], bn[:, b, k, :]).then_inc(aggr_done, 1)
                        dve.wait_ge(aggr_done, n * NB + NB)
                        dve.tensor_scalar(var_eps[:, b, :], mean_var[:, b, :, 1], EPS, None, ALU.add).then_inc(var_ready, 1)

                    def scales(t, j):
                        n, b = t * UNROLL + j, j % 2
                        dve.wait_ge(std_ready, n + 1)
                        at_least(dve, h_ready, n - 1)
                        dve.reciprocal(rstd[:, b, :], std[:, b, :]).then_inc(rstd_ready, 1)
                        dve.wait_ge(rstd_ready, n + 1)
                        dve.scalar_tensor_tensor(out=shift[:, b, :], in0=mean_var[:, b, :, 0], scalar=-1.0, in1=rstd[:, b, :],
                                                 op0=ALU.mult, op1=ALU.mult).then_inc(norm_ready, 1)

                    def copy_hT(t, j, blocks=NB):
                        n, b = t * UNROLL + j, j % 2
                        dve.wait_ge(transposed, n + 1)
                        at_least(dve, nodes_done, n - 1)
                        dve.tensor_copy(hT[:, b, 0:blocks * P], psT[:, b, 0:blocks * P]).then_inc(hT_ready, 1)

                    def step(t, j):
                        n = t * UNROLL + j
                        ahead = not isinstance(n, int)
                        copy_hT(t, j, NB if ahead or n < STEPS else REST)
                        if ahead or n + 2 <= STEPS:
                            stats(t, j + 2, NB if ahead or n + 2 < STEPS else REST)
                            scales(t, j + 2)

                    stats(0, 0)
                    stats(0, 1)
                    scales(0, 0)
                    scales(0, 1)
                    for j in range(UNROLL):
                        step(0, j)
                    with dve.Fori(1, LOOPS) as t:
                        for j in range(UNROLL):
                            step(t, j)
                    for n in range(PEELED, STEPS + 1):
                        step(n // UNROLL, n % UNROLL)

                    win = 0
                    dve.wait_ge(dst_in, 16 * GB)
                    dve.wait_ge(ones_set, 4)
                    for b, n in group_blocks():
                        dve.tensor_copy(dst_f[0:n, b, :], dst_i[0:n, b, :]).then_inc(win_step, 1)
                        dve.wait_ge(win_step, win + 1)
                        dve.tensor_scalar(dst_i[0:n, b, :], dst_i[0:n, b, :], P - 1, None, ALU.bitwise_and).then_inc(win_step, 1)
                        dve.tensor_reduce(least[0:n, b:b + 1], dst_f[0:n, b, :], AX_X, ALU.min).then_inc(win_step, 1)
                        dve.scalar_tensor_tensor(out=row1[0:n, b, :], in0=dst_f[0:n, b, :], scalar=float(NODES), in1=dst_f[0:n, b, :],
                                                 op0=ALU.is_lt, op1=ALU.mult).then_inc(win_step, 1)
                        dve.wait_ge(win_step, win + 4)
                        dve.tensor_reduce(most[0:n, b:b + 1], row1[0:n, b, :], AX_X, ALU.max).then_inc(win_step, 1)
                        dve.wait_ge(win_step, win + 5)
                        dve.tensor_scalar(row1[0:n, b, :], dst_i[0:n, b, :], 1.0, None, ALU.add).then_inc(win_step, 1)
                        dve.tensor_scalar(least[0:n, b:b + 1], least[0:n, b:b + 1], float(NODES - 1), None, ALU.min).then_inc(win_step, 1)
                        dve.wait_ge(win_step, win + 7)
                        dve.tensor_tensor(span[0:n, b:b + 1], most[0:n, b:b + 1], least[0:n, b:b + 1], ALU.subtract).then_inc(win_step, 1)
                        dve.tensor_scalar(base_diag[0:n, b, :], ident[0:n, :], least[0:n, b:b + 1], None, ALU.mult).then_inc(diag_ready, 1)
                        win += 8
                    dve.wait_ge(win_step, win)
                    dve.tensor_reduce(widest[:], span[:], AX_X, ALU.max).then_inc(win_step, 1)
                    dve.tensor_scalar(win_lo[:], least[:], float(-P), None, ALU.add).then_inc(win_step, 1)
                    dve.wait_ge(spread, 1)
                    dve.tensor_copy(base_i[:], psW[:, 0:GROUPS]).then_inc(win_step, 1)
                    dve.wait_ge(win_step, win + 3)
                    dve.tensor_scalar(off_i[:], base_i[:], P - 1, None, ALU.bitwise_and).then_inc(win_step, 1)
                    dve.tensor_scalar(blk0_i[:], base_i[0:1, :], 7, None, ALU.logical_shift_right).then_inc(win_step, 1)
                    dve.wait_ge(win_step, win + 4)
                    dve.tensor_copy(off_f[:], off_i[:]).then_inc(win_step, 1)
                    dve.wait_ge(win_step, win + 6)
                    dve.tensor_scalar(at_lo[:], off_f[:], part_f[:, 0:1], None, ALU.is_le).then_inc(win_step, 1)
                    dve.tensor_scalar(at_hi[:], off_f[:], part_f[:, 0:1], None, ALU.is_gt).then_inc(win_step, 1)
                    dve.tensor_scalar(blk_f[:], blk0_i[:], -1.0, None, ALU.add).then_inc(win_step, 1)
                    dve.wait_ge(span_row, 1)
                    dve.tensor_reduce(span_max[:], psA[0:1, 0:P], AX_X, ALU.max).then_inc(win_step, 1)
                    dve.wait_ge(win_step, win + 10)
                    dve.tensor_copy(span_i[:], span_max[:]).then_inc(win_step, 1)
                    dve.wait_ge(win_step, win + 11)
                    dve.tensor_scalar(more_i[:], span_i[:], 7, None, ALU.logical_shift_right).then_inc(win_step, 1)
                    dve.wait_ge(win_step, win + 12)
                    dve.tensor_scalar(passes_i[:], more_i[:], 1.0, None, ALU.add).then_inc(win_step, 1)

                    dve.wait_ge(abs_ready, 1)
                    dve.tensor_scalar(a_all[:], d_abs[:], TINY, FAR, ALU.max, ALU.min).then_inc(dist_step, 1)
                    dve.wait_ge(dist_step, 1)
                    dve.tensor_scalar(turns[:], a_all[:], 1.0 / (2 * CUTOFF), 0.25, ALU.mult, ALU.add).then_inc(dist_step, 1)
                    dve.wait_ge(dist_step, 2)
                    dve.tensor_scalar(d_abs[:], turns[:], ROUND, None, ALU.add).then_inc(dist_step, 1)
                    dve.wait_ge(dist_step, 3)
                    dve.scalar_tensor_tensor(out=turns[:], in0=d_abs[:], scalar=ROUND, in1=turns[:],
                                             op0=ALU.subtract, op1=ALU.subtract).then_inc(dist_step, 1)
                    dve.wait_ge(dist_step, 4)
                    dve.reciprocal(d_abs[:], a_all[:]).then_inc(dist_step, 1)
                    dve.wait_ge(cos_ready, 1)
                    dve.tensor_scalar(turns[:], turns[:], 0.5, 0.5, ALU.mult, ALU.add).then_inc(dist_step, 1)
                    dve.wait_ge(dist_step, 6)
                    dve.scalar_tensor_tensor(out=turns[:], in0=d_in[:], scalar=CUTOFF, in1=turns[:],
                                             op0=ALU.is_le, op1=ALU.mult).then_inc(dist_step, 1)
                    dve.wait_ge(dist_step, 7)
                    dve.tensor_tensor(turns[:], turns[:], d_abs[:], ALU.mult).then_inc(dist_step, 1)

                    dve.wait_ge(w_edges_in, 16 * (SEGS + 9))
                    dve.wait_ge(const_step, 7)
                    dve.tensor_scalar(w1[:], w1[:], row_scale[:, 0:1], float(CUTOFF / np.pi), ALU.mult, ALU.mult).then_inc(const_step, 1)
                    dve.tensor_scalar(w3[:], w3[:], float(HID ** -0.5), None, ALU.mult).then_inc(const_step, 1)

        passes = nc.values_load(passes_i[0:1, 0:1], min_val=1, max_val=NBLK)
        with ExitStack() as st:
            def s2(name, shape, dt=F32):
                return sb(name, shape, dt, st)

            sems = []

            def sem(name):
                sems.append(st.enter_context(nc.semaphore(name)))
                return sems[-1]

            key_all = s2("key_all", [P, GB, GROUP])
            src_ix = s2("src_ix", [P, SLOTS, TILES], I32)
            key = s2("key", [P, SLOTS, TILES])
            harm = s2("harm", [P, SLOTS, TILES, 4])
            lin_g = s2("lin_g", [P, SLOTS, TILES, DIM])
            aq = s2("aq", [SEGS, 2, SEG])
            k_turn = s2("k_turn", [P, SEG])
            frac = s2("frac", [P, SEG])
            sine = s2("sine", [P, SEG])
            rbf = s2("rbf", [P, SEG])
            h1 = s2("h1", [P, 2, UNIT])
            h2 = s2("h2", [P, HALF])
            onehot = s2("onehot", [P, 2, TILES, P])
            lin_sh = s2("lin_sh", [P, TILES, 3, MUL])
            dot2 = s2("dot2", [P, TILES, MUL])
            dot = s2("dot", [P, TILES, MUL])
            lin_sh0 = s2("lin_sh0", [P, 2, TILES, DIM])
            w_s = s2("w_s", [P, TILES, MUL])
            msg = s2("msg", [P, 2, TILES, COLS])
            ps_rbf = st.enter_context(nc.psum_tensor("ps_rbf", [P, 2, 256], F32))
            ps_h1 = st.enter_context(nc.psum_tensor("ps_h1", [P, 2, 512], F32))
            ps_h2 = st.enter_context(nc.psum_tensor("ps_h2", [P, 2, 512], F32))
            ps_w = st.enter_context(nc.psum_tensor("ps_w", [P, 8 * P], F32))
            ps_agg = st.enter_context(nc.psum_tensor("ps_agg", [P, 512], F32))

            key_step, key_out = sem("key_step"), sem("key_out")
            src_in = [sem(f"src_in{u}") for u in range(SLOTS)]
            key_in = [sem(f"key_in{u}") for u in range(SLOTS)]
            harm_in = [sem(f"harm_in{u}") for u in range(SLOTS)]
            gathered = [sem(f"gathered{u}") for u in range(SLOTS)]
            aq_in, blk_ready = sem("aq_in"), sem("blk_ready")
            rbf_spread, k_ready, frac_ready, sine_ready, rbf_ready = (
                sem("rbf_spread"), sem("k_ready"), sem("frac_ready"), sem("sine_ready"), sem("rbf_ready"))
            h1_done, h1_ready, h2_done, h2_ready = sem("h1_done"), sem("h1_ready"), sem("h2_done"), sem("h2_ready")
            w_ready, w_read, msg_ready, sums_ready = sem("w_ready"), sem("w_read"), sem("msg_ready"), sem("sums_ready")
            onehot_ready, lin_sh_ready, dot2_ready, dot_ready = (
                sem("onehot_ready"), sem("lin_sh_ready"), sem("dot2_ready"), sem("dot_ready"))
            lin_sh0_ready, w_s_ready, o00_ready, o10_ready = (
                sem("lin_sh0_ready"), sem("w_s_ready"), sem("o00_ready"), sem("o10_ready"))
            lo_added, agg_ready = sem("lo_added"), sem("agg_ready")

            def w_part(i):
                return ps_w[:, 0:TILES * P].rearrange("p (t w c) -> p t w c", t=TILES, c=MUL)[:, :, i, :]

            def sh_part(u, m):
                return harm[:, u, :, m].unsqueeze(2).to_broadcast([P, TILES, MUL])

            def sh_vec(u):
                return harm[:, u, :, 1:4].unsqueeze(3).to_broadcast([P, TILES, 3, MUL])

            def lin_s(u):
                return lin_g[:, u, :, 0:MUL]

            def lin_v(u):
                return lin_g[:, u, :, MUL:].rearrange("p t (m c) -> p t m c", m=3)

            def message(u):
                m = msg[:, u % 2]
                vec = m[:, :, 2 * MUL:MSG].rearrange("p t (m o c) -> p t m o c", m=3, o=2)
                return m[:, :, 0:MUL], m[:, :, MUL:2 * MUL], vec[:, :, :, 0, :], vec[:, :, :, 1, :]

            def spread_m(ap):
                return ap.unsqueeze(2).to_broadcast([P, TILES, 3, MUL])

            with nc.Fori(0, passes):
                with nc.Block() as block:
                    @block.sync
                    def _(sp):
                        def edges(i, u):
                            return bass.ds(i * QUAD + OFFSET[u], GROUP)

                        def load_src(i, u):
                            sp.dma_start(src_ix[:, u, :], src[edges(i, u)].rearrange("(p j) -> p j", j=TILES)).then_inc(src_in[u], 16)

                        def load_harm(i, u):
                            sp.dma_start(harm[:, u], sh[edges(i, u), :].rearrange("(p j) m -> p j m", j=TILES)).then_inc(harm_in[u], 16)

                        def load_key(i, u):
                            sp.dma_start(key[:, u, :], key_table[edges(i, u)].rearrange("(p j) -> p j", j=TILES)).then_inc(key_in[u], 16)

                        def load_aq(i):
                            for k, table in enumerate((a_table, q_table)):
                                sp.dma_start(aq[:, k, :], table[bass.ds(i * QUAD, QUAD)].rearrange("(s c) -> s c", s=SEGS)).then_inc(aq_in, 16)

                        for u in range(SLOTS):
                            load_src(0, u)
                        load_aq(0)
                        for u in range(SLOTS):
                            load_harm(0, u)
                        for b, n in group_blocks():
                            sp.wait_ge(key_step, 3 + 2 * (b + 1))
                            sp.dma_start(key_table[b * P * GROUP:(b * P + n) * GROUP].rearrange("(g e) -> g e", e=GROUP),
                                         key_all[0:n, b, :]).then_inc(key_out, 16)
                        sp.wait_ge(key_out, 16 * GB)
                        for u in range(SLOTS):
                            load_key(0, u)
                        sp.wait_ge(rbf_spread, 1)
                        load_aq(1)
                        with sp.Fori(0, ITERS) as i:
                            for u in range(SLOTS):
                                sp.wait_ge(gathered[u], 16 * TILES * (i + 1))
                                load_src(i + 1, u)
                                if u == 1:
                                    sp.wait_ge(rbf_spread, i + 2)
                                    load_aq(i + 2)
                                sp.wait_ge(msg_ready, i * SLOTS + u + 1)
                                load_key(i + 1, u)
                                load_harm(i + 1, u)
                        sp.wait_ge(aq_in, 32 * (ITERS + 2))
                        for u in range(SLOTS):
                            sp.wait_ge(src_in[u], 16 * (ITERS + 1))
                            sp.wait_ge(key_in[u], 16 * (ITERS + 1))
                            sp.wait_ge(harm_in[u], 16 * (ITERS + 1))

                    @block.gpsimd
                    def _(pool):
                        def gather(i, u, first=False):
                            pool.wait_ge(src_in[u], 16 * (i + 1))
                            if not first:
                                pool.wait_ge(w_s_ready, i * SLOTS + u - SLOTS + 1)
                            pool.nop(nofuse=True)
                            for j in range(TILES):
                                pool.indirect_dma_start(
                                    lin_g[:, u, j, :], None, lin_table,
                                    bass.IndirectOffsetOnAxis(ap=src_ix[:, u, j:j + 1], axis=0)).then_inc(gathered[u], 16)

                        for u in range(SLOTS):
                            gather(0, u, first=True)
                        with pool.Fori(1, ITERS) as i:
                            for u in range(SLOTS):
                                gather(i, u)
                        gather(ITERS, 0)

                    @block.tensor
                    def _(pe):
                        def spread_aq(i):
                            pe.wait_ge(aq_in, 32 * (i + 1))
                            at_least(pe, rbf_ready, i)
                            pe.matmul(ps_rbf[:, 0, 0:SEG], sel_freq[:], aq[:, 0, :], start=True, stop=True)
                            pe.matmul(ps_rbf[:, 1, 0:SEG], sel_one[:], aq[:, 1, :], start=True, stop=True).then_inc(rbf_spread, 1)

                        def layer1(i, k):
                            if k == 0:
                                pe.wait_ge(rbf_ready, i + 1)
                            at_least(pe, h1_ready, i * UNITS + k - 1)
                            for half in range(2):
                                mm = pe.matmul(ps_h1[:, k % 2, half * SEG:(half + 1) * SEG], w1[:, 2 * k + half, :], rbf[:],
                                               start=True, stop=True)
                            mm.then_inc(h1_done, 1)

                        def layer2(i, k):
                            pe.wait_ge(h1_ready, i * UNITS + k + 1)
                            at_least(pe, h2_ready, i * UNITS + k - 1)
                            pe.matmul(ps_h2[:, k % 2, 0:UNIT], w2[:], h1[:, k % 2, :], start=True, stop=True).then_inc(h2_done, 1)

                        def layer3(i, u):
                            units = 2 * (u // 2) + 2
                            pe.wait_ge(h2_ready, i * UNITS + units)
                            at_least(pe, w_read, i * SLOTS + u)
                            half = slice((u % 2) * HID, (u % 2) * HID + HID)
                            cols = h2[half, (u // 2) * GROUP:(u // 2 + 1) * GROUP].rearrange("p (c j) -> p j c", j=TILES)
                            for j in range(TILES):
                                mm = pe.matmul(ps_w[:, j * P:(j + 1) * P], cols[:, j, :], w3[half, :], start=True, stop=True)
                            mm.then_inc(w_ready, 1)

                        def segment_sum(i, u):
                            pe.wait_ge(msg_ready, i * SLOTS + u + 1)
                            pe.wait_ge(agg_ready, i * SLOTS + u + 1)
                            for j in range(TILES):
                                mm = pe.matmul(ps_agg[:, 0:COLS], onehot[:, u % 2, j, :], msg[:, u % 2, j, :],
                                               start=(j == 0), stop=(j == TILES - 1))
                            mm.then_inc(sums_ready, 1)

                        spread_aq(0)
                        layer1(0, 0)
                        layer1(0, 1)
                        layer2(0, 0)
                        layer1(0, 2)
                        layer2(0, 1)
                        layer1(0, 3)
                        layer2(0, 2)
                        layer2(0, 3)
                        layer3(0, 0)
                        with pe.Fori(0, ITERS) as i:
                            spread_aq(i + 1)
                            layer3(i, 1)
                            segment_sum(i, 0)
                            layer3(i, 2)
                            segment_sum(i, 1)
                            layer1(i + 1, 0)
                            layer1(i + 1, 1)
                            layer2(i + 1, 0)
                            layer3(i, 3)
                            segment_sum(i, 2)
                            layer2(i + 1, 1)
                            layer1(i + 1, 2)
                            layer1(i + 1, 3)
                            layer3(i + 1, 0)
                            segment_sum(i, 3)
                            layer2(i + 1, 2)
                            layer2(i + 1, 3)
                        segment_sum(ITERS, 0)

                    @block.scalar
                    def _(act):
                        def sines(i):
                            act.wait_ge(frac_ready, i + 1)
                            act.activation(sine[:], frac[:], ACT.Sin, scale=-TURN).then_inc(sine_ready, 1)

                        def silu1(i, k):
                            act.wait_ge(h1_done, i * UNITS + k + 1)
                            at_least(act, h2_done, i * UNITS + k - 1)
                            act.activation(h1[:, k % 2, :], ps_h1[:, k % 2, 0:UNIT], ACT.Silu,
                                           scale=float(RBF ** -0.5)).then_inc(h1_ready, 1)

                        def silu2(i, k):
                            act.wait_ge(h2_done, i * UNITS + k + 1)
                            at_least(act, w_ready, i * SLOTS - SLOTS + 2 * (k // 2) + 2)
                            act.activation(h2[:, k * UNIT:(k + 1) * UNIT], ps_h2[:, k % 2, 0:UNIT], ACT.Silu,
                                           scale=float(HID ** -0.5)).then_inc(h2_ready, 1)

                        def scale_lin(i, u):
                            n = i * SLOTS + u
                            act.wait_ge(gathered[u], 16 * TILES * (i + 1))
                            act.wait_ge(harm_in[u], 16 * (i + 1))
                            at_least(act, w_s_ready, n - 1)
                            for j in range(TILES):
                                last = act.activation(lin_sh0[:, u % 2, j, :], lin_g[:, u, j, :], ACT.Copy, scale=harm[:, u, j, 0:1])
                            last.then_inc(lin_sh0_ready, 1)

                        sines(0)
                        silu1(0, 0)
                        silu1(0, 1)
                        silu2(0, 0)
                        silu1(0, 2)
                        silu2(0, 1)
                        silu1(0, 3)
                        silu2(0, 2)
                        silu2(0, 3)
                        for u in range(3):
                            scale_lin(0, u)

                        def body(i, last=False):
                            sines(i + 1)
                            scale_lin(i, 3)
                            silu1(i + 1, 0)
                            silu1(i + 1, 1)
                            silu2(i + 1, 0)
                            scale_lin(i + 1, 0)
                            silu2(i + 1, 1)
                            silu1(i + 1, 2)
                            silu1(i + 1, 3)
                            if not last:
                                scale_lin(i + 1, 1)
                            silu2(i + 1, 2)
                            silu2(i + 1, 3)
                            if not last:
                                scale_lin(i + 1, 2)

                        with act.Fori(0, ITERS - 1) as i:
                            body(i)
                        body(ITERS - 1, last=True)

                    @block.vector
                    def _(dve):
                        dve.tensor_scalar(win_lo[:], win_lo[:], float(P), None, ALU.add).then_inc(key_step, 1)
                        dve.tensor_scalar(blk_f[:], blk_f[:], 1.0, None, ALU.add).then_inc(key_step, 1)
                        dve.wait_ge(key_step, 2)
                        dve.tensor_scalar(win_hi[:], win_lo[:], float(P), None, ALU.add).then_inc(key_step, 1)
                        dve.tensor_scalar(blk_i[:], blk_f[:], float(NBLK - 1), None, ALU.min).then_inc(blk_ready, 1)
                        dve.memset(msg[:, :, :, MSG:COLS], 1.0).then_inc(agg_ready, 1)
                        dve.wait_ge(key_step, 3)
                        for b, n in group_blocks():
                            dve.scalar_tensor_tensor(out=key_all[0:n, b, :], in0=dst_f[0:n, b, :], scalar=win_hi[0:n, b:b + 1],
                                                     in1=row1[0:n, b, :], op0=ALU.is_lt, op1=ALU.mult).then_inc(key_step, 1)
                            dve.wait_ge(key_step, 4 + 2 * b)
                            dve.scalar_tensor_tensor(out=key_all[0:n, b, :], in0=dst_f[0:n, b, :], scalar=win_lo[0:n, b:b + 1],
                                                     in1=key_all[0:n, b, :], op0=ALU.is_ge, op1=ALU.mult).then_inc(key_step, 1)

                        def fractions(i):
                            dve.wait_ge(rbf_spread, i + 1)
                            dve.tensor_scalar(k_turn[:], ps_rbf[:, 0, 0:SEG], ROUND, None, ALU.add).then_inc(k_ready, 1)
                            dve.wait_ge(k_ready, i + 1)
                            dve.scalar_tensor_tensor(out=frac[:], in0=k_turn[:], scalar=ROUND, in1=ps_rbf[:, 0, 0:SEG],
                                                     op0=ALU.subtract, op1=ALU.subtract).then_inc(frac_ready, 1)

                        def basis(i):
                            dve.wait_ge(sine_ready, i + 1)
                            at_least(dve, h1_done, i * UNITS)
                            dve.tensor_tensor(rbf[:], sine[:], ps_rbf[:, 1, 0:SEG], ALU.mult).then_inc(rbf_ready, 1)

                        def products(i, u):
                            dve.wait_ge(gathered[u], 16 * TILES * (i + 1))
                            dve.wait_ge(harm_in[u], 16 * (i + 1))
                            dve.tensor_tensor(lin_sh[:], lin_v(u), sh_vec(u), ALU.mult).then_inc(lin_sh_ready, 1)

                        def columns(i, u):
                            n = i * SLOTS + u
                            dve.wait_ge(key_in[u], 16 * (i + 1))
                            dve.tensor_tensor(onehot[:, u % 2], iota1[:].unsqueeze(1).to_broadcast([P, TILES, P]),
                                              key[:, u, :].unsqueeze(2).to_broadcast([P, TILES, P]), ALU.is_equal).then_inc(onehot_ready, 1)
                            dve.wait_ge(lin_sh_ready, n + 1)
                            dve.tensor_tensor(dot2[:], lin_sh[:, :, 0, :], lin_sh[:, :, 1, :], ALU.add).then_inc(dot2_ready, 1)
                            dve.wait_ge(dot2_ready, n + 1)
                            dve.tensor_tensor(dot[:], dot2[:], lin_sh[:, :, 2, :], ALU.add).then_inc(dot_ready, 1)

                        def late(i, u):
                            n = i * SLOTS + u
                            o00, o11, o01, o10 = message(u)
                            scaled = lin_sh0[:, u % 2]
                            dve.wait_ge(w_ready, n + 1)
                            dve.wait_ge(lin_sh0_ready, n + 1)
                            dve.tensor_tensor(o10, scaled[:, :, MUL:].rearrange("p t (m c) -> p t m c", m=3), spread_m(w_part(2)),
                                              ALU.mult).then_inc(o10_ready, 1)
                            dve.tensor_tensor(o00, scaled[:, :, 0:MUL], w_part(0), ALU.mult).then_inc(o00_ready, 1)
                            dve.tensor_tensor(w_s[:], w_part(1), lin_s(u), ALU.mult).then_inc(w_s_ready, 1)
                            dve.wait_ge(dot_ready, n + 1)
                            dve.scalar_tensor_tensor(out=o11, in0=dot[:], scalar=float(3 ** -0.5), in1=w_part(3),
                                                     op0=ALU.mult, op1=ALU.mult).then_inc(w_read, 1)
                            dve.wait_ge(w_s_ready, n + 1)
                            dve.tensor_tensor(o01, spread_m(w_s[:]), sh_vec(u), ALU.mult).then_inc(msg_ready, 1)

                        def accumulate(i, u):
                            n = i * SLOTS + u
                            g = i * SLOTS + OFFSET[u] // GROUP
                            blk = dve.value_load(blk_i[0:1, bass.ds(g, 1)], min_val=0, max_val=NBLK - 1)
                            dve.wait_ge(sums_ready, n + 1)
                            dve.wait_ge(agg_ready, n + 1)
                            for k, (part, added) in enumerate(((at_lo, lo_added), (at_hi, agg_ready))):
                                rows = agg[:, bass.ds(blk * COLS + k * COLS, COLS)]
                                dve.scalar_tensor_tensor(out=rows, in0=ps_agg[:, 0:COLS], scalar=part[:, bass.ds(g, 1)],
                                                         in1=rows, op0=ALU.mult, op1=ALU.add).then_inc(added, 1)

                        fractions(0)
                        basis(0)
                        dve.wait_ge(blk_ready, 1)
                        products(0, 0)
                        columns(0, 0)
                        late(0, 0)
                        products(0, 1)
                        columns(0, 1)

                        def body(i, last=False):
                            for u in range(SLOTS):
                                late(i + (u + 1) // SLOTS, (u + 1) % SLOTS)
                                if u == 0:
                                    fractions(i + 1)
                                ahead = None if last and u == SLOTS - 1 else (i + (u + 2) // SLOTS, (u + 2) % SLOTS)
                                if ahead:
                                    products(*ahead)
                                accumulate(i, u)
                                if ahead:
                                    columns(*ahead)
                                if u == 0:
                                    basis(i + 1)

                        with dve.Fori(0, ITERS - 1) as i:
                            body(i)
                        body(ITERS - 1, last=True)
                        accumulate(ITERS, 0)

                for s in sems:
                    nc.sync.sem_clear(s)
                nc.all_engine_barrier()

        with ExitStack() as st:
            def s3(name, shape, dt=F32):
                return sb(name, shape, dt, st)

            def sem(name):
                return st.enter_context(nc.semaphore(name))

            x3 = s3("x3", [P, 2, NB, DIM])
            sc3 = s3("sc3", [P, 2, NB, DIM])
            count = s3("count", [P, 2, NB])
            inv = s3("inv", [P, 2, NB])
            mean = s3("mean", [P, 2, NB, MSG])
            meanT = s3("meanT", [P, 2, 2, NB * P])
            pre = s3("pre", [P, 2, NB])
            alpha = s3("alpha", [P, 2, NB])
            gain = s3("gain", [P, 2, NB])
            upd = s3("upd", [P, 2, NB, DIM])
            res = s3("res", [P, 2, NB, DIM])
            ps_mT = st.enter_context(nc.psum_tensor("ps_mT", [P, 2, NB * P], F32))
            ps_l2 = st.enter_context(nc.psum_tensor("ps_l2", [P, 2, NB, DIM], F32))
            ps_al = st.enter_context(nc.psum_tensor("ps_al", [P, 2, 512], F32))

            in3 = [sem(f"in3_{b}") for b in range(2)]
            out3 = [sem(f"out3_{b}") for b in range(2)]
            count_ready, inv_ready, mean_ready, mT_done = sem("count_ready"), sem("inv_ready"), sem("mean_ready"), sem("mT_done")
            mT_lo, mT_hi, l2_done, pre_ready = sem("mT_lo"), sem("mT_hi"), sem("l2_done"), sem("pre_ready")
            alpha_ready, gain_ready, upd_ready, res_s, res_v = (
                sem("alpha_ready"), sem("gain_ready"), sem("upd_ready"), sem("res_s"), sem("res_v"))

            PRE = 2
            LOOPS = (STEPS - 2 - PRE) // 2
            AFTER = PRE + 2 * LOOPS

            def blocks_of(n):
                return REST if isinstance(n, int) and n == STEPS else NB

            def agg_step(n):
                k = blocks_of(n)
                return agg[:, bass.ds(n * (NB * COLS), k * COLS)].rearrange("p (b c) -> p b c", c=COLS)

            def steps(eng, body):
                for n in range(PRE):
                    body(n, n % 2)
                with eng.Fori(0, LOOPS) as t:
                    for j in range(2):
                        body(t * 2 + (PRE + j), (PRE + j) % 2)
                for n in range(AFTER, STEPS + 1):
                    body(n, n % 2)

            def within(n):
                return not isinstance(n, int) or 0 <= n <= STEPS

            with nc.Block() as block:
                @block.sync
                def _(sp):
                    def load(n, b):
                        if blocks_of(n) == NB:
                            sp.dma_start(x3[:, b], node_rows(x, n)).then_inc(in3[b], 16)
                            sp.dma_start(sc3[:, b], node_rows(sc_table, n)).then_inc(in3[b], 16)
                        else:
                            for r in range(REST):
                                sp.dma_start(x3[0:REST_ROWS[r], b, r], rest_rows(x, r)).then_inc(in3[b], 16)
                                sp.dma_start(sc3[0:REST_ROWS[r], b, r], rest_rows(sc_table, r)).then_inc(in3[b], 16)

                    def body(n, b):
                        sp.wait_ge(res_v, n + 1)
                        if within(n + 2):
                            load(n + 2, b)
                        if blocks_of(n) == NB:
                            sp.dma_start(node_rows(out, n), res[:, b]).then_inc(out3[b], 16)
                        else:
                            for r in range(REST):
                                sp.dma_start(rest_rows(out, r), res[0:REST_ROWS[r], b, r]).then_inc(out3[b], 16)

                    load(0, 0)
                    load(1, 1)
                    steps(sp, body)
                    for b in range(2):
                        whole = len(range(b, STEPS, 2))
                        sp.wait_ge(out3[b], 16 * (whole + (REST if b == STEPS % 2 else 0)))

                @block.vector
                def _(dve):
                    def inverse(n, b):
                        if not within(n):
                            return
                        k = blocks_of(n)
                        at_least(dve, mean_ready, n - 1)
                        dve.tensor_scalar(count[:, b, 0:k], agg_step(n)[:, :, MSG], 1.0, None, ALU.max).then_inc(count_ready, 1)
                        dve.wait_ge(count_ready, n + 1)
                        dve.reciprocal(inv[:, b, 0:k], count[:, b, 0:k]).then_inc(inv_ready, 1)

                    def update(n, b):
                        if not within(n):
                            return
                        k = blocks_of(n)
                        dve.wait_ge(alpha_ready, n + 1)
                        dve.tensor_tensor(gain[:, b, 0:k], alpha[:, b, 0:k], attr_lin2[:, bass.ds(n * NB, k)], ALU.mult).then_inc(gain_ready, 1)
                        loads = (n // 2 + 1) * 32 if isinstance(n, int) else (n - b) * 16 + 32
                        if k == REST:
                            loads = (n // 2) * 32 + 32 * REST
                        dve.wait_ge(in3[b], loads)
                        dve.wait_ge(gain_ready, n + 1)
                        at_least(dve, res_v, n - 1)
                        for j in range(k):
                            last = dve.scalar_tensor_tensor(out=upd[:, b, j, :], in0=ps_l2[:, b, j, :], scalar=gain[:, b, j:j + 1],
                                                            in1=sc3[:, b, j, :], op0=ALU.mult, op1=ALU.add)
                        last.then_inc(upd_ready, 1)

                    def body(n, b):
                        k = blocks_of(n)
                        dve.wait_ge(mT_done, n + 1)
                        at_least(dve, l2_done, n - 1)
                        dve.tensor_copy(meanT[:, b, 0, 0:k * P], ps_mT[:, 0, 0:k * P]).then_inc(mT_lo, 1)
                        update(n - 1, 1 - b)
                        inverse(n + 2, b)
                        dve.wait_ge(l2_done, n + 1)
                        at_least(dve, alpha_ready, n - 1)
                        dve.tensor_tensor(pre[:, b, 0:k], ps_al[:, b, 0:k], attr_lin2[:, bass.ds(n * NB, k)], ALU.mult).then_inc(pre_ready, 1)

                    inverse(0, 0)
                    inverse(1, 1)
                    steps(dve, body)
                    update(STEPS, STEPS % 2)

                @block.scalar
                def _(act):
                    def means(n, b):
                        if not within(n):
                            return
                        act.wait_ge(inv_ready, n + 1)
                        at_least(act, mT_done, n - 1)
                        for j in range(blocks_of(n)):
                            last = act.activation(mean[:, b, j, :], agg_step(n)[:, j, 0:MSG], ACT.Copy, scale=inv[:, b, j:j + 1])
                        last.then_inc(mean_ready, 1)

                    def body(n, b):
                        k = blocks_of(n)
                        act.wait_ge(mT_done, n + 1)
                        at_least(act, l2_done, n - 1)
                        act.activation(meanT[:, b, 1, 0:k * P], ps_mT[:, 1, 0:k * P], ACT.Copy).then_inc(mT_hi, 1)
                        means(n + 1, 1 - b)
                        act.wait_ge(pre_ready, n + 1)
                        at_least(act, gain_ready, n - 1)
                        act.activation(alpha[:, b, 0:k], pre[:, b, 0:k], ACT.Tanh).then_inc(alpha_ready, 1)

                    means(0, 0)
                    steps(act, body)

                @block.tensor
                def _(pe):
                    def turn(n, b):
                        if not within(n):
                            return
                        pe.wait_ge(mean_ready, n + 1)
                        at_least(pe, mT_lo, n)
                        at_least(pe, mT_hi, n)
                        for j in range(blocks_of(n)):
                            for c in range(2):
                                last = pe.transpose(ps_mT[:, c, j * P:(j + 1) * P], mean[:, b, j, c * P:(c + 1) * P], ident[:])
                        last.then_inc(mT_done, 1)

                    def body(n, b):
                        pe.wait_ge(mT_lo, n + 1)
                        pe.wait_ge(mT_hi, n + 1)
                        at_least(pe, upd_ready, n - 1)
                        for j in range(blocks_of(n)):
                            cols = slice(j * P, (j + 1) * P)
                            pe.matmul(ps_l2[:, b, j, 0:2 * MUL], meanT[:, b, 0, cols], w_lin2[:, 0, :], start=True, stop=True)
                            pe.matmul(ps_l2[:, b, j, 2 * MUL:], meanT[:, b, 1, cols], w_lin2[:, 1, :], start=True, stop=True)
                            last = pe.matmul(ps_al[:, b, j:j + 1], meanT[0:2 * MUL, b, 0, cols], w_alpha[:], start=True, stop=True)
                        last.then_inc(l2_done, 1)
                        turn(n + 1, 1 - b)

                    turn(0, 0)
                    steps(pe, body)

                @block.gpsimd
                def _(pool):
                    def body(n, b):
                        k = blocks_of(n)
                        pool.wait_ge(upd_ready, n + 1)
                        stores = (n // 2) * 16 if isinstance(n, int) else (n - b) * 8
                        at_least(pool, out3[b], stores)
                        pool.tensor_tensor(res[:, b, 0:k, 0:MUL], upd[:, b, 0:k, 0:MUL], x3[:, b, 0:k, 0:MUL], ALU.add).then_inc(res_s, 1)

                        def vec(t, order):
                            return t[:, b, 0:k, MUL:].rearrange(order, m=3)

                        pool.tensor_tensor(vec(res, "p b (c m) -> p b c m"), vec(upd, "p b (m c) -> p b c m"),
                                           vec(x3, "p b (c m) -> p b c m"), ALU.add).then_inc(res_v, 1)

                    steps(pool, body)


def kernel(x, src, dst, edge_attr_4, edge_weight, node_vec1, L0_gnn_sc_ws, L0_gnn_sc_wv, L0_gnn_lin1_ws, L0_gnn_lin1_wv,
           L0_gnn_fc_w1, L0_gnn_fc_w2, L0_gnn_fc_w3, L0_gnn_lin2_ws, L0_gnn_lin2_wv, L0_gnn_alpha_w):
    import concourse.bacc as bacc
    from concourse.bass_utils import run_bass_kernel_spmd

    def padded(a, n, fill):
        a = np.ascontiguousarray(a)
        return np.concatenate([a, np.full((n - a.shape[0],) + a.shape[1:], fill, a.dtype)])

    inputs = {
        "x": x, "src": padded(src, EDGES_PAD, 0), "dst": padded(dst, EDGES_PAD, NO_NODE),
        "edge_attr_4": padded(edge_attr_4, EDGES_PAD, 0), "edge_weight": padded(edge_weight, EDGES_PAD, 0),
        "node_vec1": node_vec1, "sc_ws": L0_gnn_sc_ws, "sc_wv": L0_gnn_sc_wv, "lin1_ws": L0_gnn_lin1_ws, "lin1_wv": L0_gnn_lin1_wv,
        "fc_w1": L0_gnn_fc_w1, "fc_w2": L0_gnn_fc_w2, "fc_w3": L0_gnn_fc_w3,
        "lin2_ws": L0_gnn_lin2_ws, "lin2_wv": L0_gnn_lin2_wv, "alpha_w": L0_gnn_alpha_w,
    }
    nc = bacc.Bacc("TRN2", target_bir_lowering=False, num_devices=1)
    arrays, args = {}, []
    for name, a in inputs.items():
        arrays[f"in_{name}"] = np.ascontiguousarray(a)
        args.append(nc.dram_tensor(f"in_{name}", arrays[f"in_{name}"].shape, mybir.dt.from_np(arrays[f"in_{name}"].dtype),
                                   kind="ExternalInput").ap())
    args.append(nc.dram_tensor("out_dram", (NODES, DIM), F32, kind="ExternalOutput").ap())
    gnn_kernel(nc, *args)
    return run_bass_kernel_spmd(nc, [arrays], core_ids=[0]).results[0]["out_dram"]
```

```python
from contextlib import ExitStack

import numpy as np

import concourse.bass as bass
from concourse import mybir

F32 = mybir.dt.float32
I32 = mybir.dt.int32
ALU = mybir.AluOpType
ACT = mybir.ActivationFunctionType
AX_X = mybir.AxisListType.X

P = 128
NODES, DIM = 12500, 128
EDGES = 200000
MUL, RBF, HID = 32, 8, 64
CUTOFF = 6.0
EPS = 1e-5

TILES = 6
GROUP = TILES * P
SLOTS = 4
QUAD = SLOTS * GROUP
ITERS = EDGES // QUAD
assert EDGES - ITERS * QUAD <= GROUP
HALF = QUAD // 2
SEGS = 16
SEG = QUAD // SEGS
UNIT = 2 * SEG
UNITS = HALF // UNIT
EDGES_PAD = (ITERS + 2) * QUAD
DCOLS = EDGES_PAD // P
GROUPS = (ITERS + 1) * SLOTS
OFFSET = [(u % 2) * HALF + (u // 2) * GROUP for u in range(SLOTS)]
NO_NODE = 1 << 20

NBLK = -(-NODES // P)
NB = 4
STEPS = NBLK // NB
REST = NBLK - STEPS * NB
REST_ROWS = [min(P, NODES - (STEPS * NB + j) * P) for j in range(REST)]
MSG = 8 * MUL
COLS = MSG + 1
TINY = 2e-5
FAR = 65536.0
ROUND = 1.5 * 2 ** 23
TURN = float(np.nextafter(np.float32(2 * np.pi), np.float32(0)))


def at_least(eng, sem, value):
    if not isinstance(value, int) or value > 0:
        eng.wait_ge(sem, value)


def gnn_kernel(nc, x, src, dst, sh, dist, node_vec, sc_ws, sc_wv, lin1_ws, lin1_wv,
               fc_w1, fc_w2, fc_w3, lin2_ws, lin2_wv, alpha_w, out):
    lin_table = nc.dram_tensor("lin_table", [NODES, DIM], F32, kind="Internal").ap()
    sc_table = nc.dram_tensor("sc_table", [NODES, DIM], F32, kind="Internal").ap()
    a_table = nc.dram_tensor("a_table", [EDGES_PAD], F32, kind="Internal").ap()
    q_table = nc.dram_tensor("q_table", [EDGES_PAD], F32, kind="Internal").ap()
    key_table = nc.dram_tensor("key_table", [GROUPS * GROUP], F32, kind="Internal").ap()

    def node_rows(table, step):
        return table[bass.ds(step * (NB * P), NB * P), :].rearrange("(b p) d -> p b d", p=P)

    def rest_rows(table, j):
        lo = (STEPS * NB + j) * P
        return table[lo:lo + REST_ROWS[j], :]

    def group_blocks():
        return [(b, min(P, GROUPS - b * P)) for b in range(-(-GROUPS // P))]

    GB = len(group_blocks())

    with ExitStack() as top:
        def sb(name, shape, dt=F32, ctx=top):
            return ctx.enter_context(nc.sbuf_tensor(name, shape, dt))

        agg = sb("agg", [P, (NBLK + 1) * COLS])
        ident = sb("ident", [P, P])
        iota1 = sb("iota1", [P, P])
        sel_freq = sb("sel_freq", [SEGS, P])
        sel_one = sb("sel_one", [SEGS, P])
        w1 = sb("w1", [P, SEGS // 2, P])
        w2 = sb("w2", [P, P])
        w3 = sb("w3", [P, P])
        w_lin2 = sb("w_lin2", [P, 2, DIM + 1])
        attr_lin = sb("attr_lin", [P, NBLK])
        attr_lin2 = sb("attr_lin2", [P, NBLK])
        dst_f = sb("dst_f", [P, GB, GROUP])
        row1 = sb("row1", [P, GB, GROUP])
        win_lo = sb("win_lo", [P, GB])
        win_hi = sb("win_hi", [P, GB])
        at_lo = sb("at_lo", [P, GROUPS])
        at_hi = sb("at_hi", [P, GROUPS])
        blk_f = sb("blk_f", [1, GROUPS])
        blk_i = sb("blk_i", [1, GROUPS], I32)
        passes_i = sb("passes_i", [1, 1], I32)

        with ExitStack() as st:
            def s1(name, shape, dt=F32):
                return sb(name, shape, dt, st)

            def sem(name):
                return st.enter_context(nc.semaphore(name))

            XB, OB = 6, 3
            xq = s1("xq", [P, XB, NB, DIM])
            bn = s1("bn", [P, 2, NB, 6])
            mean_var = s1("mean_var", [P, 2, NB, 2])
            eps = s1("eps", [P, 1])
            std = s1("std", [P, 2, NB])
            rstd = s1("rstd", [P, 2, NB])
            h = s1("h", [P, 2, NB, DIM])
            hT = s1("hT", [P, 2, NB * P])
            node_out = s1("node_out", [P, OB, NB, 2 * DIM])
            w_nodes = s1("w_nodes", [P, 2 * DIM])
            w_sc = s1("w_sc", [P, DIM])
            wv_in = s1("wv_in", [P, MUL])
            iota_i = s1("iota_i", [P, P], I32)
            freq_i = s1("freq_i", [SEGS, P], I32)
            freq = s1("freq", [SEGS, P])
            part_i = s1("part_i", [P, 1], I32)
            part_f = s1("part_f", [P, 1])
            rowf_i = s1("rowf_i", [P, 1], I32)
            rowf = s1("rowf", [P, 1])
            row_scale = s1("row_scale", [P, 1])
            ones = s1("ones", [P, P])
            attr_raw = s1("attr_raw", [NBLK, P])
            dst_i = s1("dst_i", [P, GB, GROUP], I32)
            least = s1("least", [P, GB])
            most = s1("most", [P, GB])
            span = s1("span", [P, GB])
            widest = s1("widest", [P, 1])
            base_diag = s1("base_diag", [P, GB, P])
            base_i = s1("base_i", [P, GROUPS], I32)
            off_i = s1("off_i", [P, GROUPS], I32)
            off_f = s1("off_f", [P, GROUPS])
            blk0_i = s1("blk0_i", [1, GROUPS], I32)
            span_max = s1("span_max", [1, 1])
            span_i = s1("span_i", [1, 1], I32)
            more_i = s1("more_i", [1, 1], I32)
            d_in = s1("d_in", [P, DCOLS])
            d_abs = s1("d_abs", [P, DCOLS])
            a_all = s1("a_all", [P, DCOLS])
            turns = s1("turns", [P, DCOLS])
            psT = st.enter_context(nc.psum_tensor("psT", [P, 2, NB * P], F32))
            psN = st.enter_context(nc.psum_tensor("psN", [P, 2, NB, 2 * DIM], F32))
            psW = st.enter_context(nc.psum_tensor("psW", [P, 512], F32))
            psA = st.enter_context(nc.psum_tensor("psA", [P, 512], F32))

            x_in = [sem(f"x_in{b}") for b in range(XB)]
            stored = [sem(f"stored{b}") for b in range(OB)]
            dist_in, dst_in, attr_in = sem("dist_in"), sem("dst_in"), sem("attr_in")
            w_nodes_in, w_edges_in, tables_out, wv_landed = sem("w_nodes_in"), sem("w_edges_in"), sem("tables_out"), sem("wv_landed")
            zeroed, shaped, iotas, ones_set = sem("zeroed"), sem("shaped"), sem("iotas"), sem("ones_set")
            bn_done, aggr_done, std_ready = sem("bn_done"), sem("aggr_done"), sem("std_ready")
            rstd_ready, h_ready, recip_ready = sem("rstd_ready"), sem("h_ready"), sem("recip_ready")
            transposed, hT_ready, nodes_done, evacuated = sem("transposed"), sem("hT_ready"), sem("nodes_done"), sem("evacuated")
            attr_turned, attr_ready = sem("attr_turned"), sem("attr_ready")
            const_step, win_step, spread, span_row = sem("const_step"), sem("win_step"), sem("spread"), sem("span_row")
            abs_ready, dist_step, cos_ready = sem("abs_ready"), sem("dist_step"), sem("cos_ready")
            agg_zero, diag_ready, w_sc_in, w_sc_done, eps_set, dst_real = (
                sem("agg_zero"), sem("diag_ready"), sem("w_sc_in"), sem("w_sc_done"), sem("eps_set"), sem("dst_real"))

            UNROLL = XB
            LOOPS = (STEPS - UNROLL) // UNROLL
            PEELED = LOOPS * UNROLL

            with nc.Block() as block:
                @block.sync
                def _(sp):
                    def load_x(t, j):
                        t, b = t + j // XB, j % XB
                        sp.dma_start(xq[:, b], node_rows(x, t * XB + b)).then_inc(x_in[b], 16)

                    def load_rest():
                        b = STEPS % XB
                        for r in range(REST):
                            sp.dma_start(xq[0:REST_ROWS[r], b, r], rest_rows(x, r)).then_inc(x_in[b], 16)

                    def store(t, j):
                        n, b = t * UNROLL + j, j % OB
                        sp.wait_ge(evacuated, n + 1)
                        sp.dma_start(node_rows(lin_table, n), node_out[:, b, :, 0:DIM]).then_inc(stored[b], 16)
                        sp.dma_start(node_rows(sc_table, n), node_out[:, b, :, DIM:]).then_inc(stored[b], 16)

                    for b, n in group_blocks():
                        sp.dma_start(dst_i[0:n, b, :], dst[b * P * GROUP:(b * P + n) * GROUP].rearrange("(g e) -> g e", e=GROUP)).then_inc(dst_in, 16)
                    sp.dma_start(d_in[:], dist.rearrange("(p c) -> p c", p=P)).then_inc(dist_in, 16)
                    for j in range(XB):
                        load_x(0, j)
                    sp.wait_ge(zeroed, 1)
                    sp.dma_start(attr_raw[0:NBLK - 1, :], node_vec[0:(NBLK - 1) * P, :].rearrange("(b p) o -> b (p o)", p=P)).then_inc(attr_in, 16)
                    sp.dma_start(attr_raw[NBLK - 1:NBLK, 0:NODES - (NBLK - 1) * P],
                                 node_vec[(NBLK - 1) * P:, :].rearrange("(b p) o -> b (p o)", b=1)).then_inc(attr_in, 16)
                    for half in range(2):
                        rows = slice(half * HID, (half + 1) * HID)
                        sp.dma_start(wv_in[rows, :], lin2_wv).then_inc(wv_landed, 16)
                    sp.wait_ge(zeroed, 7)
                    for s in range(SEGS):
                        half, q = s // (SEGS // 2), s % (SEGS // 2)
                        sp.dma_start(w1[s * RBF:(s + 1) * RBF, q, half * HID:(half + 1) * HID], fc_w1).then_inc(w_edges_in, 16)
                    for half in range(2):
                        rows = slice(half * HID, (half + 1) * HID)
                        sp.dma_start(w2[rows, rows], fc_w2).then_inc(w_edges_in, 16)
                        sp.dma_start(w3[rows, :], fc_w3).then_inc(w_edges_in, 16)
                    sp.dma_start(w_lin2[0:HID, 0, 0:MUL], lin2_ws).then_inc(w_edges_in, 16)
                    sp.dma_start(w_lin2[0:HID, 0, DIM:], alpha_w).then_inc(w_edges_in, 16)
                    with sp.Fori(0, LOOPS) as t:
                        for j in range(UNROLL):
                            sp.wait_ge(h_ready, t * UNROLL + j + 1)
                            load_x(t, j + XB)
                            store(t, j)
                    for k in range(PEELED, STEPS):
                        if k + XB == STEPS:
                            sp.wait_ge(h_ready, k + 1)
                            load_rest()
                        store(k // UNROLL, k % UNROLL)
                    b = STEPS % OB
                    sp.wait_ge(evacuated, STEPS + 1)
                    for r in range(REST):
                        sp.dma_start(rest_rows(lin_table, r), node_out[0:REST_ROWS[r], b, r, 0:DIM]).then_inc(stored[b], 16)
                    for r in range(REST):
                        sp.dma_start(rest_rows(sc_table, r), node_out[0:REST_ROWS[r], b, r, DIM:]).then_inc(stored[b], 16)
                    sp.wait_ge(dist_step, 1)
                    sp.dma_start(a_table.rearrange("(p c) -> p c", p=P), a_all[:]).then_inc(tables_out, 16)
                    sp.wait_ge(dist_step, 9)
                    sp.dma_start(q_table.rearrange("(p c) -> p c", p=P), turns[:]).then_inc(tables_out, 16)
                    sp.wait_ge(tables_out, 32)
                    for b in range(OB):
                        steps = len(range(b, STEPS, OB))
                        sp.wait_ge(stored[b], 32 * steps + (32 * REST if b == STEPS % OB else 0))

                @block.gpsimd
                def _(pool):
                    pool.memset(attr_raw[:], 0.0).then_inc(zeroed, 1)
                    pool.memset(w_nodes[:], 0.0).then_inc(zeroed, 1)
                    pool.memset(w_sc[:], 0.0).then_inc(zeroed, 1)
                    pool.memset(ident[:], 0.0).then_inc(zeroed, 1)
                    pool.memset(w1[:], 0.0).then_inc(zeroed, 1)
                    pool.memset(w2[:], 0.0).then_inc(zeroed, 1)
                    pool.memset(w_lin2[:], 0.0).then_inc(zeroed, 1)
                    pool.memset(eps[:], EPS).then_inc(eps_set, 1)
                    pool.memset(ones[:], 1.0).then_inc(ones_set, 1)
                    pool.memset(sel_one[:], 1.0).then_inc(ones_set, 1)
                    pool.memset(least[:], 0.0).then_inc(ones_set, 1)
                    pool.memset(span[:], 0.0).then_inc(ones_set, 1)
                    pool.wait_ge(zeroed, 4)
                    pool.affine_select(out=ident[:], in_=ident[:], compare_op=ALU.not_equal, fill=1.0, base=0,
                                       pattern=[[-1, P]], channel_multiplier=1).then_inc(shaped, 1)
                    pool.iota(iota_i[:], pattern=[[1, P]], base=1, channel_multiplier=0).then_inc(iotas, 1)
                    pool.iota(part_i[:], pattern=[[0, 1]], base=0, channel_multiplier=1).then_inc(iotas, 1)
                    pool.iota(freq_i[:], pattern=[[0, SEGS], [1, RBF]], base=1, channel_multiplier=0).then_inc(iotas, 1)
                    pool.wait_ge(ones_set, 2)
                    pool.affine_select(out=sel_one[:], in_=sel_one[:], compare_op=ALU.is_ge, fill=0.0, base=0,
                                       pattern=[[1, P]], channel_multiplier=-RBF).then_inc(shaped, 1)
                    pool.wait_ge(shaped, 2)
                    pool.affine_select(out=sel_one[:], in_=sel_one[:], compare_op=ALU.is_ge, fill=0.0, base=RBF - 1,
                                       pattern=[[-1, P]], channel_multiplier=RBF).then_inc(shaped, 1)
                    pool.wait_ge(abs_ready, 1)
                    pool.tensor_scalar(a_all[:], d_abs[:], TINY, FAR, ALU.max, ALU.min).then_inc(dist_step, 1)
                    pool.wait_ge(dist_step, 1)
                    pool.tensor_scalar(turns[:], a_all[:], 1.0 / (2 * CUTOFF), 0.25, ALU.mult, ALU.add).then_inc(dist_step, 1)
                    pool.wait_ge(dist_step, 2)
                    pool.tensor_scalar(d_abs[:], turns[:], ROUND, None, ALU.add).then_inc(dist_step, 1)
                    pool.wait_ge(dist_step, 3)
                    pool.tensor_scalar(d_abs[:], d_abs[:], ROUND, None, ALU.subtract).then_inc(dist_step, 1)
                    pool.wait_ge(dist_step, 4)
                    pool.tensor_tensor(turns[:], d_abs[:], turns[:], ALU.subtract).then_inc(dist_step, 1)
                    pool.memset(agg[:], 0.0).then_inc(agg_zero, 1)
                    pool.wait_ge(cos_ready, 1)
                    pool.tensor_scalar(turns[:], turns[:], 0.5, 0.5, ALU.mult, ALU.add).then_inc(dist_step, 1)
                    pool.tensor_scalar(d_in[:], d_in[:], CUTOFF, None, ALU.is_le).then_inc(dist_step, 1)
                    pool.wait_ge(dist_step, 7)
                    pool.tensor_tensor(turns[:], turns[:], d_in[:], ALU.mult).then_inc(dist_step, 1)

                @block.scalar
                def _(act):
                    act.wait_ge(zeroed, 3)
                    for w, ws, wv, landed in ((w_nodes, lin1_ws, lin1_wv, w_nodes_in), (w_sc, sc_ws, sc_wv, w_sc_in)):
                        act.dma_start(w[0:MUL, 0:MUL], ws).then_inc(landed, 16)
                        for m in range(3):
                            lo = (m + 1) * MUL
                            act.dma_start(w[MUL + m:DIM:3, lo:lo + MUL], wv).then_inc(landed, 16)

                    def sqrt(t, j):
                        n, b = t * UNROLL + j, j % 2
                        act.wait_ge(aggr_done, n * NB + NB)
                        at_least(act, rstd_ready, n - 1)
                        act.activation(std[:, b, :], mean_var[:, b, :, 1], ACT.Sqrt, bias=eps[:, 0:1]).then_inc(std_ready, 1)

                    def copy_hT(t, j, blocks=NB):
                        n, b = t * UNROLL + j, j % 2
                        act.wait_ge(transposed, n + 1)
                        at_least(act, nodes_done, n - 1)
                        act.activation(hT[:, b, 0:blocks * P], psT[:, b, 0:blocks * P], ACT.Relu).then_inc(hT_ready, 1)

                    def evacuate(t, j, blocks=NB):
                        n, b = t * UNROLL + j, j % OB
                        act.wait_ge(nodes_done, n + 1)
                        at_least(act, stored[b], 32 * (t * (UNROLL // OB) + j // OB))
                        for k in range(blocks):
                            blk = n * NB + k
                            last = act.activation(node_out[:, b, k, :], psN[:, j % 2, k, :], ACT.Copy,
                                                  scale=attr_lin[:, bass.ds(blk, 1)])
                        last.then_inc(evacuated, 1)

                    def step(t, j):
                        n = t * UNROLL + j
                        ahead = not isinstance(n, int)
                        if ahead or n + 2 <= STEPS:
                            sqrt(t, j + 2)
                        if ahead or n + 1 <= STEPS:
                            copy_hT(t, j + 1, NB if ahead or n + 1 < STEPS else REST)
                        evacuate(t, j, NB if ahead or n < STEPS else REST)

                    act.wait_ge(dist_in, 16)
                    act.activation(d_abs[:], d_in[:], ACT.Abs).then_inc(abs_ready, 1)
                    act.wait_ge(dst_in, 16 * GB)
                    for b, n in group_blocks():
                        act.activation(dst_f[0:n, b, :], dst_i[0:n, b, :], ACT.Copy).then_inc(dst_real, 1)
                    act.wait_ge(eps_set, 1)
                    sqrt(0, 0)
                    sqrt(0, 1)
                    copy_hT(0, 0)
                    act.wait_ge(attr_ready, 2)
                    for j in range(UNROLL):
                        step(0, j)
                    act.wait_ge(dist_step, 5)
                    act.activation(turns[:], turns[:], ACT.Sin, scale=-TURN).then_inc(cos_ready, 1)
                    with act.Fori(1, LOOPS) as t:
                        for j in range(UNROLL):
                            step(t, j)
                    for n in range(PEELED, STEPS + 1):
                        step(n // UNROLL, n % UNROLL)

                @block.tensor
                def _(pe):
                    def turn(t, j, blocks=NB):
                        n, b = t * UNROLL + j, j % 2
                        pe.wait_ge(h_ready, n + 1)
                        at_least(pe, hT_ready, n - 1)
                        for k in range(blocks):
                            last = pe.transpose(psT[:, b, k * P:(k + 1) * P], h[:, b, k, :], ident[:])
                        last.then_inc(transposed, 1)

                    def product(t, j, blocks=NB):
                        n, b = t * UNROLL + j, j % 2
                        pe.wait_ge(hT_ready, n + 1)
                        at_least(pe, evacuated, n - 1)
                        for k in range(blocks):
                            last = pe.matmul(psN[:, b, k, :], hT[:, b, k * P:(k + 1) * P], w_nodes[:], start=True, stop=True)
                        last.then_inc(nodes_done, 1)

                    pe.wait_ge(shaped, 1)
                    pe.wait_ge(attr_in, 32)
                    pe.transpose(psA[:, 0:NBLK], attr_raw[:], ident[0:NBLK, 0:NBLK]).then_inc(attr_turned, 1)
                    turn(0, 0)
                    pe.wait_ge(w_nodes_in, 16 * 4)
                    pe.wait_ge(w_sc_done, 2)
                    for j in range(UNROLL):
                        turn(0, j + 1)
                        product(0, j)
                    with pe.Fori(1, LOOPS) as t:
                        for j in range(UNROLL):
                            turn(t, j + 1)
                            product(t, j)
                    for n in range(PEELED, STEPS + 1):
                        if n < STEPS:
                            turn(n // UNROLL, n % UNROLL + 1, NB if n + 1 < STEPS else REST)
                        product(n // UNROLL, n % UNROLL, NB if n < STEPS else REST)

                    pe.wait_ge(ones_set, 1)
                    pe.wait_ge(diag_ready, GB)
                    for b, n in group_blocks():
                        last = pe.matmul(psW[:, b * P:b * P + n], ones[0:n, :], base_diag[0:n, b, 0:n], start=True, stop=True)
                    last.then_inc(spread, 1)
                    pe.wait_ge(win_step, 7 * GB + 1)
                    pe.wait_ge(attr_ready, 2)
                    pe.matmul(psA[0:1, 0:P], widest[:], ident[:], start=True, stop=True).then_inc(span_row, 1)

                @block.vector
                def _(dve):
                    done = {"const": 0, "win": 0}

                    dve.wait_ge(iotas, 3)
                    dve.tensor_copy(iota1[:], iota_i[:]).then_inc(const_step, 1)
                    dve.tensor_copy(part_f[:], part_i[:]).then_inc(const_step, 1)
                    dve.tensor_copy(freq[:], freq_i[:]).then_inc(const_step, 1)
                    dve.tensor_scalar(rowf_i[:], part_i[:], RBF - 1, None, ALU.bitwise_and).then_inc(const_step, 1)
                    dve.wait_ge(const_step, 4)
                    dve.tensor_scalar(rowf[:], rowf_i[:], 1.0, None, ALU.add).then_inc(const_step, 1)
                    dve.wait_ge(shaped, 3)
                    dve.scalar_tensor_tensor(out=sel_freq[:], in0=freq[:], scalar=1.0 / (2 * CUTOFF), in1=sel_one[:],
                                             op0=ALU.mult, op1=ALU.mult).then_inc(const_step, 1)
                    dve.wait_ge(const_step, 5)
                    dve.reciprocal(row_scale[:], rowf[:]).then_inc(const_step, 1)
                    def stats(t, j, blocks=NB):
                        n, b = t * UNROLL + j, j % 2
                        landed = 16 * (t + j // XB + 1)
                        dve.wait_ge(x_in[j % XB], landed if blocks == NB else landed - 16 + 16 * REST)
                        for k in range(NB):
                            dve.bn_stats(bn[:, b, k, :], xq[:, j % XB, k, :]).then_inc(bn_done, 1)
                        dve.wait_ge(bn_done, n * NB + NB)
                        dve.nop(nofuse=True)
                        for k in range(NB):
                            dve.bn_aggr(mean_var[:, b, k, :], bn[:, b, k, :]).then_inc(aggr_done, 1)

                    def normalize(t, j, blocks=NB):
                        n, b = t * UNROLL + j, j % 2
                        dve.wait_ge(std_ready, n + 1)
                        at_least(dve, transposed, n - 1)
                        dve.reciprocal(rstd[:, b, :], std[:, b, :]).then_inc(rstd_ready, 1)
                        dve.wait_ge(rstd_ready, n + 1)
                        for k in range(blocks):
                            last = dve.tensor_scalar(h[:, b, k, :], xq[:, j % XB, k, :], mean_var[:, b, k, 0:1], rstd[:, b, k:k + 1],
                                                     ALU.subtract, ALU.mult)
                        last.then_inc(h_ready, 1)

                    def step(t, j):
                        n = t * UNROLL + j
                        ahead = not isinstance(n, int)
                        if ahead or n + 1 <= STEPS:
                            normalize(t, j + 1, NB if ahead or n + 1 < STEPS else REST)
                        if ahead or n + 3 <= STEPS:
                            stats(t, j + 3, NB if ahead or n + 3 < STEPS else REST)

                    win = 0
                    dve.wait_ge(ones_set, 4)
                    for b, n in group_blocks():
                        dve.wait_ge(dst_real, b + 1)
                        dve.tensor_scalar(dst_i[0:n, b, :], dst_i[0:n, b, :], P - 1, None, ALU.bitwise_and).then_inc(win_step, 1)
                        dve.tensor_reduce(least[0:n, b:b + 1], dst_f[0:n, b, :], AX_X, ALU.min).then_inc(win_step, 1)
                        dve.scalar_tensor_tensor(out=row1[0:n, b, :], in0=dst_f[0:n, b, :], scalar=float(NODES), in1=dst_f[0:n, b, :],
                                                 op0=ALU.is_lt, op1=ALU.mult).then_inc(win_step, 1)
                        dve.wait_ge(win_step, win + 3)
                        dve.tensor_reduce(most[0:n, b:b + 1], row1[0:n, b, :], AX_X, ALU.max).then_inc(win_step, 1)
                        dve.wait_ge(win_step, win + 4)
                        dve.tensor_scalar(row1[0:n, b, :], dst_i[0:n, b, :], 1.0, None, ALU.add).then_inc(win_step, 1)
                        dve.tensor_scalar(least[0:n, b:b + 1], least[0:n, b:b + 1], float(NODES - 1), None, ALU.min).then_inc(win_step, 1)
                        dve.wait_ge(win_step, win + 6)
                        dve.tensor_tensor(span[0:n, b:b + 1], most[0:n, b:b + 1], least[0:n, b:b + 1], ALU.subtract).then_inc(win_step, 1)
                        dve.tensor_scalar(base_diag[0:n, b, :], ident[0:n, :], least[0:n, b:b + 1], None, ALU.mult).then_inc(diag_ready, 1)
                        win += 7

                    stats(0, 0)
                    stats(0, 1)
                    normalize(0, 0)
                    dve.wait_ge(attr_turned, 1)
                    dve.tensor_scalar(attr_lin[:], psA[:, 0:NBLK], float(MUL ** -0.5), None, ALU.mult).then_inc(attr_ready, 1)
                    dve.tensor_scalar(attr_lin2[:], psA[:, 0:NBLK], float((2 * MUL) ** -0.5), None, ALU.mult).then_inc(attr_ready, 1)
                    def by_m(t):
                        return t.rearrange("p (c m) -> p m c", m=3)

                    dve.wait_ge(w_sc_in, 16 * 4)
                    dve.tensor_copy(w_nodes[:, DIM:DIM + MUL], w_sc[:, 0:MUL]).then_inc(w_sc_done, 1)
                    dve.tensor_copy(by_m(w_nodes[:, DIM + MUL:]), w_sc[:, MUL:].rearrange("p (m c) -> p m c", m=3)).then_inc(w_sc_done, 1)
                    dve.wait_ge(wv_landed, 16 * 2)
                    for c, half, m in ((0, 1, 0), (1, 0, 1), (1, 1, 2)):
                        rows = slice(half * HID, (half + 1) * HID)
                        dve.tensor_copy(by_m(w_lin2[rows, c, MUL:DIM])[:, m, :], wv_in[rows, :]).then_inc(w_sc_done, 1)
                    stats(0, 2)
                    for j in range(UNROLL):
                        step(0, j)
                    with dve.Fori(1, LOOPS) as t:
                        for j in range(UNROLL):
                            step(t, j)
                    for n in range(PEELED, STEPS + 1):
                        step(n // UNROLL, n % UNROLL)

                    dve.wait_ge(dist_step, 5)
                    dve.reciprocal(d_abs[:], a_all[:]).then_inc(recip_ready, 1)

                    dve.wait_ge(win_step, win)
                    dve.tensor_reduce(widest[:], span[:], AX_X, ALU.max).then_inc(win_step, 1)
                    dve.tensor_scalar(win_lo[:], least[:], float(-P), None, ALU.add).then_inc(win_step, 1)
                    dve.wait_ge(spread, 1)
                    dve.tensor_copy(base_i[:], psW[:, 0:GROUPS]).then_inc(win_step, 1)
                    dve.wait_ge(win_step, win + 3)
                    dve.tensor_scalar(off_i[:], base_i[:], P - 1, None, ALU.bitwise_and).then_inc(win_step, 1)
                    dve.tensor_scalar(blk0_i[:], base_i[0:1, :], 7, None, ALU.logical_shift_right).then_inc(win_step, 1)
                    dve.wait_ge(win_step, win + 4)
                    dve.tensor_copy(off_f[:], off_i[:]).then_inc(win_step, 1)
                    dve.wait_ge(win_step, win + 6)
                    dve.tensor_scalar(at_lo[:], off_f[:], part_f[:, 0:1], None, ALU.is_le).then_inc(win_step, 1)
                    dve.tensor_scalar(at_hi[:], off_f[:], part_f[:, 0:1], None, ALU.is_gt).then_inc(win_step, 1)
                    dve.tensor_scalar(blk_f[:], blk0_i[:], -1.0, None, ALU.add).then_inc(win_step, 1)
                    dve.wait_ge(span_row, 1)
                    dve.tensor_reduce(span_max[:], psA[0:1, 0:P], AX_X, ALU.max).then_inc(win_step, 1)
                    dve.wait_ge(win_step, win + 10)
                    dve.tensor_copy(span_i[:], span_max[:]).then_inc(win_step, 1)
                    dve.wait_ge(win_step, win + 11)
                    dve.tensor_scalar(more_i[:], span_i[:], 7, None, ALU.logical_shift_right).then_inc(win_step, 1)
                    dve.wait_ge(win_step, win + 12)
                    dve.tensor_scalar(passes_i[:], more_i[:], 1.0, None, ALU.add).then_inc(win_step, 1)

                    dve.wait_ge(recip_ready, 1)
                    dve.wait_ge(dist_step, 8)
                    dve.tensor_tensor(turns[:], turns[:], d_abs[:], ALU.mult).then_inc(dist_step, 1)

                    dve.wait_ge(w_edges_in, 16 * (SEGS + 6))
                    dve.wait_ge(const_step, 7)
                    dve.tensor_scalar(w1[:], w1[:], row_scale[:, 0:1], float(CUTOFF / np.pi), ALU.mult, ALU.mult).then_inc(const_step, 1)
                    dve.tensor_scalar(w3[:], w3[:], float(HID ** -0.5), None, ALU.mult).then_inc(const_step, 1)

        passes = nc.values_load(passes_i[0:1, 0:1], min_val=1, max_val=NBLK)
        with ExitStack() as st:
            def s2(name, shape, dt=F32):
                return sb(name, shape, dt, st)

            sems = []

            def sem(name):
                sems.append(st.enter_context(nc.semaphore(name)))
                return sems[-1]

            key_all = s2("key_all", [P, GB, GROUP])
            src_ix = s2("src_ix", [P, SLOTS, TILES], I32)
            key = s2("key", [P, SLOTS, TILES])
            harm = s2("harm", [P, SLOTS, TILES, 4])
            lin_g = s2("lin_g", [P, SLOTS, TILES, DIM])
            aq = s2("aq", [SEGS, 2, SEG])
            k_turn = s2("k_turn", [P, SEG])
            frac = s2("frac", [P, SEG])
            sine = s2("sine", [P, SEG])
            rbf = s2("rbf", [P, SEG])
            h1 = s2("h1", [P, 2, UNIT])
            h2 = s2("h2", [P, HALF])
            onehot = s2("onehot", [P, 2, TILES, P])
            lin_sh = s2("lin_sh", [P, TILES, 3, MUL])
            dot2 = s2("dot2", [P, TILES, MUL])
            dot = s2("dot", [P, TILES, MUL])
            lin_sh0 = s2("lin_sh0", [P, 2, TILES, DIM])
            w_s = s2("w_s", [P, TILES, MUL])
            msg = s2("msg", [P, 2, TILES, COLS])
            ps_rbf = st.enter_context(nc.psum_tensor("ps_rbf", [P, 2, 256], F32))
            ps_h1 = st.enter_context(nc.psum_tensor("ps_h1", [P, 2, 512], F32))
            ps_h2 = st.enter_context(nc.psum_tensor("ps_h2", [P, 2, 512], F32))
            ps_w = st.enter_context(nc.psum_tensor("ps_w", [P, 8 * P], F32))
            ps_agg = st.enter_context(nc.psum_tensor("ps_agg", [P, 512], F32))

            key_step, key_out = sem("key_step"), sem("key_out")
            src_in = [sem(f"src_in{u}") for u in range(SLOTS)]
            key_in = [sem(f"key_in{u}") for u in range(SLOTS)]
            harm_in = [sem(f"harm_in{u}") for u in range(SLOTS)]
            gathered = [sem(f"gathered{u}") for u in range(SLOTS)]
            aq_in, blk_ready = sem("aq_in"), sem("blk_ready")
            rbf_spread, k_ready, frac_ready, sine_ready, rbf_ready = (
                sem("rbf_spread"), sem("k_ready"), sem("frac_ready"), sem("sine_ready"), sem("rbf_ready"))
            h1_done, h1_ready, h2_done, h2_ready = sem("h1_done"), sem("h1_ready"), sem("h2_done"), sem("h2_ready")
            w_ready, w_read, msg_ready, sums_ready = sem("w_ready"), sem("w_read"), sem("msg_ready"), sem("sums_ready")
            onehot_ready, lin_sh_ready, dot2_ready, dot_ready = (
                sem("onehot_ready"), sem("lin_sh_ready"), sem("dot2_ready"), sem("dot_ready"))
            lin_sh0_ready, w_s_ready, o00_ready, o10_ready = (
                sem("lin_sh0_ready"), sem("w_s_ready"), sem("o00_ready"), sem("o10_ready"))
            lo_added, agg_ready = sem("lo_added"), sem("agg_ready")

            def w_part(i):
                return ps_w[:, 0:TILES * P].rearrange("p (t w c) -> p t w c", t=TILES, c=MUL)[:, :, i, :]

            def sh_part(u, m):
                return harm[:, u, :, m].unsqueeze(2).to_broadcast([P, TILES, MUL])

            def sh_vec(u):
                return harm[:, u, :, 1:4].unsqueeze(3).to_broadcast([P, TILES, 3, MUL])

            def lin_s(u):
                return lin_g[:, u, :, 0:MUL]

            def lin_v(u):
                return lin_g[:, u, :, MUL:].rearrange("p t (m c) -> p t m c", m=3)

            def message(u):
                m = msg[:, u % 2]
                vec = m[:, :, 2 * MUL:MSG].rearrange("p t (m o c) -> p t m o c", m=3, o=2)
                return m[:, :, 0:MUL], m[:, :, MUL:2 * MUL], vec[:, :, :, 0, :], vec[:, :, :, 1, :]

            def spread_m(ap):
                return ap.unsqueeze(2).to_broadcast([P, TILES, 3, MUL])

            with nc.Fori(0, passes):
                with nc.Block() as block:
                    @block.sync
                    def _(sp):
                        def edges(i, u):
                            return bass.ds(i * QUAD + OFFSET[u], GROUP)

                        def load_src(i, u):
                            sp.dma_start(src_ix[:, u, :], src[edges(i, u)].rearrange("(p j) -> p j", j=TILES)).then_inc(src_in[u], 16)

                        def load_harm(i, u):
                            sp.dma_start(harm[:, u], sh[edges(i, u), :].rearrange("(p j) m -> p j m", j=TILES)).then_inc(harm_in[u], 16)

                        def load_key(i, u):
                            sp.dma_start(key[:, u, :], key_table[edges(i, u)].rearrange("(p j) -> p j", j=TILES)).then_inc(key_in[u], 16)

                        def load_aq(i):
                            for k, table in enumerate((a_table, q_table)):
                                sp.dma_start(aq[:, k, :], table[bass.ds(i * QUAD, QUAD)].rearrange("(s c) -> s c", s=SEGS)).then_inc(aq_in, 16)

                        for u in range(SLOTS):
                            load_src(0, u)
                        load_aq(0)
                        for u in range(SLOTS):
                            load_harm(0, u)
                        for b, n in group_blocks():
                            sp.wait_ge(key_step, 3 + 2 * (b + 1))
                            sp.dma_start(key_table[b * P * GROUP:(b * P + n) * GROUP].rearrange("(g e) -> g e", e=GROUP),
                                         key_all[0:n, b, :]).then_inc(key_out, 16)
                        sp.wait_ge(key_out, 16 * GB)
                        for u in range(SLOTS):
                            load_key(0, u)
                        sp.wait_ge(rbf_spread, 1)
                        load_aq(1)
                        with sp.Fori(0, ITERS) as i:
                            for u in range(SLOTS):
                                sp.wait_ge(gathered[u], 16 * TILES * (i + 1))
                                load_src(i + 1, u)
                                if u == 1:
                                    sp.wait_ge(rbf_spread, i + 2)
                                    load_aq(i + 2)
                                sp.wait_ge(msg_ready, i * SLOTS + u + 1)
                                load_key(i + 1, u)
                                load_harm(i + 1, u)
                        sp.wait_ge(aq_in, 32 * (ITERS + 2))
                        for u in range(SLOTS):
                            sp.wait_ge(src_in[u], 16 * (ITERS + 1))
                            sp.wait_ge(key_in[u], 16 * (ITERS + 1))
                            sp.wait_ge(harm_in[u], 16 * (ITERS + 1))

                    @block.gpsimd
                    def _(pool):
                        def gather(i, u, first=False):
                            pool.wait_ge(src_in[u], 16 * (i + 1))
                            if not first:
                                pool.wait_ge(w_s_ready, i * SLOTS + u - SLOTS + 1)
                            pool.nop(nofuse=True)
                            for j in range(TILES):
                                pool.indirect_dma_start(
                                    lin_g[:, u, j, :], None, lin_table,
                                    bass.IndirectOffsetOnAxis(ap=src_ix[:, u, j:j + 1], axis=0)).then_inc(gathered[u], 16)

                        for u in range(SLOTS):
                            gather(0, u, first=True)
                        with pool.Fori(1, ITERS) as i:
                            for u in range(SLOTS):
                                gather(i, u)
                        gather(ITERS, 0)

                    @block.tensor
                    def _(pe):
                        def spread_aq(i):
                            pe.wait_ge(aq_in, 32 * (i + 1))
                            at_least(pe, rbf_ready, i)
                            pe.matmul(ps_rbf[:, 0, 0:SEG], sel_freq[:], aq[:, 0, :], start=True, stop=True)
                            pe.matmul(ps_rbf[:, 1, 0:SEG], sel_one[:], aq[:, 1, :], start=True, stop=True).then_inc(rbf_spread, 1)

                        def layer1(i, k):
                            if k == 0:
                                pe.wait_ge(rbf_ready, i + 1)
                            at_least(pe, h1_ready, i * UNITS + k - 1)
                            for half in range(2):
                                mm = pe.matmul(ps_h1[:, k % 2, half * SEG:(half + 1) * SEG], w1[:, 2 * k + half, :], rbf[:],
                                               start=True, stop=True)
                            mm.then_inc(h1_done, 1)

                        def layer2(i, k):
                            pe.wait_ge(h1_ready, i * UNITS + k + 1)
                            at_least(pe, h2_ready, i * UNITS + k - 1)
                            pe.matmul(ps_h2[:, k % 2, 0:UNIT], w2[:], h1[:, k % 2, :], start=True, stop=True).then_inc(h2_done, 1)

                        def layer3(i, u):
                            units = 2 * (u // 2) + 2
                            pe.wait_ge(h2_ready, i * UNITS + units)
                            at_least(pe, w_read, i * SLOTS + u)
                            half = slice((u % 2) * HID, (u % 2) * HID + HID)
                            cols = h2[half, (u // 2) * GROUP:(u // 2 + 1) * GROUP].rearrange("p (c j) -> p j c", j=TILES)
                            for j in range(TILES):
                                mm = pe.matmul(ps_w[:, j * P:(j + 1) * P], cols[:, j, :], w3[half, :], start=True, stop=True)
                            mm.then_inc(w_ready, 1)

                        def segment_sum(i, u):
                            pe.wait_ge(msg_ready, i * SLOTS + u + 1)
                            pe.wait_ge(agg_ready, i * SLOTS + u + 1)
                            for j in range(TILES):
                                mm = pe.matmul(ps_agg[:, 0:COLS], onehot[:, u % 2, j, :], msg[:, u % 2, j, :],
                                               start=(j == 0), stop=(j == TILES - 1))
                            mm.then_inc(sums_ready, 1)

                        spread_aq(0)
                        layer1(0, 0)
                        layer1(0, 1)
                        layer2(0, 0)
                        layer1(0, 2)
                        layer2(0, 1)
                        layer1(0, 3)
                        layer2(0, 2)
                        layer2(0, 3)
                        layer3(0, 0)
                        with pe.Fori(0, ITERS) as i:
                            spread_aq(i + 1)
                            layer3(i, 1)
                            segment_sum(i, 0)
                            layer3(i, 2)
                            segment_sum(i, 1)
                            layer1(i + 1, 0)
                            layer1(i + 1, 1)
                            layer2(i + 1, 0)
                            layer3(i, 3)
                            segment_sum(i, 2)
                            layer2(i + 1, 1)
                            layer1(i + 1, 2)
                            layer1(i + 1, 3)
                            layer3(i + 1, 0)
                            segment_sum(i, 3)
                            layer2(i + 1, 2)
                            layer2(i + 1, 3)
                        segment_sum(ITERS, 0)

                    @block.scalar
                    def _(act):
                        def sines(i):
                            act.wait_ge(frac_ready, i + 1)
                            act.activation(sine[:], frac[:], ACT.Sin, scale=-TURN).then_inc(sine_ready, 1)

                        def silu1(i, k):
                            act.wait_ge(h1_done, i * UNITS + k + 1)
                            at_least(act, h2_done, i * UNITS + k - 1)
                            act.activation(h1[:, k % 2, :], ps_h1[:, k % 2, 0:UNIT], ACT.Silu,
                                           scale=float(RBF ** -0.5)).then_inc(h1_ready, 1)

                        def silu2(i, k):
                            act.wait_ge(h2_done, i * UNITS + k + 1)
                            at_least(act, w_ready, i * SLOTS - SLOTS + 2 * (k // 2) + 2)
                            act.activation(h2[:, k * UNIT:(k + 1) * UNIT], ps_h2[:, k % 2, 0:UNIT], ACT.Silu,
                                           scale=float(HID ** -0.5)).then_inc(h2_ready, 1)

                        def scale_lin(i, u):
                            n = i * SLOTS + u
                            act.wait_ge(gathered[u], 16 * TILES * (i + 1))
                            act.wait_ge(harm_in[u], 16 * (i + 1))
                            at_least(act, w_s_ready, n - 1)
                            for j in range(TILES):
                                last = act.activation(lin_sh0[:, u % 2, j, :], lin_g[:, u, j, :], ACT.Copy, scale=harm[:, u, j, 0:1])
                            last.then_inc(lin_sh0_ready, 1)

                        sines(0)
                        silu1(0, 0)
                        silu1(0, 1)
                        silu2(0, 0)
                        silu1(0, 2)
                        silu2(0, 1)
                        silu1(0, 3)
                        silu2(0, 2)
                        silu2(0, 3)
                        for u in range(3):
                            scale_lin(0, u)

                        def body(i, last=False):
                            sines(i + 1)
                            scale_lin(i, 3)
                            silu1(i + 1, 0)
                            silu1(i + 1, 1)
                            silu2(i + 1, 0)
                            scale_lin(i + 1, 0)
                            silu2(i + 1, 1)
                            silu1(i + 1, 2)
                            silu1(i + 1, 3)
                            if not last:
                                scale_lin(i + 1, 1)
                            silu2(i + 1, 2)
                            silu2(i + 1, 3)
                            if not last:
                                scale_lin(i + 1, 2)

                        with act.Fori(0, ITERS - 1) as i:
                            body(i)
                        body(ITERS - 1, last=True)

                    @block.vector
                    def _(dve):
                        dve.tensor_scalar(win_lo[:], win_lo[:], float(P), None, ALU.add).then_inc(key_step, 1)
                        dve.tensor_scalar(blk_f[:], blk_f[:], 1.0, None, ALU.add).then_inc(key_step, 1)
                        dve.wait_ge(key_step, 2)
                        dve.tensor_scalar(win_hi[:], win_lo[:], float(P), None, ALU.add).then_inc(key_step, 1)
                        dve.tensor_scalar(blk_i[:], blk_f[:], float(NBLK - 1), None, ALU.min).then_inc(blk_ready, 1)
                        dve.memset(msg[:, :, :, MSG:COLS], 1.0).then_inc(agg_ready, 1)
                        dve.wait_ge(key_step, 3)
                        for b, n in group_blocks():
                            dve.scalar_tensor_tensor(out=key_all[0:n, b, :], in0=dst_f[0:n, b, :], scalar=win_hi[0:n, b:b + 1],
                                                     in1=row1[0:n, b, :], op0=ALU.is_lt, op1=ALU.mult).then_inc(key_step, 1)
                            dve.wait_ge(key_step, 4 + 2 * b)
                            dve.scalar_tensor_tensor(out=key_all[0:n, b, :], in0=dst_f[0:n, b, :], scalar=win_lo[0:n, b:b + 1],
                                                     in1=key_all[0:n, b, :], op0=ALU.is_ge, op1=ALU.mult).then_inc(key_step, 1)

                        def fractions(i):
                            dve.wait_ge(rbf_spread, i + 1)
                            dve.tensor_scalar(k_turn[:], ps_rbf[:, 0, 0:SEG], ROUND, None, ALU.add).then_inc(k_ready, 1)
                            dve.wait_ge(k_ready, i + 1)
                            dve.scalar_tensor_tensor(out=frac[:], in0=k_turn[:], scalar=ROUND, in1=ps_rbf[:, 0, 0:SEG],
                                                     op0=ALU.subtract, op1=ALU.subtract).then_inc(frac_ready, 1)

                        def basis(i):
                            dve.wait_ge(sine_ready, i + 1)
                            at_least(dve, h1_done, i * UNITS)
                            dve.tensor_tensor(rbf[:], sine[:], ps_rbf[:, 1, 0:SEG], ALU.mult).then_inc(rbf_ready, 1)

                        def products(i, u):
                            dve.wait_ge(gathered[u], 16 * TILES * (i + 1))
                            dve.wait_ge(harm_in[u], 16 * (i + 1))
                            dve.tensor_tensor(lin_sh[:], lin_v(u), sh_vec(u), ALU.mult).then_inc(lin_sh_ready, 1)

                        def columns(i, u):
                            n = i * SLOTS + u
                            dve.wait_ge(key_in[u], 16 * (i + 1))
                            dve.tensor_tensor(onehot[:, u % 2], iota1[:].unsqueeze(1).to_broadcast([P, TILES, P]),
                                              key[:, u, :].unsqueeze(2).to_broadcast([P, TILES, P]), ALU.is_equal).then_inc(onehot_ready, 1)
                            dve.wait_ge(lin_sh_ready, n + 1)
                            dve.tensor_tensor(dot2[:], lin_sh[:, :, 0, :], lin_sh[:, :, 1, :], ALU.add).then_inc(dot2_ready, 1)
                            dve.wait_ge(dot2_ready, n + 1)
                            dve.tensor_tensor(dot[:], dot2[:], lin_sh[:, :, 2, :], ALU.add).then_inc(dot_ready, 1)

                        def late(i, u):
                            n = i * SLOTS + u
                            o00, o11, o01, o10 = message(u)
                            scaled = lin_sh0[:, u % 2]
                            dve.wait_ge(w_ready, n + 1)
                            dve.wait_ge(lin_sh0_ready, n + 1)
                            dve.tensor_tensor(o10, scaled[:, :, MUL:].rearrange("p t (m c) -> p t m c", m=3), spread_m(w_part(2)),
                                              ALU.mult).then_inc(o10_ready, 1)
                            dve.tensor_tensor(o00, scaled[:, :, 0:MUL], w_part(0), ALU.mult).then_inc(o00_ready, 1)
                            dve.tensor_tensor(w_s[:], w_part(1), lin_s(u), ALU.mult).then_inc(w_s_ready, 1)
                            dve.wait_ge(dot_ready, n + 1)
                            dve.scalar_tensor_tensor(out=o11, in0=dot[:], scalar=float(3 ** -0.5), in1=w_part(3),
                                                     op0=ALU.mult, op1=ALU.mult).then_inc(w_read, 1)
                            dve.wait_ge(w_s_ready, n + 1)
                            dve.tensor_tensor(o01, spread_m(w_s[:]), sh_vec(u), ALU.mult).then_inc(msg_ready, 1)

                        def accumulate(i, u):
                            n = i * SLOTS + u
                            g = i * SLOTS + OFFSET[u] // GROUP
                            blk = dve.value_load(blk_i[0:1, bass.ds(g, 1)], min_val=0, max_val=NBLK - 1)
                            dve.wait_ge(sums_ready, n + 1)
                            dve.wait_ge(agg_ready, n + 1)
                            for k, (part, added) in enumerate(((at_lo, lo_added), (at_hi, agg_ready))):
                                rows = agg[:, bass.ds(blk * COLS + k * COLS, COLS)]
                                dve.scalar_tensor_tensor(out=rows, in0=ps_agg[:, 0:COLS], scalar=part[:, bass.ds(g, 1)],
                                                         in1=rows, op0=ALU.mult, op1=ALU.add).then_inc(added, 1)

                        fractions(0)
                        basis(0)
                        dve.wait_ge(blk_ready, 1)
                        products(0, 0)
                        columns(0, 0)
                        late(0, 0)
                        products(0, 1)
                        columns(0, 1)

                        def body(i, last=False):
                            for u in range(SLOTS):
                                late(i + (u + 1) // SLOTS, (u + 1) % SLOTS)
                                if u == 0:
                                    fractions(i + 1)
                                ahead = None if last and u == SLOTS - 1 else (i + (u + 2) // SLOTS, (u + 2) % SLOTS)
                                if ahead:
                                    products(*ahead)
                                accumulate(i, u)
                                if ahead:
                                    columns(*ahead)
                                if u == 0:
                                    basis(i + 1)

                        with dve.Fori(0, ITERS - 1) as i:
                            body(i)
                        body(ITERS - 1, last=True)
                        accumulate(ITERS, 0)

                for s in sems:
                    nc.sync.sem_clear(s)
                nc.all_engine_barrier()

        with ExitStack() as st:
            def s3(name, shape, dt=F32):
                return sb(name, shape, dt, st)

            def sem(name):
                return st.enter_context(nc.semaphore(name))

            x3 = s3("x3", [P, 2, NB, DIM])
            sc3 = s3("sc3", [P, 2, NB, DIM])
            count = s3("count", [P, NBLK])
            inv = s3("inv", [P, NBLK])
            scale = s3("scale", [P, NBLK])
            sums = s3("sums", [P, 2, NB, MSG])
            aggT = s3("aggT", [P, 2, 2, NB * P])
            pre = s3("pre", [P, 2, NB])
            alpha = s3("alpha", [P, 2, NB])
            gain = s3("gain", [P, 2, NB])
            layer = s3("layer", [P, 2, NB, DIM])
            new = s3("new", [P, 2, NB, DIM])
            ps_aT = st.enter_context(nc.psum_tensor("ps_aT", [P, 2, 2, NB * P], F32))
            ps_l2 = st.enter_context(nc.psum_tensor("ps_l2", [P, 2, NB, 256], F32))

            in3 = [sem(f"in3_{b}") for b in range(2)]
            out3 = [sem(f"out3_{b}") for b in range(2)]
            count_ready, inv_ready, scale_ready, aT_done = sem("count_ready"), sem("inv_ready"), sem("scale_ready"), sem("aT_done")
            aT_lo, aT_hi, l2_done, pre_ready = sem("aT_lo"), sem("aT_hi"), sem("l2_done"), sem("pre_ready")
            alpha_ready, gain_ready, layer_ready, new_ready, sums_copied = (
                sem("alpha_ready"), sem("gain_ready"), sem("layer_ready"), sem("new_ready"), sem("sums_copied"))

            PRE = 2
            LOOPS = (STEPS - 3 - PRE) // 2
            AFTER = PRE + 2 * LOOPS

            def blocks_of(n):
                return REST if isinstance(n, int) and n == STEPS else NB

            def agg_step(n):
                k = blocks_of(n)
                return agg[:, bass.ds(n * (NB * COLS), k * COLS)].rearrange("p (b c) -> p b c", c=COLS)

            def steps(eng, body):
                for n in range(PRE):
                    body(n, n % 2)
                with eng.Fori(0, LOOPS) as t:
                    for j in range(2):
                        body(t * 2 + (PRE + j), (PRE + j) % 2)
                for n in range(AFTER, STEPS + 1):
                    body(n, n % 2)

            def loads(n, b):
                if not isinstance(n, int):
                    return (n - b) * 16 + 32
                return n // 2 * 32 + (32 if n < STEPS else 32 * REST)

            def within(n):
                return not isinstance(n, int) or 0 <= n <= STEPS

            with nc.Block() as block:
                @block.sync
                def _(sp):
                    def load(n, b):
                        if blocks_of(n) == NB:
                            sp.dma_start(x3[:, b], node_rows(x, n)).then_inc(in3[b], 16)
                            sp.dma_start(sc3[:, b], node_rows(sc_table, n)).then_inc(in3[b], 16)
                        else:
                            for r in range(REST):
                                sp.dma_start(x3[0:REST_ROWS[r], b, r], rest_rows(x, r)).then_inc(in3[b], 16)
                                sp.dma_start(sc3[0:REST_ROWS[r], b, r], rest_rows(sc_table, r)).then_inc(in3[b], 16)

                    def body(n, b):
                        sp.wait_ge(new_ready, n + 1)
                        if blocks_of(n) == NB:
                            sp.dma_start(node_rows(out, n), new[:, b]).then_inc(out3[b], 16)
                        else:
                            for r in range(REST):
                                sp.dma_start(rest_rows(out, r), new[0:REST_ROWS[r], b, r]).then_inc(out3[b], 16)
                        if within(n + 2):
                            load(n + 2, b)

                    load(0, 0)
                    load(1, 1)
                    steps(sp, body)
                    for b in range(2):
                        whole = len(range(b, STEPS, 2))
                        sp.wait_ge(out3[b], 16 * (whole + (REST if b == STEPS % 2 else 0)))

                @block.vector
                def _(dve):
                    def update(n, b):
                        if not within(n):
                            return
                        k = blocks_of(n)
                        dve.wait_ge(alpha_ready, n + 1)
                        dve.tensor_tensor(gain[:, b, 0:k], alpha[:, b, 0:k], scale[:, bass.ds(n * NB, k)], ALU.mult).then_inc(gain_ready, 1)
                        dve.wait_ge(in3[b], loads(n, b))
                        at_least(dve, new_ready, n - 1)
                        dve.wait_ge(gain_ready, n + 1)
                        for j in range(k):
                            last = dve.scalar_tensor_tensor(out=layer[:, b, j, :], in0=ps_l2[:, b, j, 0:DIM], scalar=gain[:, b, j:j + 1],
                                                            in1=sc3[:, b, j, :], op0=ALU.mult, op1=ALU.add)
                        last.then_inc(layer_ready, 1)

                    def copy_low(n, b):
                        if not within(n):
                            return
                        k = blocks_of(n)
                        dve.wait_ge(aT_done, n + 1)
                        at_least(dve, l2_done, n - 1)
                        dve.tensor_copy(aggT[:, b, 0, 0:k * P], ps_aT[:, b, 0, 0:k * P]).then_inc(aT_lo, 1)

                    def body(n, b):
                        k = blocks_of(n)
                        copy_low(n + 1, 1 - b)
                        update(n - 1, 1 - b)
                        dve.wait_ge(l2_done, n + 1)
                        at_least(dve, alpha_ready, n - 1)
                        dve.tensor_tensor(pre[:, b, 0:k], ps_l2[:, b, 0:k, DIM], scale[:, bass.ds(n * NB, k)], ALU.mult).then_inc(pre_ready, 1)

                    counts = agg[:, 0:NBLK * COLS].rearrange("p (b c) -> p b c", c=COLS)[:, :, MSG]
                    dve.tensor_scalar(count[:], counts, 1.0, None, ALU.max).then_inc(count_ready, 1)
                    dve.wait_ge(count_ready, 1)
                    dve.reciprocal(inv[:], count[:]).then_inc(inv_ready, 1)
                    dve.wait_ge(inv_ready, 1)
                    dve.tensor_tensor(scale[:], inv[:], attr_lin2[:], ALU.mult).then_inc(scale_ready, 1)
                    dve.wait_ge(scale_ready, 1)
                    copy_low(0, 0)
                    steps(dve, body)
                    update(STEPS, STEPS % 2)

                @block.scalar
                def _(act):
                    def copy_sums(n, b):
                        if not within(n):
                            return
                        k = blocks_of(n)
                        at_least(act, aT_done, n - 1)
                        act.activation(sums[:, b, 0:k, :], agg_step(n)[:, :, 0:MSG], ACT.Copy).then_inc(sums_copied, 1)

                    def copy_high(n, b):
                        if not within(n):
                            return
                        k = blocks_of(n)
                        act.wait_ge(aT_done, n + 1)
                        at_least(act, l2_done, n - 1)
                        act.activation(aggT[:, b, 1, 0:k * P], ps_aT[:, b, 1, 0:k * P], ACT.Copy).then_inc(aT_hi, 1)

                    def body(n, b):
                        k = blocks_of(n)
                        copy_high(n + 1, 1 - b)
                        copy_sums(n + 3, 1 - b)
                        act.wait_ge(pre_ready, n + 1)
                        at_least(act, gain_ready, n - 1)
                        act.activation(alpha[:, b, 0:k], pre[:, b, 0:k], ACT.Tanh).then_inc(alpha_ready, 1)

                    copy_sums(0, 0)
                    copy_sums(1, 1)
                    copy_high(0, 0)
                    copy_sums(2, 0)
                    steps(act, body)

                @block.tensor
                def _(pe):
                    def turn(n, b):
                        if not within(n):
                            return
                        pe.wait_ge(sums_copied, n + 1)
                        at_least(pe, aT_lo, n - 1)
                        at_least(pe, aT_hi, n - 1)
                        for j in range(blocks_of(n)):
                            for c in range(2):
                                last = pe.transpose(ps_aT[:, b, c, j * P:(j + 1) * P], sums[:, b, j, c * P:(c + 1) * P], ident[:])
                        last.then_inc(aT_done, 1)

                    def body(n, b):
                        pe.wait_ge(aT_lo, n + 1)
                        pe.wait_ge(aT_hi, n + 1)
                        at_least(pe, layer_ready, n - 1)
                        for j in range(blocks_of(n)):
                            cols = slice(j * P, (j + 1) * P)
                            for c in range(2):
                                last = pe.matmul(ps_l2[:, b, j, 0:DIM + 1], aggT[:, b, c, cols], w_lin2[:, c, :], start=(c == 0), stop=(c == 1))
                        last.then_inc(l2_done, 1)
                        turn(n + 2, b)

                    turn(0, 0)
                    turn(1, 1)
                    steps(pe, body)

                @block.gpsimd
                def _(pool):
                    def body(n, b):
                        k = blocks_of(n)
                        pool.wait_ge(layer_ready, n + 1)
                        at_least(pool, out3[b], n // 2 * 16 if isinstance(n, int) else (n - b) * 8)
                        pool.tensor_tensor(new[:, b, 0:k], layer[:, b, 0:k], x3[:, b, 0:k], ALU.add).then_inc(new_ready, 1)

                    steps(pool, body)

def kernel(x, src, dst, edge_attr_4, edge_weight, node_vec1, L0_gnn_sc_ws, L0_gnn_sc_wv, L0_gnn_lin1_ws, L0_gnn_lin1_wv,
           L0_gnn_fc_w1, L0_gnn_fc_w2, L0_gnn_fc_w3, L0_gnn_lin2_ws, L0_gnn_lin2_wv, L0_gnn_alpha_w):
    import concourse.bacc as bacc
    from concourse.bass_utils import run_bass_kernel_spmd

    def padded(a, n, fill):
        a = np.ascontiguousarray(a)
        return np.concatenate([a, np.full((n - a.shape[0],) + a.shape[1:], fill, a.dtype)])

    inputs = {
        "x": x, "src": padded(src, EDGES_PAD, 0), "dst": padded(dst, EDGES_PAD, NO_NODE),
        "edge_attr_4": padded(edge_attr_4, EDGES_PAD, 0), "edge_weight": padded(edge_weight, EDGES_PAD, 0),
        "node_vec1": node_vec1, "sc_ws": L0_gnn_sc_ws, "sc_wv": L0_gnn_sc_wv, "lin1_ws": L0_gnn_lin1_ws, "lin1_wv": L0_gnn_lin1_wv,
        "fc_w1": L0_gnn_fc_w1, "fc_w2": L0_gnn_fc_w2, "fc_w3": L0_gnn_fc_w3,
        "lin2_ws": L0_gnn_lin2_ws, "lin2_wv": L0_gnn_lin2_wv, "alpha_w": L0_gnn_alpha_w,
    }
    nc = bacc.Bacc("TRN2", target_bir_lowering=False, num_devices=1)
    arrays, args = {}, []
    for name, a in inputs.items():
        arrays[f"in_{name}"] = np.ascontiguousarray(a)
        args.append(nc.dram_tensor(f"in_{name}", arrays[f"in_{name}"].shape, mybir.dt.from_np(arrays[f"in_{name}"].dtype),
                                   kind="ExternalInput").ap())
    args.append(nc.dram_tensor("out_dram", (NODES, DIM), F32, kind="ExternalOutput").ap())
    gnn_kernel(nc, *args)
    return run_bass_kernel_spmd(nc, [arrays], core_ids=[0]).results[0]["out_dram"]
```

```python
from contextlib import ExitStack

import numpy as np

import concourse.bass as bass
from concourse import mybir

F32 = mybir.dt.float32
I32 = mybir.dt.int32
ALU = mybir.AluOpType
ACT = mybir.ActivationFunctionType
AX_X = mybir.AxisListType.X

P = 128
NODES, DIM = 12500, 128
EDGES = 200000
MUL, RBF, HID = 32, 8, 64
CUTOFF = 6.0
EPS = 1e-5

TILES = 6
GROUP = TILES * P
SLOTS = 4
QUAD = SLOTS * GROUP
ITERS = EDGES // QUAD
assert EDGES - ITERS * QUAD <= GROUP
HALF = QUAD // 2
SEGS = 16
SEG = QUAD // SEGS
UNIT = 2 * SEG
UNITS = HALF // UNIT
EDGES_PAD = (ITERS + 2) * QUAD
DCOLS = EDGES_PAD // P
GROUPS = (ITERS + 1) * SLOTS
OFFSET = [(u % 2) * HALF + (u // 2) * GROUP for u in range(SLOTS)]
NO_NODE = 1 << 20

NBLK = -(-NODES // P)
NB = 4
STEPS = NBLK // NB
REST = NBLK - STEPS * NB
REST_ROWS = [min(P, NODES - (STEPS * NB + j) * P) for j in range(REST)]
MSG = 8 * MUL
COLS = MSG + 1
TINY = 2e-5
FAR = 65536.0
ROUND = 1.5 * 2 ** 23
TURN = float(np.nextafter(np.float32(2 * np.pi), np.float32(0)))


def at_least(eng, sem, value):
    if not isinstance(value, int) or value > 0:
        eng.wait_ge(sem, value)


def gnn_kernel(nc, x, src, dst, sh, dist, node_vec, sc_ws, sc_wv, lin1_ws, lin1_wv,
               fc_w1, fc_w2, fc_w3, lin2_ws, lin2_wv, alpha_w, out):
    lin_table = nc.dram_tensor("lin_table", [NODES, DIM], F32, kind="Internal").ap()
    sc_table = nc.dram_tensor("sc_table", [NODES, DIM], F32, kind="Internal").ap()
    a_table = nc.dram_tensor("a_table", [EDGES_PAD], F32, kind="Internal").ap()
    q_table = nc.dram_tensor("q_table", [EDGES_PAD], F32, kind="Internal").ap()
    key_table = nc.dram_tensor("key_table", [GROUPS * GROUP], F32, kind="Internal").ap()

    def node_rows(table, step):
        return table[bass.ds(step * (NB * P), NB * P), :].rearrange("(b p) d -> p b d", p=P)

    def rest_rows(table, j):
        lo = (STEPS * NB + j) * P
        return table[lo:lo + REST_ROWS[j], :]

    def group_blocks():
        return [(b, min(P, GROUPS - b * P)) for b in range(-(-GROUPS // P))]

    GB = len(group_blocks())

    def padded(b):
        return (b * P + group_blocks()[b][1]) * GROUP > EDGES

    def window_steps(b):
        return sum(7 if padded(k) else 6 for k in range(b))

    def edges(i, u):
        return bass.ds(i * QUAD + OFFSET[u], GROUP)


    with ExitStack() as top:
        def sb(name, shape, dt=F32, ctx=top):
            return ctx.enter_context(nc.sbuf_tensor(name, shape, dt))

        agg = sb("agg", [P, (NBLK + 1) * COLS])
        ident = sb("ident", [P, P])
        iota1 = sb("iota1", [P, P])
        sel_freq = sb("sel_freq", [SEGS, P])
        sel_one = sb("sel_one", [SEGS, P])
        w1 = sb("w1", [P, SEGS // 2, P])
        w2 = sb("w2", [P, P])
        w3 = sb("w3", [P, P])
        w_lin2 = sb("w_lin2", [P, 2, DIM + 1])
        attr_lin = sb("attr_lin", [P, NBLK])
        attr_lin2 = sb("attr_lin2", [P, NBLK])
        dst_f = sb("dst_f", [P, GB, GROUP])
        row1 = sb("row1", [P, GB, GROUP])
        win_lo = sb("win_lo", [P, GB])
        win_hi = sb("win_hi", [P, GB])
        at_lo = sb("at_lo", [P, GROUPS])
        at_hi = sb("at_hi", [P, GROUPS])
        blk_f = sb("blk_f", [1, GROUPS])
        blk_i = sb("blk_i", [1, GROUPS], I32)
        passes_i = sb("passes_i", [1, 1], I32)
        src_ix = sb("src_ix", [P, SLOTS, TILES], I32)

        with ExitStack() as st:
            def s1(name, shape, dt=F32):
                return sb(name, shape, dt, st)

            def sem(name):
                return st.enter_context(nc.semaphore(name))

            XB, OB = 6, 3
            xq = s1("xq", [P, XB, NB, DIM])
            bn = s1("bn", [P, XB, NB, 6])
            mean_var = s1("mean_var", [P, XB, NB, 2])
            zero = s1("zero", [P, 1])
            eps = s1("eps", [P, 1])
            std = s1("std", [P, XB, NB])
            rstd = s1("rstd", [P, XB, NB])
            shift = s1("shift", [P, XB, NB])
            h = s1("h", [P, 2, NB, DIM])
            hT = s1("hT", [P, 2, NB * P])
            node_out = s1("node_out", [P, OB, NB, 2 * DIM])
            w_nodes = s1("w_nodes", [P, 2 * DIM])
            w_sc = s1("w_sc", [P, DIM])
            wv_in = s1("wv_in", [P, MUL])
            iota_i = s1("iota_i", [P, P], I32)
            freq_i = s1("freq_i", [SEGS, P], I32)
            freq = s1("freq", [SEGS, P])
            part_i = s1("part_i", [P, 1], I32)
            part_f = s1("part_f", [P, 1])
            rowf_i = s1("rowf_i", [P, 1], I32)
            rowf = s1("rowf", [P, 1])
            row_scale = s1("row_scale", [P, 1])
            ones = s1("ones", [P, P])
            attr_raw = s1("attr_raw", [NBLK, P])
            dst_i = s1("dst_i", [P, GB, GROUP], I32)
            least = s1("least", [P, GB])
            most = s1("most", [P, GB])
            span = s1("span", [P, GB])
            widest = s1("widest", [P, 1])
            base_diag = s1("base_diag", [P, GB, P])
            base_i = s1("base_i", [P, GROUPS], I32)
            off_i = s1("off_i", [P, GROUPS], I32)
            blk0_i = s1("blk0_i", [1, GROUPS], I32)
            span_max = s1("span_max", [1, 1])
            span_i = s1("span_i", [1, 1], I32)
            more_i = s1("more_i", [1, 1], I32)
            d_in = s1("d_in", [P, DCOLS])
            d_abs = s1("d_abs", [P, DCOLS])
            a_all = s1("a_all", [P, DCOLS])
            turns = s1("turns", [P, DCOLS])
            psT = st.enter_context(nc.psum_tensor("psT", [P, 2, NB * P], F32))
            psN = st.enter_context(nc.psum_tensor("psN", [P, 2, NB, 2 * DIM], F32))
            psW = st.enter_context(nc.psum_tensor("psW", [P, 512], F32))
            psA = st.enter_context(nc.psum_tensor("psA", [P, 512], F32))

            x_in = [sem(f"x_in{b}") for b in range(XB)]
            stored = [sem(f"stored{b}") for b in range(OB)]
            dst_in = [sem(f"dst_in{b}") for b in range(GB)]
            dist_in, attr_in = sem("dist_in"), sem("attr_in")
            w_nodes_in, w_edges_in, a_out, q_out, wv_landed, first_src = sem("w_nodes_in"), sem("w_edges_in"), sem("a_out"), sem("q_out"), sem("wv_landed"), sem("first_src")
            zeroed, shaped, iotas, ones_set = sem("zeroed"), sem("shaped"), sem("iotas"), sem("ones_set")
            bn_done, aggr_done, std_ready = sem("bn_done"), sem("aggr_done"), sem("std_ready")
            rstd_ready, shift_ready, h_ready, recip_ready = sem("rstd_ready"), sem("shift_ready"), sem("h_ready"), sem("recip_ready")
            transposed, hT_ready, nodes_done, evacuated = sem("transposed"), sem("hT_ready"), sem("nodes_done"), sem("evacuated")
            attr_turned, attr_ready = sem("attr_turned"), sem("attr_ready")
            const_step, win_step, spread, span_row = sem("const_step"), sem("win_step"), sem("spread"), sem("span_row")
            abs_ready, dist_step, cos_ready = sem("abs_ready"), sem("dist_step"), sem("cos_ready")
            agg_zero, diag_ready, w_sc_in, w_sc_done, zero_set, dst_real = (
                sem("agg_zero"), sem("diag_ready"), sem("w_sc_in"), sem("w_sc_done"), sem("zero_set"), sem("dst_real"))

            UNROLL = XB
            AGG = (NBLK + 1) * COLS
            LOOPS = (STEPS - UNROLL) // UNROLL
            PEELED = LOOPS * UNROLL
            CLEAR = AGG // 30
            ZERO_ACT, ZERO_FIRST, ZERO_SECOND = AGG // 16, AGG * 5 // 16, AGG - 2 * UNROLL * CLEAR
            RECIP = DCOLS // (PEELED - UNROLL)
            assert RECIP * (PEELED - UNROLL) == DCOLS

            with nc.Block() as block:
                @block.sync
                def _(sp):
                    def load_x(t, j):
                        t, b = t + j // XB, j % XB
                        sp.dma_start(xq[:, b], node_rows(x, t * XB + b)).then_inc(x_in[b], 16)

                    def load_rest():
                        b = STEPS % XB
                        for r in range(REST):
                            sp.dma_start(xq[0:REST_ROWS[r], b, r], rest_rows(x, r)).then_inc(x_in[b], 16)

                    def store(t, j):
                        n, b = t * UNROLL + j, j % OB
                        sp.wait_ge(evacuated, n + 1)
                        sp.dma_start(node_rows(lin_table, n), node_out[:, b, :, 0:DIM]).then_inc(stored[b], 16)
                        sp.dma_start(node_rows(sc_table, n), node_out[:, b, :, DIM:]).then_inc(stored[b], 16)

                    sp.dma_start(d_in[:], dist.rearrange("(p c) -> p c", p=P)).then_inc(dist_in, 16)
                    for b, n in group_blocks():
                        sp.dma_start(dst_i[0:n, b, :], dst[b * P * GROUP:(b * P + n) * GROUP].rearrange("(g e) -> g e", e=GROUP)).then_inc(dst_in[b], 16)
                    sp.wait_ge(zeroed, 1)
                    sp.dma_start(attr_raw[0:NBLK - 1, :], node_vec[0:(NBLK - 1) * P, :].rearrange("(b p) o -> b (p o)", p=P)).then_inc(attr_in, 16)
                    sp.dma_start(attr_raw[NBLK - 1:NBLK, 0:NODES - (NBLK - 1) * P],
                                 node_vec[(NBLK - 1) * P:, :].rearrange("(b p) o -> b (p o)", b=1)).then_inc(attr_in, 16)
                    for j in range(XB):
                        load_x(0, j)
                    sp.wait_ge(zeroed, 3)
                    for w, ws, wv, landed in ((w_nodes, lin1_ws, lin1_wv, w_nodes_in), (w_sc, sc_ws, sc_wv, w_sc_in)):
                        sp.dma_start(w[0:MUL, 0:MUL], ws).then_inc(landed, 16)
                        for m in range(3):
                            lo = (m + 1) * MUL
                            sp.dma_start(w[MUL + m:DIM:3, lo:lo + MUL], wv).then_inc(landed, 16)
                    for half in range(2):
                        rows = slice(half * HID, (half + 1) * HID)
                        sp.dma_start(wv_in[rows, :], lin2_wv).then_inc(wv_landed, 16)
                    sp.wait_ge(dist_step, 1)
                    sp.dma_start(a_table.rearrange("(p c) -> p c", p=P), a_all[:]).then_inc(a_out, 16)
                    sp.wait_ge(zeroed, 7)
                    for s in range(SEGS):
                        half, q = s // (SEGS // 2), s % (SEGS // 2)
                        sp.dma_start(w1[s * RBF:(s + 1) * RBF, q, half * HID:(half + 1) * HID], fc_w1).then_inc(w_edges_in, 16)
                    for half in range(2):
                        rows = slice(half * HID, (half + 1) * HID)
                        sp.dma_start(w2[rows, rows], fc_w2).then_inc(w_edges_in, 16)
                        sp.dma_start(w3[rows, :], fc_w3).then_inc(w_edges_in, 16)
                    sp.dma_start(w_lin2[0:HID, 0, 0:MUL], lin2_ws).then_inc(w_edges_in, 16)
                    sp.dma_start(w_lin2[0:HID, 0, DIM:], alpha_w).then_inc(w_edges_in, 16)
                    for u in range(SLOTS):
                        sp.dma_start(src_ix[:, u, :], src[edges(0, u)].rearrange("(p j) -> p j", j=TILES)).then_inc(first_src, 16)
                    def refill(t, j):
                        sp.wait_ge(h_ready, t * UNROLL + j + 1)
                        load_x(t, j + XB)

                    refill(0, 0)
                    refill(0, 1)
                    with sp.Fori(0, LOOPS - 1) as t:
                        for j in range(UNROLL):
                            store(t, j)
                            refill(t, j + 2)
                    for k in range(PEELED - UNROLL, STEPS):
                        store(k // UNROLL, k % UNROLL)
                        if k == PEELED + 1:
                            sp.wait_ge(dist_step, 7)
                            sp.dma_start(q_table.rearrange("(p c) -> p c", p=P), turns[:]).then_inc(q_out, 16)
                        if k + 2 + XB < STEPS:
                            refill(0, k + 2)
                        if k + 2 + XB == STEPS:
                            sp.wait_ge(h_ready, k + 3)
                            load_rest()
                    b = STEPS % OB
                    sp.wait_ge(evacuated, STEPS + 1)
                    for r in range(REST):
                        sp.dma_start(rest_rows(lin_table, r), node_out[0:REST_ROWS[r], b, r, 0:DIM]).then_inc(stored[b], 16)
                    for r in range(REST):
                        sp.dma_start(rest_rows(sc_table, r), node_out[0:REST_ROWS[r], b, r, DIM:]).then_inc(stored[b], 16)
                    sp.wait_ge(first_src, 16 * SLOTS)
                    sp.wait_ge(a_out, 16)
                    sp.wait_ge(q_out, 16)
                    for b in range(OB):
                        steps = len(range(b, STEPS, OB))
                        sp.wait_ge(stored[b], 32 * steps + (32 * REST if b == STEPS % OB else 0))

                @block.gpsimd
                def _(pool):
                    pool.memset(attr_raw[:], 0.0).then_inc(zeroed, 1)
                    pool.memset(w_nodes[:], 0.0).then_inc(zeroed, 1)
                    pool.memset(w_sc[:], 0.0).then_inc(zeroed, 1)
                    pool.memset(ident[:], 0.0).then_inc(zeroed, 1)
                    pool.memset(w1[:], 0.0).then_inc(zeroed, 1)
                    pool.memset(w2[:], 0.0).then_inc(zeroed, 1)
                    pool.memset(w_lin2[:], 0.0).then_inc(zeroed, 1)
                    pool.memset(zero[:], 0.0).then_inc(zero_set, 1)
                    pool.memset(eps[:], EPS).then_inc(zero_set, 1)
                    pool.memset(ones[:], 1.0).then_inc(ones_set, 1)
                    pool.memset(sel_one[:], 1.0).then_inc(ones_set, 1)
                    pool.memset(least[:], 0.0).then_inc(ones_set, 1)
                    pool.memset(span[:], 0.0).then_inc(ones_set, 1)
                    pool.wait_ge(zeroed, 4)
                    pool.affine_select(out=ident[:], in_=ident[:], compare_op=ALU.not_equal, fill=1.0, base=0,
                                       pattern=[[-1, P]], channel_multiplier=1).then_inc(shaped, 1)
                    pool.iota(iota_i[:], pattern=[[1, P]], base=1, channel_multiplier=0).then_inc(iotas, 1)
                    pool.iota(part_i[:], pattern=[[0, 1]], base=0, channel_multiplier=1).then_inc(iotas, 1)
                    pool.iota(freq_i[:], pattern=[[0, SEGS], [1, RBF]], base=1, channel_multiplier=0).then_inc(iotas, 1)
                    pool.wait_ge(ones_set, 2)
                    pool.affine_select(out=sel_one[:], in_=sel_one[:], compare_op=ALU.is_ge, fill=0.0, base=0,
                                       pattern=[[1, P]], channel_multiplier=-RBF).then_inc(shaped, 1)
                    pool.wait_ge(shaped, 2)
                    pool.affine_select(out=sel_one[:], in_=sel_one[:], compare_op=ALU.is_ge, fill=0.0, base=RBF - 1,
                                       pattern=[[-1, P]], channel_multiplier=RBF).then_inc(shaped, 1)
                    pool.memset(agg[:, ZERO_ACT:ZERO_FIRST], 0.0).then_inc(agg_zero, 1)
                    pool.wait_ge(dist_step, 1)
                    pool.tensor_scalar(turns[:], a_all[:], 1.0 / (2 * CUTOFF), 0.25, ALU.mult, ALU.add).then_inc(dist_step, 1)
                    pool.wait_ge(dist_step, 2)
                    pool.tensor_scalar(d_abs[:], turns[:], 1.0, ROUND, ALU.mult, ALU.add).then_inc(dist_step, 1)
                    pool.memset(agg[:, ZERO_FIRST:ZERO_SECOND], 0.0).then_inc(agg_zero, 1)

                    def normalize(t, j, blocks=NB):
                        n, b = t * UNROLL + j, j % 2
                        pool.wait_ge(shift_ready, n + 1)
                        at_least(pool, transposed, n - 1)
                        pool.nop(nofuse=True)
                        for k in range(blocks):
                            last = pool.tensor_scalar(h[:, b, k, :], xq[:, j % XB, k, :], rstd[:, j % XB, k:k + 1], shift[:, j % XB, k:k + 1],
                                                      ALU.mult, ALU.add)
                        last.then_inc(h_ready, 1)

                    def clear(k):
                        lo = ZERO_SECOND + k * CLEAR
                        pool.memset(agg[:, lo:lo + CLEAR], 0.0).then_inc(agg_zero, 1)

                    for j in range(UNROLL):
                        normalize(0, j)
                        if j == 1:
                            pool.wait_ge(cos_ready, 1)
                            pool.tensor_scalar(turns[:], turns[:], 0.5, 0.5, ALU.mult, ALU.add).then_inc(dist_step, 1)
                        clear(j)
                    with pool.Fori(1, LOOPS) as t:
                        for j in range(UNROLL):
                            normalize(t, j)
                    for n in range(PEELED, STEPS + 1):
                        normalize(n // UNROLL, n % UNROLL, NB if n < STEPS else REST)
                        if n - PEELED < UNROLL:
                            clear(UNROLL + n - PEELED)

                @block.scalar
                def _(act):
                    def sqrt(t, j):
                        n, b = t * UNROLL + j, j % XB
                        act.wait_ge(aggr_done, n * NB + NB)
                        at_least(act, rstd_ready, n - XB + 1)
                        act.activation(std[:, b, :], mean_var[:, b, :, 1], ACT.Sqrt, bias=eps[:, 0:1]).then_inc(std_ready, 1)

                    def copy_hT(t, j, blocks=NB):
                        n, b = t * UNROLL + j, j % 2
                        act.wait_ge(transposed, n + 1)
                        at_least(act, nodes_done, n - 1)
                        act.activation(hT[:, b, 0:blocks * P], psT[:, b, 0:blocks * P], ACT.Relu).then_inc(hT_ready, 1)

                    def evacuate(t, j, blocks=NB):
                        n, b = t * UNROLL + j, j % OB
                        act.wait_ge(nodes_done, n + 1)
                        at_least(act, stored[b], 32 * (t * (UNROLL // OB) + j // OB))
                        for k in range(blocks):
                            blk = n * NB + k
                            last = act.activation(node_out[:, b, k, :], psN[:, j % 2, k, :], ACT.Copy,
                                                  scale=attr_lin[:, bass.ds(blk, 1)])
                        last.then_inc(evacuated, 1)

                    def step(t, j):
                        n = t * UNROLL + j
                        ahead = not isinstance(n, int)
                        if ahead or n + 3 <= STEPS:
                            sqrt(t, j + 3)
                        if ahead or n + 1 <= STEPS:
                            copy_hT(t, j + 1, NB if ahead or n + 1 < STEPS else REST)
                        evacuate(t, j, NB if ahead or n < STEPS else REST)

                    act.wait_ge(dist_in, 16)
                    act.activation(d_abs[:], d_in[:], ACT.Abs).then_inc(abs_ready, 1)
                    for b, n in group_blocks():
                        act.wait_ge(dst_in[b], 16)
                        act.activation(dst_f[0:n, b, :], dst_i[0:n, b, :], ACT.Copy).then_inc(dst_real, 1)
                    act.wait_ge(zero_set, 2)
                    act.activation(agg[:, 0:ZERO_ACT], zero[:].to_broadcast([P, ZERO_ACT]), ACT.Copy).then_inc(agg_zero, 1)
                    act.wait_ge(dist_step, 4)
                    act.activation(turns[:], turns[:], ACT.Sin, scale=-TURN).then_inc(cos_ready, 1)
                    for j in range(3):
                        sqrt(0, j)
                    copy_hT(0, 0)
                    act.wait_ge(attr_ready, 2)
                    for j in range(UNROLL):
                        step(0, j)
                    with act.Fori(1, LOOPS) as t:
                        for j in range(UNROLL):
                            step(t, j)
                    for n in range(PEELED, STEPS + 1):
                        step(n // UNROLL, n % UNROLL)

                @block.tensor
                def _(pe):
                    def turn(t, j, blocks=NB):
                        n, b = t * UNROLL + j, j % 2
                        pe.wait_ge(h_ready, n + 1)
                        at_least(pe, hT_ready, n - 1)
                        for k in range(blocks):
                            last = pe.transpose(psT[:, b, k * P:(k + 1) * P], h[:, b, k, :], ident[:])
                        last.then_inc(transposed, 1)

                    def product(t, j, blocks=NB):
                        n, b = t * UNROLL + j, j % 2
                        pe.wait_ge(hT_ready, n + 1)
                        at_least(pe, evacuated, n - 1)
                        for k in range(blocks):
                            last = pe.matmul(psN[:, b, k, :], hT[:, b, k * P:(k + 1) * P], w_nodes[:], start=True, stop=True)
                        last.then_inc(nodes_done, 1)

                    def spread_windows():
                        pe.wait_ge(ones_set, 1)
                        pe.wait_ge(diag_ready, GB)
                        for b, n in group_blocks():
                            last = pe.matmul(psW[:, b * P:b * P + n], ones[0:n, :], base_diag[0:n, b, 0:n], start=True, stop=True)
                        last.then_inc(spread, 1)
                        pe.wait_ge(win_step, window_steps(GB) + 1)
                        pe.wait_ge(attr_ready, 2)
                        pe.matmul(psA[0:1, 0:P], widest[:], ident[:], start=True, stop=True).then_inc(span_row, 1)

                    pe.wait_ge(shaped, 1)
                    pe.wait_ge(attr_in, 32)
                    pe.transpose(psA[:, 0:NBLK], attr_raw[:], ident[0:NBLK, 0:NBLK]).then_inc(attr_turned, 1)
                    turn(0, 0)
                    pe.wait_ge(w_nodes_in, 16 * 4)
                    pe.wait_ge(w_sc_done, 2)
                    for j in range(UNROLL):
                        turn(0, j + 1)
                        product(0, j)
                        if j == 2:
                            spread_windows()
                    with pe.Fori(1, LOOPS) as t:
                        for j in range(UNROLL):
                            turn(t, j + 1)
                            product(t, j)
                    for n in range(PEELED, STEPS + 1):
                        if n < STEPS:
                            turn(n // UNROLL, n % UNROLL + 1, NB if n + 1 < STEPS else REST)
                        product(n // UNROLL, n % UNROLL, NB if n < STEPS else REST)

                @block.vector
                def _(dve):
                    dve.wait_ge(iotas, 3)
                    dve.tensor_copy(iota1[:], iota_i[:]).then_inc(const_step, 1)
                    dve.tensor_copy(part_f[:], part_i[:]).then_inc(const_step, 1)
                    dve.tensor_copy(freq[:], freq_i[:]).then_inc(const_step, 1)
                    dve.tensor_scalar(rowf_i[:], part_i[:], RBF - 1, None, ALU.bitwise_and).then_inc(const_step, 1)
                    dve.wait_ge(const_step, 4)
                    dve.tensor_scalar(rowf[:], rowf_i[:], 1.0, None, ALU.add).then_inc(const_step, 1)
                    dve.wait_ge(shaped, 3)
                    dve.scalar_tensor_tensor(out=sel_freq[:], in0=freq[:], scalar=1.0 / (2 * CUTOFF), in1=sel_one[:],
                                             op0=ALU.mult, op1=ALU.mult).then_inc(const_step, 1)
                    dve.wait_ge(const_step, 5)
                    dve.reciprocal(row_scale[:], rowf[:]).then_inc(const_step, 1)

                    def stats(t, j, blocks=NB):
                        landed = 16 * (t + j // XB + 1)
                        dve.wait_ge(x_in[j % XB], landed if blocks == NB else landed - 16 + 16 * REST)
                        for k in range(NB):
                            dve.bn_stats(bn[:, j % XB, k, :], xq[:, j % XB, k, :]).then_inc(bn_done, 1)

                    def means(t, j):
                        n, b = t * UNROLL + j, j % XB
                        dve.wait_ge(bn_done, n * NB + NB)
                        dve.nop(nofuse=True)
                        for k in range(NB):
                            dve.bn_aggr(mean_var[:, b, k, :], bn[:, b, k, :]).then_inc(aggr_done, 1)

                    def factor(t, j):
                        n, b = t * UNROLL + j, j % XB
                        dve.wait_ge(std_ready, n + 1)
                        at_least(dve, h_ready, n - XB + 1)
                        dve.reciprocal(rstd[:, b, :], std[:, b, :]).then_inc(rstd_ready, 1)

                    def offset(t, j):
                        n, b = t * UNROLL + j, j % XB
                        dve.wait_ge(rstd_ready, n + 1)
                        dve.scalar_tensor_tensor(out=shift[:, b, :], in0=mean_var[:, b, :, 0], scalar=-1.0, in1=rstd[:, b, :],
                                                 op0=ALU.mult, op1=ALU.mult).then_inc(shift_ready, 1)

                    def step(t, j, between=None):
                        n = t * UNROLL + j
                        ahead = not isinstance(n, int)
                        if ahead or n + 2 <= STEPS:
                            factor(t, j + 2)
                        if ahead or n + 4 <= STEPS:
                            stats(t, j + 4, NB if ahead or n + 4 < STEPS else REST)
                        if ahead or n + 2 <= STEPS:
                            offset(t, j + 2)
                        if between:
                            between()
                        if ahead or n + 4 <= STEPS:
                            means(t, j + 4)

                    def windows(b):
                        n, win = group_blocks()[b][1], window_steps(b)
                        dve.wait_ge(dst_real, b + 1)
                        dve.tensor_scalar(dst_i[0:n, b, :], dst_i[0:n, b, :], P - 1, None, ALU.bitwise_and).then_inc(win_step, 1)
                        dve.tensor_reduce(least[0:n, b:b + 1], dst_f[0:n, b, :], AX_X, ALU.min).then_inc(win_step, 1)
                        values = dst_f
                        if padded(b):
                            dve.scalar_tensor_tensor(out=row1[0:n, b, :], in0=dst_f[0:n, b, :], scalar=float(NODES), in1=dst_f[0:n, b, :],
                                                     op0=ALU.is_lt, op1=ALU.mult).then_inc(win_step, 1)
                            values, win = row1, win + 1
                            dve.wait_ge(win_step, win + 2)
                        dve.tensor_reduce(most[0:n, b:b + 1], values[0:n, b, :], AX_X, ALU.max).then_inc(win_step, 1)
                        dve.wait_ge(win_step, win + 3)
                        dve.tensor_scalar(row1[0:n, b, :], dst_i[0:n, b, :], 1.0, None, ALU.add).then_inc(win_step, 1)
                        dve.tensor_scalar(least[0:n, b:b + 1], least[0:n, b:b + 1], float(NODES - 1), None, ALU.min).then_inc(win_step, 1)
                        dve.wait_ge(win_step, win + 5)
                        dve.tensor_tensor(span[0:n, b:b + 1], most[0:n, b:b + 1], least[0:n, b:b + 1], ALU.subtract).then_inc(win_step, 1)
                        dve.tensor_scalar(base_diag[0:n, b, :], ident[0:n, :], least[0:n, b:b + 1], None, ALU.mult).then_inc(diag_ready, 1)

                    def widest_span():
                        win = window_steps(GB)
                        dve.wait_ge(win_step, win)
                        dve.tensor_reduce(widest[:], span[:], AX_X, ALU.max).then_inc(win_step, 1)
                        dve.tensor_scalar(win_lo[:], least[:], float(-P), None, ALU.add).then_inc(win_step, 1)

                    dve.wait_ge(abs_ready, 1)
                    dve.tensor_scalar(a_all[:], d_abs[:], TINY, FAR, ALU.max, ALU.min).then_inc(dist_step, 1)
                    dve.wait_ge(ones_set, 4)
                    windows(0)
                    dve.wait_ge(attr_turned, 1)
                    dve.tensor_scalar(attr_lin[:], psA[:, 0:NBLK], float(MUL ** -0.5), None, ALU.mult).then_inc(attr_ready, 1)
                    dve.tensor_scalar(attr_lin2[:], psA[:, 0:NBLK], float((2 * MUL) ** -0.5), None, ALU.mult).then_inc(attr_ready, 1)
                    stats(0, 0)
                    dve.wait_ge(dist_step, 3)
                    dve.scalar_tensor_tensor(out=turns[:], in0=d_abs[:], scalar=ROUND, in1=turns[:],
                                             op0=ALU.subtract, op1=ALU.subtract).then_inc(dist_step, 1)
                    stats(0, 1)
                    means(0, 0)
                    stats(0, 2)
                    means(0, 1)
                    stats(0, 3)
                    means(0, 2)
                    means(0, 3)
                    for j in range(2):
                        factor(0, j)
                        offset(0, j)

                    def by_m(t):
                        return t.rearrange("p (c m) -> p m c", m=3)

                    dve.wait_ge(w_sc_in, 16 * 4)
                    dve.tensor_copy(w_nodes[:, DIM:DIM + MUL], w_sc[:, 0:MUL]).then_inc(w_sc_done, 1)
                    dve.tensor_copy(by_m(w_nodes[:, DIM + MUL:]), w_sc[:, MUL:].rearrange("p (m c) -> p m c", m=3)).then_inc(w_sc_done, 1)
                    dve.wait_ge(wv_landed, 16 * 2)
                    for c, half, m in ((0, 1, 0), (1, 0, 1), (1, 1, 2)):
                        rows = slice(half * HID, (half + 1) * HID)
                        dve.tensor_copy(by_m(w_lin2[rows, c, MUL:DIM])[:, m, :], wv_in[rows, :]).then_inc(w_sc_done, 1)

                    def places():
                        win = window_steps(GB)
                        dve.wait_ge(spread, 1)
                        dve.tensor_copy(base_i[:], psW[:, 0:GROUPS]).then_inc(win_step, 1)
                        dve.wait_ge(win_step, win + 3)
                        dve.tensor_scalar(off_i[:], base_i[:], P - 1, None, ALU.bitwise_and).then_inc(win_step, 1)
                        dve.tensor_scalar(blk0_i[:], base_i[0:1, :], 7, None, ALU.logical_shift_right).then_inc(win_step, 1)
                        dve.wait_ge(win_step, win + 4)
                        dve.tensor_copy(at_hi[:], off_i[:]).then_inc(win_step, 1)
                        dve.wait_ge(win_step, win + 6)
                        dve.tensor_scalar(at_lo[:], at_hi[:], part_f[:, 0:1], None, ALU.is_le).then_inc(win_step, 1)
                        dve.tensor_scalar(at_hi[:], at_hi[:], part_f[:, 0:1], None, ALU.is_gt).then_inc(win_step, 1)
                        dve.tensor_scalar(blk_f[:], blk0_i[:], -1.0, None, ALU.add).then_inc(win_step, 1)
                        dve.wait_ge(span_row, 1)
                        dve.tensor_reduce(span_max[:], psA[0:1, 0:P], AX_X, ALU.max).then_inc(win_step, 1)
                        dve.wait_ge(win_step, win + 10)
                        dve.tensor_copy(span_i[:], span_max[:]).then_inc(win_step, 1)
                        dve.wait_ge(win_step, win + 11)
                        dve.tensor_scalar(more_i[:], span_i[:], 7, None, ALU.logical_shift_right).then_inc(win_step, 1)
                        dve.wait_ge(win_step, win + 12)
                        dve.tensor_scalar(passes_i[:], more_i[:], 1.0, None, ALU.add).then_inc(win_step, 1)

                    between = {0: lambda: windows(1), 1: lambda: windows(2), 2: widest_span}
                    for j in range(UNROLL):
                        step(0, j)
                        if j in between:
                            between[j]()
                    dve.wait_ge(a_out, 16)
                    with dve.Fori(1, LOOPS) as t:
                        for j in range(UNROLL):
                            cols = bass.ds((t * UNROLL + (j - UNROLL)) * RECIP, RECIP)
                            step(t, j, lambda: dve.reciprocal(a_all[:, cols], a_all[:, cols]).then_inc(recip_ready, 1))
                    for n in range(PEELED, STEPS + 1):
                        step(n // UNROLL, n % UNROLL)
                        if n == PEELED:
                            dve.wait_ge(dist_step, 5)
                            dve.scalar_tensor_tensor(out=turns[:], in0=d_in[:], scalar=CUTOFF, in1=turns[:],
                                                     op0=ALU.is_le, op1=ALU.mult).then_inc(dist_step, 1)
                        if n == PEELED + 1:
                            dve.wait_ge(dist_step, 6)
                            dve.wait_ge(recip_ready, PEELED - UNROLL)
                            dve.tensor_tensor(turns[:], turns[:], a_all[:], ALU.mult).then_inc(dist_step, 1)
                        if n == PEELED + 3:
                            places()

                    dve.wait_ge(w_edges_in, 16 * (SEGS + 6))
                    dve.wait_ge(const_step, 7)
                    dve.tensor_scalar(w1[:], w1[:], row_scale[:, 0:1], float(CUTOFF / np.pi), ALU.mult, ALU.mult).then_inc(const_step, 1)
                    dve.tensor_scalar(w3[:], w3[:], float(HID ** -0.5), None, ALU.mult).then_inc(const_step, 1)

        passes = nc.values_load(passes_i[0:1, 0:1], min_val=1, max_val=NBLK)
        with ExitStack() as st:
            def s2(name, shape, dt=F32):
                return sb(name, shape, dt, st)

            sems = []

            def sem(name):
                sems.append(st.enter_context(nc.semaphore(name)))
                return sems[-1]

            key_all = s2("key_all", [P, GB, GROUP])
            key = s2("key", [P, SLOTS, TILES])
            harm = s2("harm", [P, SLOTS, TILES, 4])
            lin_g = s2("lin_g", [P, SLOTS, TILES, DIM])
            aq = s2("aq", [SEGS, 2, SEG])
            k_turn = s2("k_turn", [P, SEG])
            frac = s2("frac", [P, SEG])
            sine = s2("sine", [P, SEG])
            rbf = s2("rbf", [P, SEG])
            h1 = s2("h1", [P, 2, UNIT])
            h2 = s2("h2", [P, HALF])
            onehot = s2("onehot", [P, 2, TILES, P])
            lin_sh = s2("lin_sh", [P, TILES, 3, MUL])
            dot2 = s2("dot2", [P, TILES, MUL])
            dot = s2("dot", [P, TILES, MUL])
            lin_sh0 = s2("lin_sh0", [P, 2, TILES, DIM])
            w_s = s2("w_s", [P, TILES, MUL])
            msg = s2("msg", [P, 2, TILES, COLS])
            ps_rbf = st.enter_context(nc.psum_tensor("ps_rbf", [P, 2, 256], F32))
            ps_h1 = st.enter_context(nc.psum_tensor("ps_h1", [P, 2, 512], F32))
            ps_h2 = st.enter_context(nc.psum_tensor("ps_h2", [P, 2, 512], F32))
            ps_w = st.enter_context(nc.psum_tensor("ps_w", [P, 8 * P], F32))
            ps_agg = st.enter_context(nc.psum_tensor("ps_agg", [P, 512], F32))

            key_step, key_out = sem("key_step"), sem("key_out")
            src_in = [sem(f"src_in{u}") for u in range(SLOTS)]
            key_in = [sem(f"key_in{u}") for u in range(SLOTS)]
            harm_in = [sem(f"harm_in{u}") for u in range(SLOTS)]
            gathered = [sem(f"gathered{u}") for u in range(SLOTS)]
            aq_in, blk_ready = sem("aq_in"), sem("blk_ready")
            rbf_spread, k_ready, frac_ready, sine_ready, rbf_ready = (
                sem("rbf_spread"), sem("k_ready"), sem("frac_ready"), sem("sine_ready"), sem("rbf_ready"))
            h1_done, h1_ready, h2_done, h2_ready = sem("h1_done"), sem("h1_ready"), sem("h2_done"), sem("h2_ready")
            w_ready, w_read, msg_ready, sums_ready = sem("w_ready"), sem("w_read"), sem("msg_ready"), sem("sums_ready")
            onehot_ready, lin_sh_ready, dot2_ready, dot_ready = (
                sem("onehot_ready"), sem("lin_sh_ready"), sem("dot2_ready"), sem("dot_ready"))
            lin_sh0_ready, w_s_ready, o00_ready, o10_ready = (
                sem("lin_sh0_ready"), sem("w_s_ready"), sem("o00_ready"), sem("o10_ready"))
            lo_added, agg_ready = sem("lo_added"), sem("agg_ready")

            def w_part(i):
                return ps_w[:, 0:TILES * P].rearrange("p (t w c) -> p t w c", t=TILES, c=MUL)[:, :, i, :]

            def sh_part(u, m):
                return harm[:, u, :, m].unsqueeze(2).to_broadcast([P, TILES, MUL])

            def sh_vec(u):
                return harm[:, u, :, 1:4].unsqueeze(3).to_broadcast([P, TILES, 3, MUL])

            def lin_s(u):
                return lin_g[:, u, :, 0:MUL]

            def lin_v(u):
                return lin_g[:, u, :, MUL:].rearrange("p t (m c) -> p t m c", m=3)

            def message(u):
                m = msg[:, u % 2]
                vec = m[:, :, 2 * MUL:MSG].rearrange("p t (m o c) -> p t m o c", m=3, o=2)
                return m[:, :, 0:MUL], m[:, :, MUL:2 * MUL], vec[:, :, :, 0, :], vec[:, :, :, 1, :]

            def spread_m(ap):
                return ap.unsqueeze(2).to_broadcast([P, TILES, 3, MUL])

            with nc.Fori(0, passes):
                with nc.Block() as block:
                    @block.sync
                    def _(sp):
                        def load_src(i, u):
                            sp.dma_start(src_ix[:, u, :], src[edges(i, u)].rearrange("(p j) -> p j", j=TILES)).then_inc(src_in[u], 16)

                        def load_harm(i, u):
                            sp.dma_start(harm[:, u], sh[edges(i, u), :].rearrange("(p j) m -> p j m", j=TILES)).then_inc(harm_in[u], 16)

                        def load_key(i, u):
                            sp.dma_start(key[:, u, :], key_table[edges(i, u)].rearrange("(p j) -> p j", j=TILES)).then_inc(key_in[u], 16)

                        def load_aq(i):
                            for k, table in enumerate((a_table, q_table)):
                                sp.dma_start(aq[:, k, :], table[bass.ds(i * QUAD, QUAD)].rearrange("(s c) -> s c", s=SEGS)).then_inc(aq_in, 16)

                        load_aq(0)
                        for u in range(SLOTS):
                            load_harm(0, u)
                        for b, n in group_blocks():
                            sp.wait_ge(key_step, 3 + 2 * (b + 1))
                            sp.dma_start(key_table[b * P * GROUP:(b * P + n) * GROUP].rearrange("(g e) -> g e", e=GROUP),
                                         key_all[0:n, b, :]).then_inc(key_out, 16)
                        sp.wait_ge(key_out, 16 * GB)
                        for u in range(SLOTS):
                            load_key(0, u)
                        sp.wait_ge(rbf_spread, 1)
                        load_aq(1)
                        with sp.Fori(0, ITERS) as i:
                            for u in range(SLOTS):
                                sp.wait_ge(gathered[u], 16 * TILES * (i + 1))
                                load_src(i + 1, u)
                                if u == 1:
                                    sp.wait_ge(rbf_spread, i + 2)
                                    load_aq(i + 2)
                                sp.wait_ge(msg_ready, i * SLOTS + u + 1)
                                load_key(i + 1, u)
                                load_harm(i + 1, u)
                        sp.wait_ge(gathered[0], 16 * TILES * (ITERS + 1))
                        for u in range(SLOTS):
                            sp.wait_ge(src_in[u], 16 * ITERS)
                            load_src(0, u)
                        sp.wait_ge(aq_in, 32 * (ITERS + 2))
                        for u in range(SLOTS):
                            sp.wait_ge(src_in[u], 16 * (ITERS + 1))
                            sp.wait_ge(key_in[u], 16 * (ITERS + 1))
                            sp.wait_ge(harm_in[u], 16 * (ITERS + 1))

                    @block.gpsimd
                    def _(pool):
                        def gather(i, u, first=False):
                            if not first:
                                pool.wait_ge(src_in[u], 16 * i)
                                pool.wait_ge(w_s_ready, i * SLOTS + u - SLOTS + 1)
                                pool.nop(nofuse=True)
                            for j in range(TILES):
                                pool.indirect_dma_start(
                                    lin_g[:, u, j, :], None, lin_table,
                                    bass.IndirectOffsetOnAxis(ap=src_ix[:, u, j:j + 1], axis=0)).then_inc(gathered[u], 16)

                        for u in range(SLOTS):
                            gather(0, u, first=True)
                        with pool.Fori(1, ITERS) as i:
                            for u in range(SLOTS):
                                gather(i, u)
                        gather(ITERS, 0)
                        for u in range(SLOTS):
                            pool.wait_ge(gathered[u], 16 * TILES * (ITERS + (u == 0)))
                        pool.dma_reset()

                    @block.tensor
                    def _(pe):
                        def spread_aq(i):
                            pe.wait_ge(aq_in, 32 * (i + 1))
                            at_least(pe, rbf_ready, i)
                            pe.matmul(ps_rbf[:, 0, 0:SEG], sel_freq[:], aq[:, 0, :], start=True, stop=True)
                            pe.matmul(ps_rbf[:, 1, 0:SEG], sel_one[:], aq[:, 1, :], start=True, stop=True).then_inc(rbf_spread, 1)

                        def layer1(i, k):
                            if k == 0:
                                pe.wait_ge(rbf_ready, i + 1)
                            at_least(pe, h1_ready, i * UNITS + k - 1)
                            for half in range(2):
                                mm = pe.matmul(ps_h1[:, k % 2, half * SEG:(half + 1) * SEG], w1[:, 2 * k + half, :], rbf[:],
                                               start=True, stop=True)
                            mm.then_inc(h1_done, 1)

                        def layer2(i, k):
                            pe.wait_ge(h1_ready, i * UNITS + k + 1)
                            at_least(pe, h2_ready, i * UNITS + k - 1)
                            pe.matmul(ps_h2[:, k % 2, 0:UNIT], w2[:], h1[:, k % 2, :], start=True, stop=True).then_inc(h2_done, 1)

                        def layer3(i, u):
                            units = 2 * (u // 2) + 2
                            pe.wait_ge(h2_ready, i * UNITS + units)
                            at_least(pe, w_read, i * SLOTS + u)
                            half = slice((u % 2) * HID, (u % 2) * HID + HID)
                            cols = h2[half, (u // 2) * GROUP:(u // 2 + 1) * GROUP].rearrange("p (c j) -> p j c", j=TILES)
                            for j in range(TILES):
                                mm = pe.matmul(ps_w[:, j * P:(j + 1) * P], cols[:, j, :], w3[half, :], start=True, stop=True)
                            mm.then_inc(w_ready, 1)

                        def segment_sum(i, u):
                            pe.wait_ge(msg_ready, i * SLOTS + u + 1)
                            pe.wait_ge(agg_ready, i * SLOTS + u + 1)
                            for j in range(TILES):
                                mm = pe.matmul(ps_agg[:, 0:COLS], onehot[:, u % 2, j, :], msg[:, u % 2, j, :],
                                               start=(j == 0), stop=(j == TILES - 1))
                            mm.then_inc(sums_ready, 1)

                        spread_aq(0)
                        layer1(0, 0)
                        layer1(0, 1)
                        layer2(0, 0)
                        layer1(0, 2)
                        layer2(0, 1)
                        layer1(0, 3)
                        layer2(0, 2)
                        layer2(0, 3)
                        layer3(0, 0)
                        def body(i, last=False):
                            spread_aq(i + 1)
                            layer3(i, 1)
                            segment_sum(i, 0)
                            layer3(i, 2)
                            segment_sum(i, 1)
                            layer1(i + 1, 0)
                            layer1(i + 1, 1)
                            layer2(i + 1, 0)
                            layer3(i, 3)
                            if last:
                                layer2(i + 1, 1)
                            segment_sum(i, 2)
                            if not last:
                                layer2(i + 1, 1)
                                layer1(i + 1, 2)
                                layer1(i + 1, 3)
                            layer3(i + 1, 0)
                            segment_sum(i, 3)
                            if not last:
                                layer2(i + 1, 2)
                                layer2(i + 1, 3)

                        with pe.Fori(0, ITERS - 1) as i:
                            body(i)
                        body(ITERS - 1, last=True)
                        segment_sum(ITERS, 0)

                    @block.scalar
                    def _(act):
                        def sines(i):
                            act.wait_ge(frac_ready, i + 1)
                            act.activation(sine[:], frac[:], ACT.Sin, scale=-TURN).then_inc(sine_ready, 1)

                        def silu1(i, k):
                            act.wait_ge(h1_done, i * UNITS + k + 1)
                            at_least(act, h2_done, i * UNITS + k - 1)
                            act.activation(h1[:, k % 2, :], ps_h1[:, k % 2, 0:UNIT], ACT.Silu,
                                           scale=float(RBF ** -0.5)).then_inc(h1_ready, 1)

                        def silu2(i, k):
                            act.wait_ge(h2_done, i * UNITS + k + 1)
                            at_least(act, w_ready, i * SLOTS - SLOTS + 2 * (k // 2) + 2)
                            act.activation(h2[:, k * UNIT:(k + 1) * UNIT], ps_h2[:, k % 2, 0:UNIT], ACT.Silu,
                                           scale=float(HID ** -0.5)).then_inc(h2_ready, 1)

                        def scale_lin(i, u):
                            n = i * SLOTS + u
                            act.wait_ge(gathered[u], 16 * TILES * (i + 1))
                            act.wait_ge(harm_in[u], 16 * (i + 1))
                            at_least(act, w_s_ready, n - 1)
                            for j in range(TILES):
                                last = act.activation(lin_sh0[:, u % 2, j, :], lin_g[:, u, j, :], ACT.Copy, scale=harm[:, u, j, 0:1])
                            last.then_inc(lin_sh0_ready, 1)

                        sines(0)
                        silu1(0, 0)
                        silu1(0, 1)
                        silu2(0, 0)
                        silu1(0, 2)
                        silu2(0, 1)
                        silu1(0, 3)
                        silu2(0, 2)
                        silu2(0, 3)
                        for u in range(3):
                            scale_lin(0, u)

                        def body(i, last=False):
                            sines(i + 1)
                            scale_lin(i, 3)
                            silu1(i + 1, 0)
                            silu1(i + 1, 1)
                            silu2(i + 1, 0)
                            if last:
                                silu2(i + 1, 1)
                                scale_lin(i + 1, 0)
                                return
                            scale_lin(i + 1, 0)
                            silu2(i + 1, 1)
                            silu1(i + 1, 2)
                            silu1(i + 1, 3)
                            scale_lin(i + 1, 1)
                            silu2(i + 1, 2)
                            silu2(i + 1, 3)
                            scale_lin(i + 1, 2)

                        with act.Fori(0, ITERS - 1) as i:
                            body(i)
                        body(ITERS - 1, last=True)

                    @block.vector
                    def _(dve):
                        dve.tensor_scalar(win_lo[:], win_lo[:], float(P), None, ALU.add).then_inc(key_step, 1)
                        dve.tensor_scalar(blk_f[:], blk_f[:], 1.0, None, ALU.add).then_inc(key_step, 1)
                        dve.wait_ge(key_step, 2)
                        dve.tensor_scalar(win_hi[:], win_lo[:], float(P), None, ALU.add).then_inc(key_step, 1)
                        dve.tensor_scalar(blk_i[:], blk_f[:], float(NBLK - 1), None, ALU.min).then_inc(blk_ready, 1)
                        dve.memset(msg[:, :, :, MSG:COLS], 1.0).then_inc(agg_ready, 1)
                        dve.wait_ge(key_step, 3)
                        for b, n in group_blocks():
                            dve.scalar_tensor_tensor(out=key_all[0:n, b, :], in0=dst_f[0:n, b, :], scalar=win_hi[0:n, b:b + 1],
                                                     in1=row1[0:n, b, :], op0=ALU.is_lt, op1=ALU.mult).then_inc(key_step, 1)
                            dve.wait_ge(key_step, 4 + 2 * b)
                            dve.scalar_tensor_tensor(out=key_all[0:n, b, :], in0=dst_f[0:n, b, :], scalar=win_lo[0:n, b:b + 1],
                                                     in1=key_all[0:n, b, :], op0=ALU.is_ge, op1=ALU.mult).then_inc(key_step, 1)

                        def fractions(i):
                            dve.wait_ge(rbf_spread, i + 1)
                            dve.tensor_scalar(k_turn[:], ps_rbf[:, 0, 0:SEG], ROUND, None, ALU.add).then_inc(k_ready, 1)
                            dve.wait_ge(k_ready, i + 1)
                            dve.scalar_tensor_tensor(out=frac[:], in0=k_turn[:], scalar=ROUND, in1=ps_rbf[:, 0, 0:SEG],
                                                     op0=ALU.subtract, op1=ALU.subtract).then_inc(frac_ready, 1)

                        def basis(i):
                            dve.wait_ge(sine_ready, i + 1)
                            at_least(dve, h1_done, i * UNITS)
                            dve.tensor_tensor(rbf[:], sine[:], ps_rbf[:, 1, 0:SEG], ALU.mult).then_inc(rbf_ready, 1)

                        def products(i, u):
                            dve.wait_ge(gathered[u], 16 * TILES * (i + 1))
                            dve.wait_ge(harm_in[u], 16 * (i + 1))
                            dve.tensor_tensor(lin_sh[:], lin_v(u), sh_vec(u), ALU.mult).then_inc(lin_sh_ready, 1)

                        def columns(i, u):
                            n = i * SLOTS + u
                            dve.wait_ge(key_in[u], 16 * (i + 1))
                            dve.tensor_tensor(onehot[:, u % 2], iota1[:].unsqueeze(1).to_broadcast([P, TILES, P]),
                                              key[:, u, :].unsqueeze(2).to_broadcast([P, TILES, P]), ALU.is_equal).then_inc(onehot_ready, 1)
                            dve.wait_ge(lin_sh_ready, n + 1)
                            dve.tensor_tensor(dot2[:], lin_sh[:, :, 0, :], lin_sh[:, :, 1, :], ALU.add).then_inc(dot2_ready, 1)
                            dve.wait_ge(dot2_ready, n + 1)
                            dve.tensor_tensor(dot[:], dot2[:], lin_sh[:, :, 2, :], ALU.add).then_inc(dot_ready, 1)

                        def late(i, u):
                            n = i * SLOTS + u
                            o00, o11, o01, o10 = message(u)
                            scaled = lin_sh0[:, u % 2]
                            dve.wait_ge(w_ready, n + 1)
                            dve.wait_ge(lin_sh0_ready, n + 1)
                            dve.tensor_tensor(o10, scaled[:, :, MUL:].rearrange("p t (m c) -> p t m c", m=3), spread_m(w_part(2)),
                                              ALU.mult).then_inc(o10_ready, 1)
                            dve.tensor_tensor(o00, scaled[:, :, 0:MUL], w_part(0), ALU.mult).then_inc(o00_ready, 1)
                            dve.tensor_tensor(w_s[:], w_part(1), lin_s(u), ALU.mult).then_inc(w_s_ready, 1)
                            dve.wait_ge(dot_ready, n + 1)
                            dve.scalar_tensor_tensor(out=o11, in0=dot[:], scalar=float(3 ** -0.5), in1=w_part(3),
                                                     op0=ALU.mult, op1=ALU.mult).then_inc(w_read, 1)
                            dve.wait_ge(w_s_ready, n + 1)
                            dve.tensor_tensor(o01, spread_m(w_s[:]), sh_vec(u), ALU.mult).then_inc(msg_ready, 1)

                        def accumulate(i, u):
                            n = i * SLOTS + u
                            g = i * SLOTS + OFFSET[u] // GROUP
                            blk = dve.value_load(blk_i[0:1, bass.ds(g, 1)], min_val=0, max_val=NBLK - 1)
                            dve.wait_ge(sums_ready, n + 1)
                            dve.wait_ge(agg_ready, n + 1)
                            for k, (part, added) in enumerate(((at_lo, lo_added), (at_hi, agg_ready))):
                                rows = agg[:, bass.ds(blk * COLS + k * COLS, COLS)]
                                dve.scalar_tensor_tensor(out=rows, in0=ps_agg[:, 0:COLS], scalar=part[:, bass.ds(g, 1)],
                                                         in1=rows, op0=ALU.mult, op1=ALU.add).then_inc(added, 1)

                        fractions(0)
                        basis(0)
                        dve.wait_ge(blk_ready, 1)
                        products(0, 0)
                        columns(0, 0)
                        late(0, 0)
                        products(0, 1)
                        columns(0, 1)

                        def body(i, last=False):
                            for u in range(SLOTS):
                                late(i + (u + 1) // SLOTS, (u + 1) % SLOTS)
                                if u == 0:
                                    fractions(i + 1)
                                ahead = None if last and u == SLOTS - 1 else (i + (u + 2) // SLOTS, (u + 2) % SLOTS)
                                if ahead:
                                    products(*ahead)
                                accumulate(i, u)
                                if ahead:
                                    columns(*ahead)
                                if u == 0:
                                    basis(i + 1)

                        with dve.Fori(0, ITERS - 1) as i:
                            body(i)
                        body(ITERS - 1, last=True)
                        accumulate(ITERS, 0)

                assert [s.num for s in sems] == list(range(sems[0].num, sems[0].num + len(sems)))
                nc.sync.sem_clear(range(sems[0].num, sems[0].num + len(sems)))
                nc.all_engine_barrier()

        with ExitStack() as st:
            def s3(name, shape, dt=F32):
                return sb(name, shape, dt, st)

            def sem(name):
                return st.enter_context(nc.semaphore(name))

            IN = 4
            x3 = s3("x3", [P, IN, NB, DIM])
            sc3 = s3("sc3", [P, IN, NB, DIM])
            count = s3("count", [P, NBLK])
            inv = s3("inv", [P, NBLK])
            scale = s3("scale", [P, NBLK])
            sums = s3("sums", [P, 2, NB, MSG])
            aggT = s3("aggT", [P, 2, 2, NB * P])
            pre = s3("pre", [P, 2, NB])
            alpha = s3("alpha", [P, 2, NB])
            gain = s3("gain", [P, 2, NB])
            layer = s3("layer", [P, 2, NB, DIM])
            new = s3("new", [P, 2, NB, DIM])
            ps_aT = st.enter_context(nc.psum_tensor("ps_aT", [P, 2, 2, NB * P], F32))
            ps_l2 = st.enter_context(nc.psum_tensor("ps_l2", [P, 2, NB, 256], F32))

            in3 = [sem(f"in3_{i}") for i in range(IN)]
            out3 = [sem(f"out3_{b}") for b in range(2)]
            count_ready, inv_ready, scale_ready, aT_done = sem("count_ready"), sem("inv_ready"), sem("scale_ready"), sem("aT_done")
            aT_lo, aT_hi, l2_done, pre_ready = sem("aT_lo"), sem("aT_hi"), sem("l2_done"), sem("pre_ready")
            alpha_ready, gain_ready, layer_ready, new_ready, sums_copied = (
                sem("alpha_ready"), sem("gain_ready"), sem("layer_ready"), sem("new_ready"), sem("sums_copied"))

            PRE = IN
            LOOPS = (STEPS - 3 - PRE) // IN
            AFTER = PRE + IN * LOOPS

            def blocks_of(n):
                return REST if isinstance(n, int) and n == STEPS else NB

            def agg_step(n):
                k = blocks_of(n)
                return agg[:, bass.ds(n * (NB * COLS), k * COLS)].rearrange("p (b c) -> p b c", c=COLS)

            def steps(eng, body):
                for n in range(PRE):
                    body(n, n)
                with eng.Fori(0, LOOPS) as t:
                    for j in range(IN):
                        body(t * IN + (PRE + j), j)
                for n in range(AFTER, STEPS + 1):
                    body(n, n % IN)

            def loads(n, i):
                if not isinstance(n, int):
                    return (n - i) * (32 // IN) + 32
                return n // IN * 32 + (32 if n < STEPS else 32 * REST)

            def within(n):
                return not isinstance(n, int) or 0 <= n <= STEPS

            with nc.Block() as block:
                @block.sync
                def _(sp):
                    def load(n, i):
                        if blocks_of(n) == NB:
                            sp.dma_start(x3[:, i], node_rows(x, n)).then_inc(in3[i], 16)
                            sp.dma_start(sc3[:, i], node_rows(sc_table, n)).then_inc(in3[i], 16)
                        else:
                            for r in range(REST):
                                sp.dma_start(x3[0:REST_ROWS[r], i, r], rest_rows(x, r)).then_inc(in3[i], 16)
                                sp.dma_start(sc3[0:REST_ROWS[r], i, r], rest_rows(sc_table, r)).then_inc(in3[i], 16)

                    def body(n, i):
                        b = i % 2
                        sp.wait_ge(new_ready, n + 1)
                        if blocks_of(n) == NB:
                            sp.dma_start(node_rows(out, n), new[:, b]).then_inc(out3[b], 16)
                        else:
                            for r in range(REST):
                                sp.dma_start(rest_rows(out, r), new[0:REST_ROWS[r], b, r]).then_inc(out3[b], 16)
                        if within(n + IN):
                            load(n + IN, i)

                    for i in range(IN):
                        load(i, i)
                    steps(sp, body)
                    for b in range(2):
                        whole = len(range(b, STEPS, 2))
                        sp.wait_ge(out3[b], 16 * (whole + (REST if b == STEPS % 2 else 0)))

                @block.vector
                def _(dve):
                    def update(n, i):
                        if not within(n):
                            return
                        k, b = blocks_of(n), i % 2
                        dve.wait_ge(alpha_ready, n + 1)
                        dve.tensor_tensor(gain[:, b, 0:k], alpha[:, b, 0:k], scale[:, bass.ds(n * NB, k)], ALU.mult).then_inc(gain_ready, 1)
                        dve.wait_ge(in3[i], loads(n, i))
                        at_least(dve, new_ready, n - 1)
                        dve.wait_ge(gain_ready, n + 1)
                        for j in range(k):
                            last = dve.scalar_tensor_tensor(out=layer[:, b, j, :], in0=ps_l2[:, b, j, 0:DIM], scalar=gain[:, b, j:j + 1],
                                                            in1=sc3[:, i, j, :], op0=ALU.mult, op1=ALU.add)
                        last.then_inc(layer_ready, 1)

                    def copy_low(n, b):
                        if not within(n):
                            return
                        k = blocks_of(n)
                        dve.wait_ge(aT_done, n + 1)
                        at_least(dve, l2_done, n - 1)
                        dve.tensor_copy(aggT[:, b, 0, 0:k * P], ps_aT[:, b, 0, 0:k * P]).then_inc(aT_lo, 1)

                    def body(n, i):
                        k, b = blocks_of(n), i % 2
                        copy_low(n + 1, 1 - b)
                        update(n - 1, (i - 1) % IN)
                        dve.wait_ge(l2_done, n + 1)
                        at_least(dve, alpha_ready, n - 1)
                        dve.tensor_tensor(pre[:, b, 0:k], ps_l2[:, b, 0:k, DIM], scale[:, bass.ds(n * NB, k)], ALU.mult).then_inc(pre_ready, 1)

                    counts = agg[:, 0:NBLK * COLS].rearrange("p (b c) -> p b c", c=COLS)[:, :, MSG]
                    dve.tensor_scalar(count[:], counts, 1.0, None, ALU.max).then_inc(count_ready, 1)
                    dve.wait_ge(count_ready, 1)
                    dve.reciprocal(inv[:], count[:]).then_inc(inv_ready, 1)
                    dve.wait_ge(inv_ready, 1)
                    dve.tensor_tensor(scale[:], inv[:], attr_lin2[:], ALU.mult).then_inc(scale_ready, 1)
                    dve.wait_ge(scale_ready, 1)
                    copy_low(0, 0)
                    steps(dve, body)
                    update(STEPS, STEPS % IN)

                @block.scalar
                def _(act):
                    def copy_sums(n, b):
                        if not within(n):
                            return
                        k = blocks_of(n)
                        at_least(act, aT_done, n - 1)
                        act.activation(sums[:, b, 0:k, :], agg_step(n)[:, :, 0:MSG], ACT.Copy).then_inc(sums_copied, 1)

                    def copy_high(n, b):
                        if not within(n):
                            return
                        k = blocks_of(n)
                        act.wait_ge(aT_done, n + 1)
                        at_least(act, l2_done, n - 1)
                        act.activation(aggT[:, b, 1, 0:k * P], ps_aT[:, b, 1, 0:k * P], ACT.Copy).then_inc(aT_hi, 1)

                    def body(n, i):
                        k, b = blocks_of(n), i % 2
                        copy_high(n + 1, 1 - b)
                        copy_sums(n + 3, 1 - b)
                        act.wait_ge(pre_ready, n + 1)
                        at_least(act, gain_ready, n - 1)
                        act.activation(alpha[:, b, 0:k], pre[:, b, 0:k], ACT.Tanh).then_inc(alpha_ready, 1)

                    copy_sums(0, 0)
                    copy_sums(1, 1)
                    copy_high(0, 0)
                    copy_sums(2, 0)
                    steps(act, body)

                @block.tensor
                def _(pe):
                    def turn(n, b):
                        if not within(n):
                            return
                        pe.wait_ge(sums_copied, n + 1)
                        at_least(pe, aT_lo, n - 1)
                        at_least(pe, aT_hi, n - 1)
                        for j in range(blocks_of(n)):
                            for c in range(2):
                                last = pe.transpose(ps_aT[:, b, c, j * P:(j + 1) * P], sums[:, b, j, c * P:(c + 1) * P], ident[:])
                        last.then_inc(aT_done, 1)

                    def body(n, i):
                        b = i % 2
                        pe.wait_ge(aT_lo, n + 1)
                        pe.wait_ge(aT_hi, n + 1)
                        at_least(pe, layer_ready, n - 1)
                        for j in range(blocks_of(n)):
                            cols = slice(j * P, (j + 1) * P)
                            for c in range(2):
                                last = pe.matmul(ps_l2[:, b, j, 0:DIM + 1], aggT[:, b, c, cols], w_lin2[:, c, :], start=(c == 0), stop=(c == 1))
                        last.then_inc(l2_done, 1)
                        turn(n + 2, b)

                    turn(0, 0)
                    turn(1, 1)
                    steps(pe, body)

                @block.gpsimd
                def _(pool):
                    def body(n, i):
                        k, b = blocks_of(n), i % 2
                        pool.wait_ge(layer_ready, n + 1)
                        at_least(pool, out3[b], n // 2 * 16 if isinstance(n, int) else (n - b) * 8)
                        pool.tensor_tensor(new[:, b, 0:k], layer[:, b, 0:k], x3[:, i, 0:k], ALU.add).then_inc(new_ready, 1)

                    steps(pool, body)

def kernel(x, src, dst, edge_attr_4, edge_weight, node_vec1, L0_gnn_sc_ws, L0_gnn_sc_wv, L0_gnn_lin1_ws, L0_gnn_lin1_wv,
           L0_gnn_fc_w1, L0_gnn_fc_w2, L0_gnn_fc_w3, L0_gnn_lin2_ws, L0_gnn_lin2_wv, L0_gnn_alpha_w):
    import concourse.bacc as bacc
    from concourse.bass_utils import run_bass_kernel_spmd

    def padded(a, n, fill):
        a = np.ascontiguousarray(a)
        return np.concatenate([a, np.full((n - a.shape[0],) + a.shape[1:], fill, a.dtype)])

    inputs = {
        "x": x, "src": padded(src, EDGES_PAD, 0), "dst": padded(dst, EDGES_PAD, NO_NODE),
        "edge_attr_4": padded(edge_attr_4, EDGES_PAD, 0), "edge_weight": padded(edge_weight, EDGES_PAD, 0),
        "node_vec1": node_vec1, "sc_ws": L0_gnn_sc_ws, "sc_wv": L0_gnn_sc_wv, "lin1_ws": L0_gnn_lin1_ws, "lin1_wv": L0_gnn_lin1_wv,
        "fc_w1": L0_gnn_fc_w1, "fc_w2": L0_gnn_fc_w2, "fc_w3": L0_gnn_fc_w3,
        "lin2_ws": L0_gnn_lin2_ws, "lin2_wv": L0_gnn_lin2_wv, "alpha_w": L0_gnn_alpha_w,
    }
    nc = bacc.Bacc("TRN2", target_bir_lowering=False, num_devices=1)
    arrays, args = {}, []
    for name, a in inputs.items():
        arrays[f"in_{name}"] = np.ascontiguousarray(a)
        args.append(nc.dram_tensor(f"in_{name}", arrays[f"in_{name}"].shape, mybir.dt.from_np(arrays[f"in_{name}"].dtype),
                                   kind="ExternalInput").ap())
    args.append(nc.dram_tensor("out_dram", (NODES, DIM), F32, kind="ExternalOutput").ap())
    gnn_kernel(nc, *args)
    return run_bass_kernel_spmd(nc, [arrays], core_ids=[0]).results[0]["out_dram"]
```
